# Optimizing a Trainium2 kernel written in Bass

```python
import numpy as np
import jax
import jax.numpy as jnp

def _softmax(x, axis=-1):
    return jax.nn.softmax(x, axis=axis)

def _gelu(x):
    return jax.nn.gelu(x, approximate=True)

def _silu(x):
    return jax.nn.silu(x)

def _sigmoid(x):
    return jax.nn.sigmoid(x)

def _layernorm(x, axis=-1, eps=1e-05):
    m = jnp.mean(x, axis=axis, keepdims=True)
    v = jnp.var(x, axis=axis, keepdims=True)
    return (x - m) / jnp.sqrt(v + eps)

def _scatter_add(tgt, idx, src, axis=0):
    return tgt.at[idx].add(src)

def _segment_sum(src, seg, n):
    return jax.ops.segment_sum(src, seg, n)
kernel_name = 'mk_seq_postln_d1_jaxref_r4_b9217c'

def setup_inputs(seed: int=0):
    np.random.seed(seed)
    _w = jnp.asarray

    def _L0_attn_setup():
        import jax, jax.numpy as jnp
        import numpy as np
        B, S, D = (2, 512, 1024)
        NH, NKV = (32, 8)
        HD = D // NH
        NREP = NH // NKV
        SCALE = HD ** (-0.5)
        key = jax.random.key(seed)
        kx, kq, kk, kv, ko = jax.random.split(key, 5)
        s = 0.02
        return {'x': jax.random.normal(kx, (B, S, D), dtype=jnp.float32), 'wq': jax.random.normal(kq, (D, NH * HD), dtype=jnp.float32) * s, 'wk': jax.random.normal(kk, (D, NKV * HD), dtype=jnp.float32) * s, 'wv': jax.random.normal(kv, (D, NKV * HD), dtype=jnp.float32) * s, 'wo': jax.random.normal(ko, (NH * HD, D), dtype=jnp.float32) * s}
    _L0_attn_in = _L0_attn_setup()

    def _L0_ffn_setup():
        import jax, jax.numpy as jnp
        import numpy as np
        B, S, IN, OUT = (4, 512, 1024, 1024)
        E, K, R = (8, 2, 16)
        CAP_FACTOR = 3.0
        ALPHA = 1.0 / R
        LN_EPS = 1e-05
        key = jax.random.key(seed)
        ks = jax.random.split(key, 6)
        return {'x': jax.random.normal(ks[0], (B, S, IN), dtype=jnp.float32), 'weight': jax.random.normal(ks[1], (OUT, IN), dtype=jnp.float32) * 0.02, 'lora_A': jax.random.normal(ks[2], (E, IN, R), dtype=jnp.float32) / np.sqrt(R), 'lora_B': jax.random.normal(ks[3], (E, R, OUT), dtype=jnp.float32) * 0.02, 'gw1': jax.random.normal(ks[4], (4 * E, IN), dtype=jnp.float32) * 0.02, 'gb1': jnp.zeros((4 * E,), dtype=jnp.float32), 'ln_gamma': jnp.ones((4 * E,), dtype=jnp.float32), 'ln_beta': jnp.zeros((4 * E,), dtype=jnp.float32), 'gw2': jax.random.normal(ks[5], (E, 4 * E), dtype=jnp.float32) * 0.02, 'gb2': jnp.zeros((E,), dtype=jnp.float32)}
    _L0_ffn_in = _L0_ffn_setup()
    _d = {'L0_attn_x': _L0_attn_in['x'], 'L0_attn_wq': _L0_attn_in['wq'], 'L0_attn_wk': _L0_attn_in['wk'], 'L0_attn_wv': _L0_attn_in['wv'], 'L0_attn_wo': _L0_attn_in['wo'], 'L0_ffn_weight': _L0_ffn_in['weight'], 'L0_ffn_lora_A': _L0_ffn_in['lora_A'], 'L0_ffn_lora_B': _L0_ffn_in['lora_B'], 'L0_ffn_gw1': _L0_ffn_in['gw1'], 'L0_ffn_gb1': _L0_ffn_in['gb1'], 'L0_ffn_ln_gamma': _L0_ffn_in['ln_gamma'], 'L0_ffn_ln_beta': _L0_ffn_in['ln_beta'], 'L0_ffn_gw2': _L0_ffn_in['gw2'], 'L0_ffn_gb2': _L0_ffn_in['gb2']}
    _x0 = _d['L0_attn_x']
    _d['L0_attn_x'] = jax.random.normal(jax.random.fold_in(jax.random.key(seed), 1), (2, 2048, 1024), dtype=_x0.dtype)
    del _x0
    return _d

def reference(L0_attn_x, L0_attn_wq, L0_attn_wk, L0_attn_wv, L0_attn_wo, L0_ffn_weight, L0_ffn_lora_A, L0_ffn_lora_B, L0_ffn_gw1, L0_ffn_gb1, L0_ffn_ln_gamma, L0_ffn_ln_beta, L0_ffn_gw2, L0_ffn_gb2):

    def _L0_attn_ref(x, wq, wk, wv, wo):
        import jax, jax.numpy as jnp
        import numpy as np
        B, S, D = (2, 512, 1024)
        NH, NKV = (32, 8)
        HD = D // NH
        NREP = NH // NKV
        SCALE = HD ** (-0.5)
        b, s, _ = x.shape
        q = (x @ wq).reshape(b, s, NH, HD)
        k = (x @ wk).reshape(b, s, NKV, HD)
        v = (x @ wv).reshape(b, s, NKV, HD)
        k = jnp.repeat(k, NREP, axis=2)
        v = jnp.repeat(v, NREP, axis=2)
        scores = jnp.einsum('bihd,bjhd->bhij', q, k) * SCALE
        causal = jnp.tril(jnp.ones((s, s), dtype=bool))
        scores = jnp.where(causal, scores, jnp.finfo(scores.dtype).min)
        attn = jax.nn.softmax(scores, axis=-1)
        out = jnp.einsum('bhij,bjhd->bihd', attn, v)
        out = out.reshape(b, s, NH * HD)
        return out @ wo

    def _L0_ffn_ref(x, weight, lora_A, lora_B, gw1, gb1, ln_gamma, ln_beta, gw2, gb2):
        import jax, jax.numpy as jnp
        import numpy as np
        B, S, IN, OUT = (4, 512, 1024, 1024)
        E, K, R = (8, 2, 16)
        CAP_FACTOR = 3.0
        ALPHA = 1.0 / R
        LN_EPS = 1e-05
        orig_shape = x.shape
        xf = x.reshape(-1, orig_shape[-1])
        N = xf.shape[0]
        capacity = int(CAP_FACTOR * N / E)
        h = xf @ gw1.T + gb1
        mu = jnp.mean(h, axis=-1, keepdims=True)
        var = jnp.mean((h - mu) ** 2, axis=-1, keepdims=True)
        h = (h - mu) * jax.lax.rsqrt(var + LN_EPS) * ln_gamma + ln_beta
        h = jax.nn.relu(h)
        gates = h @ gw2.T + gb2
        top_v, top_i = jax.lax.top_k(gates, K)
        top_g = jax.nn.softmax(top_v, axis=-1)
        onehot = (top_i[..., None] == jnp.arange(E)).astype(xf.dtype)
        counts = onehot.sum(axis=0)
        allowed = (counts <= capacity).astype(xf.dtype)
        w = jnp.einsum('nke,nk,ke->ne', onehot, top_g, allowed)
        main = xf @ weight.T
        tmp = jnp.einsum('ni,eir->enr', xf, lora_A)
        tmp = tmp * w.T[:, :, None]
        lora = jnp.einsum('enr,ero->no', tmp, lora_B) * ALPHA
        out = main + lora
        return out.reshape(*orig_shape[:-1], weight.shape[0])
    x = L0_attn_x
    x = _layernorm(x + _L0_attn_ref(x, L0_attn_wq, L0_attn_wk, L0_attn_wv, L0_attn_wo), axis=-1)
    x = _layernorm(x + _L0_ffn_ref(x, L0_ffn_weight, L0_ffn_lora_A, L0_ffn_lora_B, L0_ffn_gw1, L0_ffn_gb1, L0_ffn_ln_gamma, L0_ffn_ln_beta, L0_ffn_gw2, L0_ffn_gb2), axis=-1)
    return x

_drawn_inputs = setup_inputs


def setup_inputs(seed=0):
    import zlib

    import numpy as np

    out = dict(_drawn_inputs(seed))
    spreads = {'L0_ffn_gb1': (0.0, 0.8),
     'L0_ffn_ln_gamma': (1.0, 0.6),
     'L0_ffn_ln_beta': (0.0, 0.8),
     'L0_ffn_gb2': (0.0, 0.369)}
    factors = {'L0_attn_wq': 5.303,
     'L0_attn_wk': 5.276,
     'L0_ffn_lora_A': 3.626,
     'L0_ffn_lora_B': 3.624,
     'L0_ffn_gw1': 4.077,
     'L0_ffn_gw2': 4.125}
    for name, (base, spread) in spreads.items():
        noise = np.random.default_rng([zlib.crc32(name.encode()), seed]).standard_normal(out[name].shape)
        drawn = base * np.exp(spread * noise) if base else spread * noise
        out[name] = jnp.asarray(drawn.astype(out[name].dtype))
    for name, factor in factors.items():
        out[name] = (out[name] * factor).astype(out[name].dtype)
    return out
```

```python
import concourse.bass as bass
from concourse import mybir
from contextlib import ExitStack

F32 = mybir.dt.float32
F32R = mybir.dt.float32r
BF16 = mybir.dt.bfloat16
I32 = mybir.dt.int32
U32 = mybir.dt.uint32
ALU = mybir.AluOpType
ACT = mybir.ActivationFunctionType
AX = mybir.AxisListType

P = 128
BANK = 512
B, S, D = 2, 2048, 1024
N = B * S
NH, NKV, HD = 32, 8, 32
REP = NH // NKV
KC = D // P
SCALE = HD ** -0.5
NEG = -1e30
E, R, TOPK = 8, 16, 2
GH = 4 * E
CAPACITY = int(3.0 * N / E)
LN_EPS = 1e-5


def make_identity(pool, ident, sem):
    pool.memset(ident[:, :], 0.0).then_inc(sem, 1)
    pool.wait_ge(sem, 1)
    pool.affine_select(out=ident[:, :], in_=ident[:, :], compare_op=ALU.not_equal, fill=1.0,
                       base=0, pattern=[[-1, P]], channel_multiplier=1).then_inc(sem, 1)


def matmul3(pe, out, lhs_hi, lhs_lo, rhs_hi, rhs_lo, first, last):
    pe.matmul(out, lhs_hi, rhs_hi, start=first, stop=False)
    pe.matmul(out, lhs_hi, rhs_lo, start=False, stop=False)
    return pe.matmul(out, lhs_lo, rhs_hi, start=False, stop=last)


def project_qkv(nc, sem, x, wq, wk, wv, q_hi, q_lo, k_hi, k_lo, v_d):
    TT = 512
    NT = N // TT
    SUB = TT // P
    KV = NKV * HD
    WC = D + 2 * KV
    QG, KG, VG = D // P, KV // P, SUB
    G = QG + KG + VG
    GB = 4
    TB = 4
    T_AT = 4
    assert GB + TB == 8 and G % 2 == 0
    x_t = x.rearrange("b (t s p) d -> (b t) p s d", s=SUB, p=P)

    ctx = ExitStack()
    with ctx:
        sb = lambda name, shape, dt: ctx.enter_context(nc.sbuf_tensor(name, shape, dt))
        ident = sb("p1_ident", [P, P], F32)
        w_hi = sb("p1_w_hi", [P, KC, WC], F32R)
        w_lo = sb("p1_w_lo", [P, KC, WC], F32R)
        w_raw = sb("p1_w_raw", [P, 2, WC], F32)
        x_raw = sb("p1_x_raw", [P, SUB, D], F32)
        xT_hi = [sb(f"p1_xT_hi{i}", [P, KC, TT], F32R) for i in range(2)]
        xT_lo = [sb(f"p1_xT_lo{i}", [P, KC, TT], F32R) for i in range(2)]
        out_hi = sb("p1_out_hi", [P, 2, TT], F32R)
        out_lo = sb("p1_out_lo", [P, 2, TT], F32R)
        v_out = sb("p1_v_out", [P, 2, KV], F32)
        tp = [ctx.enter_context(nc.psum_tensor(f"p1_tp{i}", [P, BANK], F32)) for i in range(TB)]
        acc = [ctx.enter_context(nc.psum_tensor(f"p1_acc{i}", [P, BANK], F32)) for i in range(GB)]

        ident_done = sem("p1_ident_done")
        w_in = [sem(f"p1_w_in{i}") for i in range(2)]
        w_hi_done = sem("p1_w_hi_done")
        w_lo_done = sem("p1_w_lo_done")
        x_in = sem("p1_x_in")
        transposed = sem("p1_transposed")
        xT_hi_done = sem("p1_xT_hi_done")
        xT_lo_done = sem("p1_xT_lo_done")
        group_done = sem("p1_group_done")
        out_hi_done = sem("p1_out_hi_done")
        evacuated = sem("p1_evacuated")
        stored = [sem(f"p1_stored{i}") for i in range(2)]

        HALF = (QG + KG) // 2 * 32 + VG // 2 * 16

        def stored_before(t, g):
            n = g // 2
            return t * HALF + min(n, (QG + KG) // 2) * 32 + max(0, n - (QG + KG) // 2) * 16

        block = ctx.enter_context(nc.Block())

        @block.gpsimd
        def _(pool):
            make_identity(pool, ident, ident_done)

        @block.sync
        def _(sp):
            def load_x(t):
                sp.dma_start(x_raw[:, :, :], x_t[t, :, :, :]).then_inc(x_in, 16)

            def load_w(k):
                if k >= 2:
                    sp.wait_ge(w_lo_done, k - 1)
                rows = slice(k * P, (k + 1) * P)
                sp.dma_start(w_raw[:, k % 2, 0:D], wq[rows, :]).then_inc(w_in[k % 2], 16)
                sp.dma_start(w_raw[:, k % 2, D:D + KV], wk[rows, :]).then_inc(w_in[k % 2], 16)
                sp.dma_start(w_raw[:, k % 2, D + KV:WC], wv[rows, :]).then_inc(w_in[k % 2], 16)

            def tile(t, first=False, last=False):
                for g in range(G):
                    sp.wait_ge(evacuated, t * G + g + 1)
                    cols = bass.ds(t * TT, TT)
                    if g < QG + KG:
                        hi, lo, r = (q_hi, q_lo, g) if g < QG else (k_hi, k_lo, g - QG)
                        rows = slice(r * P, (r + 1) * P)
                        sp.dma_start(hi[rows, cols], out_hi[:, g % 2, :].bitcast(F32)).then_inc(stored[g % 2], 16)
                        sp.dma_start(lo[rows, cols], out_lo[:, g % 2, :].bitcast(F32)).then_inc(stored[g % 2], 16)
                    else:
                        s = g - QG - KG
                        sp.dma_start(v_d[:, :, bass.ds(t * SUB + s, 1), :].rearrange("g p t d -> p g (t d)"),
                                     v_out[:, g % 2, :].rearrange("p (g d) -> p g d", d=HD)
                                     ).then_inc(stored[g % 2], 16)
                    if g == T_AT + KC - 1 and not last and load_next[0]:
                        sp.wait_ge(transposed, (t + 2) * KC)
                        load_x(t + 2)

            load_next = [True]
            load_w(0)
            load_x(0)
            for k in range(1, KC):
                load_w(k)
            sp.wait_ge(transposed, KC)
            load_x(1)
            tile(0, first=True)
            with sp.Fori(0, NT // 2 - 2) as i:
                tile(2 * i + 1)
                tile(2 * i + 2)
            tile(NT - 3)
            load_next[0] = False
            tile(NT - 2)
            tile(NT - 1, last=True)
            for i in range(2):
                sp.wait_ge(stored[i], NT * HALF)

        @block.tensor
        def _(pe):
            def transpose_chunk(t, k):
                if k == 0:
                    pe.wait_ge(x_in, 16 * t + 16)
                if not (isinstance(t, int) and t * KC + k < TB):
                    pe.wait_ge(xT_lo_done, t * KC + k + 1 - TB)
                for s in range(SUB):
                    last = pe.transpose(tp[k % TB][:, s * P:(s + 1) * P], x_raw[:, s, k * P:(k + 1) * P],
                                        ident[:, :])
                last.then_inc(transposed, 1)

            def tile(t, par, last=False):
                xh, xl = xT_hi[par], xT_lo[par]
                pe.wait_ge(xT_lo_done, (t + 1) * KC)
                for g in range(G):
                    bank = acc[(par * G + g) % GB]
                    if not (isinstance(t, int) and t * G + g < GB):
                        pe.wait_ge(evacuated, t * G + g + 1 - GB)
                    for k in range(KC):
                        if g < QG + KG:
                            cols = slice(g * P, (g + 1) * P)
                            done = matmul3(pe, bank[:, :], w_hi[:, k, cols], w_lo[:, k, cols],
                                           xh[:, k, :], xl[:, k, :], k == 0, k == KC - 1)
                        else:
                            rows = slice((g - QG - KG) * P, (g - QG - KG + 1) * P)
                            done = matmul3(pe, bank[:, 0:KV], xh[:, k, rows], xl[:, k, rows],
                                           w_hi[:, k, D + KV:WC], w_lo[:, k, D + KV:WC], k == 0, k == KC - 1)
                    done.then_inc(group_done, 1)
                    if T_AT <= g < T_AT + KC and not last:
                        transpose_chunk(t + 1, g - T_AT)

            pe.wait_ge(ident_done, 2)
            for k in range(KC):
                transpose_chunk(0, k)
            pe.wait_ge(w_lo_done, KC)
            tile(0, 0)
            with pe.Fori(0, NT // 2 - 1) as i:
                tile(2 * i + 1, 1)
                tile(2 * i + 2, 0)
            tile(NT - 1, 1, last=True)

        @block.scalar
        def _(act):
            def split_x(t, par, k):
                act.wait_ge(transposed, t * KC + k + 1)
                act.activation(xT_hi[par][:, k, :], tp[k % TB][:, :], ACT.Copy).then_inc(xT_hi_done, 1)

            def tile(t, par, last=False):
                for g in range(G):
                    if g < QG + KG:
                        act.wait_ge(stored[g % 2], stored_before(t, g))
                        act.wait_ge(group_done, t * G + g + 1)
                        act.activation(out_hi[:, g % 2, :], acc[(par * G + g) % GB][:, :],
                                       ACT.Copy).then_inc(out_hi_done, 1)
                    if T_AT <= g < T_AT + KC and not last:
                        split_x(t + 1, 1 - par, g - T_AT)

            for k in range(KC):
                act.wait_ge(w_in[k % 2], 48 * (k // 2 + 1))
                act.activation(w_hi[:, k, :], w_raw[:, k % 2, :], ACT.Copy).then_inc(w_hi_done, 1)
                split_x(0, 0, k)
            tile(0, 0)
            with act.Fori(0, NT // 2 - 1) as i:
                tile(2 * i + 1, 1)
                tile(2 * i + 2, 0)
            tile(NT - 1, 1, last=True)

        @block.vector
        def _(dve):
            def split_x(t, par, k):
                dve.wait_ge(xT_hi_done, t * KC + k + 1)
                dve.tensor_tensor(xT_lo[par][:, k, :], tp[k % TB][:, :], xT_hi[par][:, k, :].bitcast(F32),
                                  ALU.subtract).then_inc(xT_lo_done, 1)

            def tile(t, par, last=False):
                for g in range(G):
                    bank = acc[(par * G + g) % GB]
                    if g < QG + KG:
                        dve.wait_ge(out_hi_done, t * (QG + KG) + g + 1)
                        dve.tensor_tensor(out_lo[:, g % 2, :], bank[:, :], out_hi[:, g % 2, :].bitcast(F32),
                                          ALU.subtract).then_inc(evacuated, 1)
                    else:
                        dve.wait_ge(stored[g % 2], stored_before(t, g))
                        dve.wait_ge(group_done, t * G + g + 1)
                        dve.tensor_copy(v_out[:, g % 2, :], bank[:, 0:KV]).then_inc(evacuated, 1)
                    if T_AT <= g < T_AT + KC and not last:
                        split_x(t + 1, 1 - par, g - T_AT)

            for k in range(KC):
                dve.wait_ge(w_hi_done, k + 1)
                dve.tensor_tensor(w_lo[:, k, :], w_raw[:, k % 2, :], w_hi[:, k, :].bitcast(F32),
                                  ALU.subtract).then_inc(w_lo_done, 1)
                split_x(0, 0, k)
            tile(0, 0)
            with dve.Fori(0, NT // 2 - 1) as i:
                tile(2 * i + 1, 1)
                tile(2 * i + 2, 0)
            tile(NT - 1, 1, last=True)


def attend(nc, sem, q_hi, q_lo, k_hi, k_lo, v_d, aT_d):
    NG = B * NKV
    CH = 512
    NC = S // CH
    SUB = CH // P
    NT = S // P
    ROWS = 3 * HD
    STEPS = [(c, t) for c in range(NC) for t in range(SUB * (c + 1))]
    NS = len(STEPS)
    FIRST_STEP = [STEPS.index((c, 0)) for c in range(NC)] + [NS]
    PB = 4
    assert NS % PB == 0
    FIN = 1

    def offset(c, t):
        return max(0, t - SUB * c) * P

    def summed_by_pe(c, t):
        return c > 0 and t % 3 == 2

    TLAG = 4
    units = [[("score", c, h, i, j) for h in range(REP) for i in range(SUB) for j in range(c + 1)]
             for c in range(NC)]
    ITEMS = []
    for c in range(NC):
        ITEMS += units[c][:TLAG] + ([("maxrow", c - 1)] if c else []) + units[c][TLAG:]
    ITEMS.append(("maxrow", NC - 1))
    NI = len(ITEMS)
    assert NI % 2 == 0
    LEAD = 3
    ITEM_OF_STEP = [max(0, (s - LEAD) * NI // (NS - LEAD)) for s in range(NS)] + [NI]
    STEP_OF_ITEM = [max(s for s in range(NS) if ITEM_OF_STEP[s] <= i) for i in range(NI)]

    POOL_STEPS = [s for s, (c, t) in enumerate(STEPS) if not summed_by_pe(c, t) and (t > 0 or c == 0)]
    NPOOL = len(POOL_STEPS)

    def pool_steps_through(s):
        return sum(x <= s for x in POOL_STEPS) if s >= 0 else sum(x <= s + NS for x in POOL_STEPS) - NPOOL

    def at_least(engine, semaphore, value):
        if not isinstance(value, int) or value > 0:
            engine.wait_ge(semaphore, value)

    ctx = ExitStack()
    with ctx:
        sb = lambda name, shape, dt: ctx.enter_context(nc.sbuf_tensor(name, shape, dt))
        ps = lambda name, shape: ctx.enter_context(nc.psum_tensor(name, shape, F32))
        ident = sb("p2_ident", [P, P], F32)
        ident_bf = sb("p2_ident_bf", [P, P], BF16)
        mask_q = sb("p2_mask_q", [P, P], BF16)
        mask_k = sb("p2_mask_k", [P, P], BF16)
        ones = sb("p2_ones", [P, HD], F32)
        zeros = sb("p2_zeros", [P, REP, P], F32)
        q_st = [sb(f"p2_q_st{i}", [P, REP, S], F32R) for i in range(2)]
        k_st = [sb(f"p2_k_st{i}", [P, S], F32R) for i in range(2)]
        v = [sb(f"p2_v{i}", [P, NT, HD], F32) for i in range(2)]
        probs = [sb(f"p2_probs{i}", [P, REP, CH], F32) for i in range(PB)]
        psums = [sb(f"p2_psums{i}", [P, REP, CH], F32) for i in range(2)]
        part_max = [sb(f"p2_part_max{c}", [P, REP * SUB, c + 1], F32) for c in range(NC)]
        row_max = [sb(f"p2_row_max{c}", [P, REP * SUB], F32) for c in range(NC)]
        neg_max = [sb(f"p2_neg_max{c}", [REP, CH], F32R) for c in range(NC)]
        o_raw = [sb(f"p2_o_raw{i}", [P, CH], F32) for i in range(2)]
        recip = sb("p2_recip", [P, CH], F32)
        o_out = [sb(f"p2_o_out{i}", [P, CH], F32) for i in range(2)]
        qm = [ps(f"p2_qm{i}", [P, BANK]) for i in range(2)]
        km = [ps(f"p2_km{i}", [P, 2, BANK]) for i in range(2)]
        o_ps = ps("p2_o", [P, BANK])
        d_ps = ps("p2_d", [P, BANK])

        ident_done = sem("p2_ident_done")
        consts_done = sem("p2_consts_done")
        q_in = [[sem(f"p2_q_in{i}_{c}") for c in range(NC)] for i in range(2)]
        k_in = [sem(f"p2_k_in{i}") for i in range(2)]
        v_in = [sem(f"p2_v_in{i}") for i in range(2)]
        m_in = [[sem(f"p2_m_in{i}_{c}") for c in range(NC)] for i in range(2)]
        item_done = sem("p2_item_done")
        item_read = sem("p2_item_read")
        max_done = sem("p2_max_done")
        scored = sem("p2_scored")
        exp_done = sem("p2_exp_done")
        pv_done = sem("p2_pv_done")
        added = sem("p2_added")
        o_read = sem("p2_o_read")
        sums_done = sem("p2_sums_done")
        recip_done = sem("p2_recip_done")
        normed = sem("p2_normed")
        stored = [sem(f"p2_stored{i}") for i in range(2)]
        held = sem("p2_held")

        block = ctx.enter_context(nc.Block())


        @block.sync
        def _(sp):
            def batch_head(n):
                b, g = (n >> (NKV.bit_length() - 1)) & (B - 1), n & (NKV - 1)
                return b, g

            def hold():
                sp.sem_inc(held, 1)

            def load_q(b, g, par, c):
                rows, cols = bass.ds(g * P, P), bass.ds(b * S + c * CH, CH)
                for at, src in ((0, q_hi), (HD, q_lo), (2 * HD, q_hi)):
                    sp.dma_start(q_st[par][at:at + HD, :, c * CH:(c + 1) * CH].bitcast(F32),
                                 src[rows, cols].rearrange("(h d) t -> d h t", d=HD)).then_inc(q_in[par][c], 16)

            def load_k(b, g, par):
                rows, cols = bass.ds(g * HD, HD), bass.ds(b * S, S)
                for at, src in ((0, k_hi), (HD, k_hi), (2 * HD, k_lo)):
                    sp.dma_start(k_st[par][at:at + HD, :].bitcast(F32), src[rows, cols]).then_inc(k_in[par], 16)

            def load_v(b, g, par):
                sp.dma_start(v[par][:, :, :],
                             v_d[bass.ds(g, 1), :, bass.ds(b * NT, NT), :].rearrange("g p t d -> (g p) t d")
                             ).then_inc(v_in[par], 16)

            def send_max(done, par, c):
                sp.wait_ge(item_read, done)
                sp.dma_start(q_st[par][ROWS:ROWS + 1, :, c * CH:(c + 1) * CH].bitcast(F32),
                             neg_max[c][:, :].bitcast(F32)).then_inc(m_in[par][c], 16)

            def store_out(n, b, g, c):
                sp.wait_ge(normed, n * NC + c + 1)
                hold()
                sp.dma_start(aT_d[bass.ds(g * P, P), bass.ds(b * S + c * CH, CH)],
                             o_out[c % 2][:, :]).then_inc(stored[c % 2], 16)

            def group(n, par, last=False, load=True):
                b, g = batch_head(n)
                b2, g2 = batch_head(n + 2)
                before = batch_head(n - 1)
                events = []
                for c in range(NC):
                    end = FIRST_STEP[c + 1]
                    if load:
                        events.append((end + 0.5, "load", c))
                    if c < NC - 1:
                        events.append((end + FIN + 2.5, "store", c))
                    if not last:
                        events.append((STEP_OF_ITEM[ITEMS.index(("maxrow", c))] + 1, "max", c))
                events.append((FIN + 2.5, "store before", NC - 1))
                for _, what, c in sorted(events):
                    if what == "load":
                        sp.wait_ge(scored, 2 * (n * NS + FIRST_STEP[c + 1]))
                        hold()
                        load_q(b2, g2, par, c)
                        if c == NC - 1:
                            load_k(b2, g2, par)
                            sp.wait_ge(pv_done, (n + 1) * NS)
                            hold()
                            load_v(b2, g2, par)
                    elif what == "store":
                        store_out(n, b, g, c)
                    elif what == "max":
                        send_max((n + 1) * NI + ITEMS.index(("maxrow", c)) + 1, 1 - par, c)
                    elif not (isinstance(n, int) and n == 0):
                        store_out(n - 1, *before, c)

            load_k(0, 0, 0)
            for c in range(NC):
                load_q(0, 0, 0, c)
            load_v(0, 0, 0)
            load_k(0, 1, 1)
            for c in range(NC):
                load_q(0, 1, 1, c)
            load_v(0, 1, 1)
            for c in range(NC):
                send_max(ITEMS.index(("maxrow", c)) + 1, 0, c)
            group(0, 0)
            with sp.Fori(0, NG // 2 - 2) as i:
                group(2 * i + 1, 1)
                group(2 * i + 2, 0)
            group(NG - 3, 1)
            group(NG - 2, 0, load=False)
            group(NG - 1, 1, last=True, load=False)
            store_out(NG - 1, B - 1, NKV - 1, NC - 1)
            for i in range(2):
                sp.wait_ge(stored[i], 16 * NG * NC // 2)

        @block.gpsimd
        def _(pool):
            make_identity(pool, ident, ident_done)
            pool.memset(ones[:, :], 1.0).then_inc(consts_done, 1)
            pool.memset(zeros[:, :, :], 0.0).then_inc(ident_done, 1)
            pool.memset(mask_q[:, :], 0.0).then_inc(ident_done, 1)
            pool.memset(mask_k[:, :], 0.0).then_inc(ident_done, 1)
            pool.wait_ge(ident_done, 5)
            pool.tensor_copy(ident_bf[:, :], ident[:, :]).then_inc(consts_done, 1)
            pool.affine_select(out=mask_q[:, :], in_=mask_q[:, :], compare_op=ALU.is_ge, fill=NEG,
                               base=0, pattern=[[-1, P]], channel_multiplier=1).then_inc(consts_done, 1)
            pool.affine_select(out=mask_k[:, :], in_=mask_k[:, :], compare_op=ALU.is_ge, fill=NEG,
                               base=0, pattern=[[1, P]], channel_multiplier=-1).then_inc(consts_done, 1)

            def group(n):
                for s in POOL_STEPS:
                    c, t = STEPS[s]
                    o = offset(c, t)
                    sums, new = psums[c % 2], probs[s % PB]
                    if t == (c > 0):
                        at_least(pool, sums_done, n * NC + c - 1)
                    pool.wait_ge(exp_done, 2 * (n * NS + s + 1))
                    if t == 0:
                        pool.tensor_tensor(sums[:, :, 0:P], new[:, :, 0:P], zeros[:, :, :], ALU.add).then_inc(added, 1)
                    elif t == 1:
                        pool.tensor_tensor(sums[:, :, o:CH], probs[(s - 1) % PB][:, :, o:CH], new[:, :, o:CH],
                                           ALU.add).then_inc(added, 1)
                    else:
                        pool.wait_ge(added, n * NPOOL + pool_steps_through(s) - 1)
                        pool.tensor_tensor(sums[:, :, o:CH], sums[:, :, o:CH], new[:, :, o:CH], ALU.add
                                           ).then_inc(added, 1)

            group(0)
            with pool.Fori(0, NG // 2 - 1) as i:
                group(2 * i + 1)
                group(2 * i + 2)
            group(NG - 1)

        @block.tensor
        def _(pe):
            def item(m, par, i):
                at_least(pe, item_read, m * NI + i - 1)
                bank = qm[i % 2]
                if ITEMS[i][0] == "maxrow":
                    c = ITEMS[i][1]
                    pe.wait_ge(max_done, m * NC + c + 1)
                    for sub in range(SUB):
                        last = pe.transpose(bank[0:REP, sub * P:(sub + 1) * P],
                                            row_max[c][:, sub * REP:(sub + 1) * REP], ident[:, :])
                    last.then_inc(item_done, 1)
                    return
                _, c, h, sub, j = ITEMS[i]
                if (h, sub, j) == (0, 0, 0):
                    pe.wait_ge(q_in[par][c], 48 * (m // 2 + 1) if isinstance(m, int) else q_loads(m, par))
                    if c == 0:
                        pe.wait_ge(k_in[par], 48 * (m // 2 + 1) if isinstance(m, int) else q_loads(m, par))
                q0 = c * CH + sub * P
                w = min(BANK, (SUB * c + sub + 1) * P - j * BANK)
                last = pe.matmul(bank[:, 0:w], q_st[par][0:ROWS, h, q0:q0 + P],
                                 k_st[par][0:ROWS, j * BANK:j * BANK + w], start=True, stop=j < c)
                if j == c:
                    last = pe.matmul(bank[:, w - P:w], ident_bf[:, :], mask_q[:, :], start=False, stop=True)
                last.then_inc(item_done, 1)

            def q_loads(m, par):
                return 24 * (m - par) + 48

            def scores(n, par, s, half):
                c, t = STEPS[s]
                o = offset(c, t)
                at_least(pe, exp_done, 2 * (n * NS + s) + half - 1)
                if half == 0 and t == 0:
                    pe.wait_ge(m_in[par][c], q_loads(n, par) // 3)
                diag = t >= SUB * c
                for x in range(2):
                    h = 2 * half + x
                    last = pe.matmul(km[half][:, x, o:CH], k_st[par][0:ROWS + 1, t * P:(t + 1) * P],
                                     q_st[par][0:ROWS + 1, h, c * CH + o:(c + 1) * CH], start=True, stop=not diag)
                    if diag:
                        last = pe.matmul(km[half][:, x, o:o + P], ident_bf[:, :], mask_k[:, :],
                                         start=False, stop=True)
                last.then_inc(scored, 1)

            def heads_matmul(out, lhs, rhs, o, start, stop):
                for h in range(REP):
                    last = pe.matmul(out[h * HD:(h + 1) * HD, o:CH], lhs, rhs[:, h, o:CH], start=start, stop=stop)
                return last

            def sums(n, s):
                c, t = STEPS[s]
                pe.wait_ge(exp_done, 2 * (n * NS + s + 1))
                if t == 2:
                    pe.wait_ge(recip_done, n * NC + c)
                heads_matmul(d_ps, ones[:, :], probs[s % PB], offset(c, t), t == 2, False)

            def values(n, par, s):
                c, t = STEPS[s]
                if s == 0:
                    pe.wait_ge(v_in[par], q_loads(n, par) // 3)
                pe.wait_ge(exp_done, 2 * (n * NS + s + 1))
                if t == 0:
                    at_least(pe, o_read, n * NC + c)
                heads_matmul(o_ps, v[par][:, t, :], probs[s % PB], offset(c, t), t == 0,
                             t == SUB * (c + 1) - 1).then_inc(pv_done, 1)

            def finish(n, c):
                pe.wait_ge(added, n * NPOOL + pool_steps_through(FIRST_STEP[c + 1] - 1))
                if c == 0:
                    at_least(pe, recip_done, n * NC + c)
                heads_matmul(d_ps, ones[:, :], psums[c % 2], 0, c == 0, True).then_inc(sums_done, 1)

            def group(n, par, last=False):
                for s in range(NS + 1):
                    todo = list(range(ITEM_OF_STEP[s], ITEM_OF_STEP[s + 1])) if s < NS and not last else []

                    def items(share):
                        for _ in range(min(len(todo), share)):
                            item(n + 1, 1 - par, todo.pop(0))

                    if s < NS:
                        scores(n, par, s, 0)
                        items(1)
                        scores(n, par, s, 1)
                        items(1)
                    if s > 0:
                        if summed_by_pe(*STEPS[s - 1]):
                            sums(n, s - 1)
                            items(1)
                        values(n, par, s - 1)
                        items(1)
                        c, t = STEPS[s - 1]
                        if t == FIN and c > 0:
                            finish(n, c - 1)
                        elif t == FIN and not (isinstance(n, int) and n == 0):
                            finish(n - 1, NC - 1)
                    items(NI)

            pe.wait_ge(ident_done, 2)
            pe.wait_ge(consts_done, 6)
            for i in range(NI):
                item(0, 0, i)
            group(0, 0)
            with pe.Fori(0, NG // 2 - 1) as i:
                group(2 * i + 1, 1)
                group(2 * i + 2, 0)
            group(NG - 1, 1, last=True)
            finish(NG - 1, NC - 1)

        @block.scalar
        def _(act):
            def group(n, par):
                for s in range(NS + 1):
                    if s < NS:
                        c, t = STEPS[s]
                        o = offset(c, t)
                        at_least(act, pv_done, n * NS + s + 1 - PB)
                        before = s - PB
                        if not summed_by_pe(*STEPS[before % NS]):
                            before += STEPS[before % NS][1] == 0
                            at_least(act, added, n * NPOOL + pool_steps_through(before))
                        for half in range(2):
                            act.wait_ge(scored, 2 * (n * NS + s) + half + 1)
                            act.activation(probs[s % PB][:, 2 * half:2 * half + 2, o:CH], km[half][:, :, o:CH],
                                           ACT.Exp, scale=SCALE).then_inc(exp_done, 1)
                    if s > 0 and (s == NS or STEPS[s][1] == 0):
                        c = STEPS[s - 1][0]
                        act.wait_ge(pv_done, n * NS + s)
                        at_least(act, normed, n * NC + c - 1)
                        act.activation(o_raw[c % 2][:, :], o_ps[:, :], ACT.Copy).then_inc(o_read, 1)

            group(0, 0)
            with act.Fori(0, NG // 2 - 1) as i:
                group(2 * i + 1, 1)
                group(2 * i + 2, 0)
            group(NG - 1, 1)

        @block.vector
        def _(dve):
            def item(m, i):
                dve.wait_ge(item_done, m * NI + i + 1)
                bank = qm[i % 2]
                if ITEMS[i][0] == "maxrow":
                    c = ITEMS[i][1]
                    dve.tensor_scalar(neg_max[c][:, :], bank[0:REP, 0:CH], -1.0, None, ALU.mult
                                      ).then_inc(item_read, 1)
                    return
                _, c, h, sub, j = ITEMS[i]
                w = min(BANK, (SUB * c + sub + 1) * P - j * BANK)
                dve.reduce_max(part_max[c][:, sub * REP + h, j:j + 1], bank[:, 0:w], AX.X).then_inc(item_read, 1)
                if (h, sub, j) == (REP - 1, SUB - 1, c):
                    dve.wait_ge(item_read, m * NI + i + 1)
                    dve.reduce_max(row_max[c][:, :], part_max[c][:, :, :], AX.X).then_inc(max_done, 1)

            def finish(n, c):
                dve.wait_ge(sums_done, n * NC + c + 1)
                at_least(dve, normed, n * NC + c)
                dve.reciprocal(recip[:, :], d_ps[:, :]).then_inc(recip_done, 1)
                dve.wait_ge(recip_done, n * NC + c + 1)
                dve.wait_ge(o_read, n * NC + c + 1)
                dve.wait_ge(stored[c % 2], 16 * (n * NC // 2 + c // 2) if isinstance(n, int)
                            else n * (8 * NC) + 16 * (c // 2))
                dve.tensor_tensor(o_out[c % 2][:, :], o_raw[c % 2][:, :], recip[:, :], ALU.mult
                                  ).then_inc(normed, 1)

            def group(n, last=False):
                for s in range(NS + 1):
                    if s < NS and not last:
                        for i in range(ITEM_OF_STEP[s], ITEM_OF_STEP[s + 1]):
                            item(n + 1, i)
                    if s > 0:
                        c, t = STEPS[s - 1]
                        if t == FIN and c > 0:
                            finish(n, c - 1)
                        elif t == FIN and not (isinstance(n, int) and n == 0):
                            finish(n - 1, NC - 1)

            for i in range(2):
                dve.memset(k_st[i][ROWS:ROWS + 1, :].bitcast(F32), 1.0).then_inc(consts_done, 1)
            for i in range(NI):
                item(0, i)
            group(0)
            with dve.Fori(0, NG // 2 - 1) as i:
                group(2 * i + 1)
                group(2 * i + 2)
            group(NG - 1, last=True)
            finish(NG - 1, NC - 1)


class Chain:

    def __init__(self, engine, semaphore, held):
        self.engine, self.semaphore, self.held, self.base, self.n = engine, semaphore, held, 0, 0

    def start(self, base):
        self.base, self.n = base, 0

    def link(self, instruction):
        self.n += 1
        instruction.then_inc(self.semaphore, 1)
        self.engine.wait_ge(self.semaphore, self.base + self.n)

    def hold(self):
        self.engine.sem_inc(self.held, 1)


def moments(dve, chain, rows, width, stats, mean_var):
    parts = max(1, width // BANK)
    for i in range(parts):
        ins = dve.bn_stats(stats[:, i, :], rows[:, i * (width // parts):(i + 1) * (width // parts)])
        if i == parts - 1:
            chain.link(ins)
    chain.hold()
    chain.link(dve.bn_aggr(mean_var, stats[:, 0:parts, :]))


def project_and_gate(nc, sem, keep, x, aT_d, wo, weight, lora_A, gw1, gb1, gamma, beta, gw2, gb2, u_d):
    ER = E * R
    AG = ER + GH
    NT = N // P
    HALF = D // 2
    STEPS = NT + 2
    low, diff, onehot = keep
    x_t = x.rearrange("b (t p) d -> (b t) p d", p=P)
    u_t = u_d.rearrange("(t p) d -> t p d", p=P)

    def at_least(engine, semaphore, value):
        if not isinstance(value, int) or value > 0:
            engine.wait_ge(semaphore, value)

    ctx = ExitStack()
    with ctx:
        sb = lambda name, shape, dt=F32: ctx.enter_context(nc.sbuf_tensor(name, shape, dt))
        ps = lambda name, shape: ctx.enter_context(nc.psum_tensor(name, shape, F32))
        ident = sb("p3_ident", [P, P])
        ones_row = sb("p3_ones_row", [1, P])
        eps = sb("p3_eps", [P, 1])
        experts = sb("p3_experts", [P, E])
        experts_i = sb("p3_experts_i", [P, E], I32)
        wo_hi, wo_lo = sb("p3_wo_hi", [P, KC, D], F32R), sb("p3_wo_lo", [P, KC, D], F32R)
        wm_hi, wm_lo = sb("p3_wm_hi", [P, KC, D], F32R), sb("p3_wm_lo", [P, KC, D], F32R)
        ag_hi, ag_lo = sb("p3_ag_hi", [P, KC, AG], F32R), sb("p3_ag_lo", [P, KC, AG], F32R)
        gw2_raw = sb("p3_gw2_raw", [E, GH])
        gw2T = sb("p3_gw2T", [GH, E])
        rows_raw = sb("p3_rows_raw", [1, 3 * GH + E])
        rows = sb("p3_rows", [P, 3 * GH + E])
        x_in_sb = [sb(f"p3_x{i}", [P, D]) for i in range(2)]
        y = [sb(f"p3_y{i}", [P, D]) for i in range(2)]
        a_raw = sb("p3_a_raw", [P, KC, P])
        a_hi = [sb(f"p3_a_hi{i}", [P, KC, P], F32R) for i in range(2)]
        a_lo = [sb(f"p3_a_lo{i}", [P, KC, P], F32R) for i in range(2)]
        yT_hi, yT_lo = sb("p3_yT_hi", [P, KC, P], F32R), sb("p3_yT_lo", [P, KC, P], F32R)
        stats = sb("p3_stats", [P, 2, 6])
        mean_var = sb("p3_mean_var", [P, 2])
        std = sb("p3_std", [P, 1])
        rstd = sb("p3_rstd", [P, 1])
        g_stats = sb("p3_g_stats", [P, 1, 6])
        g_mean_var = sb("p3_g_mean_var", [P, 2])
        g_std = sb("p3_g_std", [P, 1])
        g_rstd = sb("p3_g_rstd", [P, 1])
        hid = [sb(f"p3_hid{i}", [P, GH]) for i in range(2)]
        hidT = sb("p3_hidT", [GH, P])
        gates = sb("p3_gates", [P, E])
        top = sb("p3_top", [P, 8])
        top_at = sb("p3_top_at", [P, 8], U32)
        top_at_f = sb("p3_top_at_f", [P, 8])
        at_ps = ps("p3_at_ps", [P, 2, BANK])
        tr_ps = ps("p3_tr_ps", [P, 2, BANK])
        mm_ps = ps("p3_mm_ps", [P, 2, BANK])
        ag_ps = ps("p3_ag_ps", [P, BANK])
        sm_ps = ps("p3_sm_ps", [P, BANK])

        ident_done = sem("p3_ident_done")
        pool_const = sem("p3_pool_const")
        raw_in = [sem(f"p3_raw_in{i}") for i in range(2)]
        small_in = sem("p3_small_in")
        turned = sem("p3_turned")
        w_hi_done, w_lo_done = sem("p3_w_hi_done"), sem("p3_w_lo_done")
        small_pe, small_dve = sem("p3_small_pe"), sem("p3_small_dve")
        x_in = [sem(f"p3_x_in{i}") for i in range(2)]
        a_in = sem("p3_a_in")
        a_hi_done, a_lo_done = sem("p3_a_hi_done"), sem("p3_a_lo_done")
        wo_done = sem("p3_wo_done")
        sum_done = sem("p3_sum_done")
        var_done, std_done = sem("p3_var_done"), sem("p3_std_done")
        y_done = sem("p3_y_done")
        tr_done = sem("p3_tr_done")
        yT_hi_done, yT_lo_done = sem("p3_yT_hi_done"), sem("p3_yT_lo_done")
        mm_done = sem("p3_mm_done")
        u_done = sem("p3_u_done")
        u_stored = [sem(f"p3_u_stored{i}") for i in range(2)]
        ag_done = sem("p3_ag_done")
        low_done = sem("p3_low_done")
        h_done = sem("p3_h_done")
        g_var_done, g_std_done = sem("p3_g_var_done"), sem("p3_g_std_done")
        hid_done = sem("p3_hid_done")
        hidT_ps_done, hidT_done = sem("p3_hidT_ps_done"), sem("p3_hidT_done")
        gates_ps_done, gates_done = sem("p3_gates_ps_done"), sem("p3_gates_done")
        chain_sem, held_sem = sem("p3_chain"), sem("p3_held")

        block = ctx.enter_context(nc.Block())
        LOOPS = (NT - 2) // 2


        @block.sync
        def _(sp):
            def load_a(t):
                sp.dma_start(a_raw[:, :, :], aT_d[:, bass.ds(t * P, P)].rearrange("(k p) t -> p k t", p=P)
                             ).then_inc(a_in, 16)

            def load_x(t, par):
                sp.dma_start(x_in_sb[par][:, :], x_t[bass.ds(t, 1), :, :].rearrange("o p d -> (o p) d")
                             ).then_inc(x_in[par], 16)

            def step(t, par):
                if not isinstance(t, int) or t + 2 < NT:
                    sp.wait_ge(a_lo_done, t + 2)
                    load_a(t + 2)
                    sp.wait_ge(sum_done, t + 1)
                    load_x(t + 2, par)
                if not isinstance(t, int) or t >= 1:
                    sp.wait_ge(u_done, t)
                    sp.dma_start(u_t[bass.ds(t - 1, 1), :, :].rearrange("o p d -> (o p) d"),
                                 y[1 - par][:, :]).then_inc(u_stored[1 - par], 16)

            sp.dma_start(gw2_raw[:, :], gw2).then_inc(small_in, 16)
            for i, row in enumerate((gb1, gamma, beta, gb2)):
                sp.dma_start(rows_raw[:, i * GH:i * GH + row.shape[0]],
                             row.rearrange("(o n) -> o n", o=1)).then_inc(small_in, 16)
            sp.dma_start(y[1][0:GH, :], gw1).then_inc(small_in, 16)
            for k in range(KC):
                sp.dma_start(y[0][:, k * ER:(k + 1) * ER].rearrange("p (e r) -> p e r", e=E),
                             lora_A[:, k * P:(k + 1) * P, :].rearrange("e p r -> p e r")).then_inc(small_in, 16)
            load_a(0)
            for n in range(2 * KC):
                if n >= 2:
                    sp.wait_ge(w_lo_done, 2 * (n - 1))
                src = wo if n < KC else weight
                sp.dma_start(x_in_sb[n % 2][:, :], src[(n % KC) * P:(n % KC + 1) * P, :]).then_inc(raw_in[n % 2], 16)
            for t in range(2):
                sp.wait_ge(w_lo_done, 2 * (2 * KC - 1 + t))
                load_x(t, t)
            sp.wait_ge(a_lo_done, 1)
            load_a(1)
            step(0, 0)
            step(1, 1)
            with sp.Fori(0, LOOPS - 1) as i:
                step(2 * i + 2, 0)
                step(2 * i + 3, 1)
            step(NT - 2, 0)
            step(NT - 1, 1)
            step(NT, 0)
            for i in range(2):
                sp.wait_ge(u_stored[i], 16 * NT // 2)

        @block.gpsimd
        def _(pool):
            make_identity(pool, ident, ident_done)
            pool.memset(ones_row[:, :], 1.0).then_inc(pool_const, 1)
            pool.memset(eps[:, :], LN_EPS).then_inc(pool_const, 1)
            pool.iota(experts_i[:, :], pattern=[[1, E]], base=0, channel_multiplier=0).then_inc(pool_const, 1)

        @block.tensor
        def _(pe):
            pe.wait_ge(ident_done, 2)
            pe.wait_ge(pool_const, 3)
            pe.wait_ge(small_in, 16 * (6 + KC))
            pe.transpose(sm_ps[0:GH, 0:E], gw2_raw[:, :], ident[0:E, 0:E])
            pe.matmul(sm_ps[:, P:P + 3 * GH + E], ones_row[:, :], rows_raw[:, :], start=True, stop=True)
            for k in range(KC):
                last = pe.transpose(ag_ps[:, k * GH:(k + 1) * GH], y[1][0:GH, k * P:(k + 1) * P],
                                    ident[0:GH, 0:GH])
            last.then_inc(small_pe, 1)
            for n in range(KC):
                pe.wait_ge(raw_in[n % 2], 16 * ((KC + n) // 2 + 1))
                for half in range(2):
                    if n > 0:
                        pe.wait_ge(w_lo_done, 2 * (KC + n - 1) + half + 1)
                    for k in range(half * 4, half * 4 + 4):
                        last = pe.transpose(tr_ps[:, half, (k % 4) * P:(k % 4 + 1) * P],
                                            x_in_sb[n % 2][:, k * P:(k + 1) * P], ident[:, :])
                    last.then_inc(turned, 1)

            def step(t, par):
                a_ok = not isinstance(t, int) or t < NT
                b_ok = not isinstance(t, int) or 1 <= t <= NT
                c_ok = not isinstance(t, int) or t >= 2
                if a_ok:
                    at_least(pe, sum_done, t)
                    pe.wait_ge(a_lo_done, t + 1)
                    for half in range(2):
                        cols = slice(half * HALF, (half + 1) * HALF)
                        for k in range(KC):
                            last = matmul3(pe, at_ps[:, half, :], a_hi[par][:, k, :], a_lo[par][:, k, :],
                                           wo_hi[:, k, cols], wo_lo[:, k, cols], k == 0, k == KC - 1)
                    last.then_inc(wo_done, 1)
                if c_ok:
                    pe.wait_ge(hid_done, t - 1)
                    at_least(pe, gates_done, t - 2)
                    pe.transpose(sm_ps[0:GH, 0:P], hid[par][:, :], ident[:, :]).then_inc(hidT_ps_done, 1)
                if b_ok:
                    pe.wait_ge(yT_lo_done, t)
                    at_least(pe, u_done, t - 1)
                    for half in range(2):
                        cols = slice(half * HALF, (half + 1) * HALF)
                        for k in range(KC):
                            last = matmul3(pe, mm_ps[:, half, :], yT_hi[:, k, :], yT_lo[:, k, :],
                                           wm_hi[:, k, cols], wm_lo[:, k, cols], k == 0, k == KC - 1)
                    last.then_inc(mm_done, 1)
                    at_least(pe, low_done, t - 1)
                    at_least(pe, h_done, t - 1)
                    for k in range(KC):
                        last = matmul3(pe, ag_ps[:, 0:AG], yT_hi[:, k, :], yT_lo[:, k, :],
                                       ag_hi[:, k, :], ag_lo[:, k, :], k == 0, k == KC - 1)
                    last.then_inc(ag_done, 1)
                if c_ok:
                    pe.wait_ge(hidT_done, t - 1)
                    pe.matmul(sm_ps[:, P:P + E], hidT[:, :], gw2T[:, :], start=True, stop=True
                              ).then_inc(gates_ps_done, 1)
                if a_ok:
                    pe.wait_ge(y_done, t + 1)
                    at_least(pe, yT_lo_done, t)
                    for k in range(KC):
                        last = pe.transpose(tr_ps[:, k // 4, (k % 4) * P:(k % 4 + 1) * P],
                                            y[par][:, k * P:(k + 1) * P], ident[:, :])
                    last.then_inc(tr_done, 1)

            pe.wait_ge(w_lo_done, 4 * KC)
            pe.wait_ge(small_dve, 5)
            step(0, 0)
            step(1, 1)
            with pe.Fori(0, LOOPS) as i:
                step(2 * i + 2, 0)
                step(2 * i + 3, 1)
            step(NT, 0)
            step(NT + 1, 1)

        @block.scalar
        def _(act):
            def split_a(t, par):
                act.wait_ge(a_in, 16 * (t + 1))
                at_least(act, wo_done, t - 1)
                act.activation(a_hi[par][:, :, :], a_raw[:, :, :], ACT.Copy).then_inc(a_hi_done, 1)

            def step(t, par):
                a_ok = not isinstance(t, int) or t < NT
                b_ok = not isinstance(t, int) or 1 <= t <= NT
                c_ok = not isinstance(t, int) or t >= 2
                if not isinstance(t, int) or t + 1 < NT:
                    split_a(t + 1, 1 - par)
                if a_ok:
                    act.wait_ge(var_done, t + 1)
                    act.activation(std[:, :], mean_var[:, 1:2], ACT.Sqrt, bias=eps[:, :]).then_inc(std_done, 1)
                if c_ok:
                    act.wait_ge(hidT_ps_done, t - 1)
                    act.activation(hidT[:, :], sm_ps[0:GH, 0:P], ACT.Copy).then_inc(hidT_done, 1)
                if b_ok:
                    act.wait_ge(ag_done, t)
                    act.activation(low[:, bass.ds(t - 1, 1), :].rearrange("p o r -> p (o r)"), ag_ps[:, 0:ER],
                                   ACT.Copy).then_inc(low_done, 1)
                    act.wait_ge(g_var_done, t)
                    act.activation(g_std[:, :], g_mean_var[:, 1:2], ACT.Sqrt, bias=eps[:, :]
                                   ).then_inc(g_std_done, 1)
                if a_ok:
                    act.wait_ge(tr_done, t + 1)
                    act.activation(yT_hi[:, :, :].rearrange("p k t -> p (k t)"),
                                   tr_ps[:, :, :].rearrange("p a b -> p (a b)"), ACT.Copy
                                   ).then_inc(yT_hi_done, 1)

            for n in range(KC):
                act.wait_ge(raw_in[n % 2], 16 * (n // 2 + 1))
                for half in range(2):
                    cols = slice(half * HALF, (half + 1) * HALF)
                    act.activation(wo_hi[:, n, cols], x_in_sb[n % 2][:, cols], ACT.Copy).then_inc(w_hi_done, 1)
            split_a(0, 0)
            for n in range(KC):
                for half in range(2):
                    act.wait_ge(turned, 2 * n + half + 1)
                    act.activation(wm_hi[:, 4 * half:4 * half + 4, n * P:(n + 1) * P],
                                   tr_ps[:, half, :].rearrange("p (k o) -> p k o", k=4), ACT.Copy
                                   ).then_inc(w_hi_done, 1)
            act.wait_ge(pool_const, 3)
            step(0, 0)
            step(1, 1)
            with act.Fori(0, LOOPS - 1) as i:
                step(2 * i + 2, 0)
                step(2 * i + 3, 1)
            step(NT - 2, 0)
            step(NT - 1, 1)
            step(NT, 0)
            step(NT + 1, 1)

        @block.vector
        def _(dve):
            chain = Chain(dve, chain_sem, held_sem)
            gb1_b, gamma_b, beta_b, gb2_b = (rows[:, 0:GH], rows[:, GH:2 * GH], rows[:, 2 * GH:3 * GH],
                                             rows[:, 3 * GH:3 * GH + E])

            def split_a(t, par):
                dve.wait_ge(a_hi_done, t + 1)
                at_least(dve, wo_done, t - 1)
                dve.tensor_tensor(a_lo[par][:, :, :], a_raw[:, :, :], a_hi[par][:, :, :].bitcast(F32),
                                  ALU.subtract).then_inc(a_lo_done, 1)

            def step(t, par):
                a_ok = not isinstance(t, int) or t < NT
                b_ok = not isinstance(t, int) or 1 <= t <= NT
                c_ok = not isinstance(t, int) or t >= 2
                if not isinstance(t, int) or t + 1 < NT:
                    split_a(t + 1, 1 - par)
                if a_ok:
                    dve.wait_ge(x_in[par], 16 * (t // 2 + 1) if isinstance(t, int) else 8 * (t - par) + 16)
                    if not isinstance(t, int) or t >= 2:
                        dve.wait_ge(u_stored[par], 16 * (t // 2) if isinstance(t, int) else 8 * (t - par))
                    dve.wait_ge(wo_done, t + 1)
                    dve.tensor_tensor(y[par][:, :], at_ps[:, :, :].rearrange("p a b -> p (a b)"),
                                      x_in_sb[par][:, :], ALU.add).then_inc(sum_done, 1)
                    dve.wait_ge(sum_done, t + 1)
                    moments(dve, chain, y[par], D, stats, mean_var[:, :])
                    dve.sem_inc(var_done, 1)
                    dve.wait_ge(std_done, t + 1)
                    chain.link(dve.reciprocal(rstd[:, :], std[:, :]))
                    dve.tensor_scalar(y[par][:, :], y[par][:, :], mean_var[:, 0:1], rstd[:, :],
                                      ALU.subtract, ALU.mult).then_inc(y_done, 1)
                if c_ok:
                    dve.wait_ge(gates_ps_done, t - 1)
                    dve.tensor_tensor(gates[:, :], sm_ps[:, P:P + E], gb2_b, ALU.add).then_inc(gates_done, 1)
                    dve.wait_ge(gates_done, t - 1)
                    chain.hold()
                    chain.link(dve.max(top[:, :], gates[:, :]))
                    chain.hold()
                    chain.link(dve.max_index(top_at[:, :], top[:, :], gates[:, :]))
                    chain.link(dve.tensor_copy(top_at_f[:, :], top_at[:, :]))
                    dve.tensor_tensor(diff[:, bass.ds(t - 2, 1)], top[:, 1:2], top[:, 0:1], ALU.subtract)
                    for k in range(TOPK):
                        last = dve.tensor_scalar(onehot[:, bass.ds(t - 2, 1), k, :].rearrange("p o e -> p (o e)"),
                                                 experts[:, :], top_at_f[:, k:k + 1], None, ALU.is_equal)
                    chain.link(last)
                if b_ok:
                    dve.wait_ge(mm_done, t)
                    dve.tensor_tensor(y[1 - par][:, :], mm_ps[:, :, :].rearrange("p a b -> p (a b)"),
                                      y[1 - par][:, :], ALU.add).then_inc(u_done, 1)
                    h = hid[1 - par]
                    dve.wait_ge(ag_done, t)
                    dve.wait_ge(low_done, t)
                    dve.tensor_tensor(h[:, :], ag_ps[:, ER:AG], gb1_b, ALU.add).then_inc(h_done, 1)
                    dve.wait_ge(h_done, t)
                    moments(dve, chain, h, GH, g_stats, g_mean_var[:, :])
                    dve.sem_inc(g_var_done, 1)
                    dve.wait_ge(g_std_done, t)
                    chain.link(dve.reciprocal(g_rstd[:, :], g_std[:, :]))
                    chain.link(dve.tensor_scalar(h[:, :], h[:, :], g_mean_var[:, 0:1], g_rstd[:, :],
                                                 ALU.subtract, ALU.mult))
                    chain.link(dve.tensor_tensor(h[:, :], h[:, :], gamma_b, ALU.mult))
                    chain.link(dve.tensor_tensor(h[:, :], h[:, :], beta_b, ALU.add))
                    dve.tensor_scalar(h[:, :], h[:, :], 0.0, None, ALU.max).then_inc(hid_done, 1)
                if a_ok:
                    dve.wait_ge(yT_hi_done, t + 1)
                    dve.tensor_tensor(yT_lo[:, :, :].rearrange("p k t -> p (k t)"),
                                      tr_ps[:, :, :].rearrange("p a b -> p (a b)"),
                                      yT_hi[:, :, :].rearrange("p k t -> p (k t)").bitcast(F32),
                                      ALU.subtract).then_inc(yT_lo_done, 1)

            LINKS = 3 + 4 + 6

            dve.wait_ge(pool_const, 3)
            dve.tensor_copy(experts[:, :], experts_i[:, :]).then_inc(small_dve, 1)
            dve.wait_ge(small_pe, 1)
            dve.tensor_copy(gw2T[:, :], sm_ps[0:GH, 0:E]).then_inc(small_dve, 1)
            dve.tensor_copy(rows[:, :], sm_ps[:, P:P + 3 * GH + E]).then_inc(small_dve, 1)
            gw1T = ag_ps[:, 0:KC * GH].rearrange("p (k g) -> p k g", k=KC)
            A_raw = y[0][:, :].rearrange("p (k er) -> p k er", k=KC)
            dve.wait_ge(small_in, 16 * (6 + KC))
            chain.link(dve.tensor_copy(ag_hi[:, :, ER:AG], gw1T))
            chain.link(dve.tensor_copy(ag_hi[:, :, 0:ER], A_raw))
            dve.tensor_tensor(ag_lo[:, :, ER:AG], gw1T, ag_hi[:, :, ER:AG].bitcast(F32), ALU.subtract
                              ).then_inc(small_dve, 1)
            dve.tensor_tensor(ag_lo[:, :, 0:ER], A_raw, ag_hi[:, :, 0:ER].bitcast(F32), ALU.subtract
                              ).then_inc(small_dve, 1)
            dve.wait_ge(small_dve, 5)
            for n in range(KC):
                for half in range(2):
                    cols = slice(half * HALF, (half + 1) * HALF)
                    dve.wait_ge(w_hi_done, 2 * n + half + 1)
                    dve.tensor_tensor(wo_lo[:, n, cols], x_in_sb[n % 2][:, cols], wo_hi[:, n, cols].bitcast(F32),
                                      ALU.subtract).then_inc(w_lo_done, 1)
            split_a(0, 0)
            for n in range(KC):
                for half in range(2):
                    dve.wait_ge(w_hi_done, 2 * (KC + n) + half + 1)
                    out = slice(n * P, (n + 1) * P)
                    dve.tensor_tensor(wm_lo[:, 4 * half:4 * half + 4, out],
                                      tr_ps[:, half, :].rearrange("p (k o) -> p k o", k=4),
                                      wm_hi[:, 4 * half:4 * half + 4, out].bitcast(F32), ALU.subtract
                                      ).then_inc(w_lo_done, 1)
            step(0, 0)
            step(1, 1)
            before = chain.n
            with dve.Fori(0, LOOPS - 1) as i:
                chain.start(before + i * (2 * LINKS))
                step(2 * i + 2, 0)
                step(2 * i + 3, 1)
            assert chain.n == 2 * LINKS, chain.n
            chain.start(before + (LOOPS - 1) * 2 * LINKS)
            step(NT - 2, 0)
            step(NT - 1, 1)
            step(NT, 0)
            step(NT + 1, 1)


def mix_experts(nc, sem, keep, u_d, lora_B, out):
    ER = E * R
    NT = N // P
    HALF = D // 2
    NB = 4
    low, diff, onehot = keep
    u_t = u_d.rearrange("(t p) d -> t p d", p=P)
    out_t = out.rearrange("b (t p) d -> (b t) p d", p=P)

    def at_least(engine, semaphore, value):
        if not isinstance(value, int) or value > 0:
            engine.wait_ge(semaphore, value)

    ctx = ExitStack()
    with ctx:
        sb = lambda name, shape, dt=F32: ctx.enter_context(nc.sbuf_tensor(name, shape, dt))
        ident = sb("p4_ident", [P, P])
        ones = sb("p4_ones", [P, P])
        eps = sb("p4_eps", [P, 1])
        lb = sb("p4_lora_B", [ER, D])
        counts = sb("p4_counts", [P, TOPK * E])
        allowed = sb("p4_allowed", [P, TOPK, E])
        exp_d = sb("p4_exp", [P, NT])
        den = sb("p4_den", [P, NT])
        prob = sb("p4_prob", [P, TOPK, NT])
        weights = sb("p4_weights", [P, NT, E])
        second = sb("p4_second", [P, NT, E])
        u = [sb(f"p4_u{i}", [P, D]) for i in range(2 * NB)]
        lw = [sb(f"p4_lw{i}", [P, ER]) for i in range(NB)]
        lwT = [sb(f"p4_lwT{i}", [ER, P]) for i in range(NB)]
        res = [sb(f"p4_res{i}", [P, D]) for i in range(NB)]
        stats = [sb(f"p4_stats{i}", [P, 2, 6]) for i in range(NB)]
        mean_var = [sb(f"p4_mean_var{i}", [P, 2]) for i in range(NB)]
        std = [sb(f"p4_std{i}", [P, 1]) for i in range(NB)]
        rstd = [sb(f"p4_rstd{i}", [P, 1]) for i in range(NB)]
        shift = [sb(f"p4_shift{i}", [P, 1]) for i in range(NB)]
        tr = [ctx.enter_context(nc.psum_tensor(f"p4_tr{i}", [P, BANK], F32)) for i in range(2)]
        lo = [ctx.enter_context(nc.psum_tensor(f"p4_lo{i}", [P, 2, BANK], F32)) for i in range(3)]

        ident_done, pool_const = sem("p4_ident_done"), sem("p4_pool_const")
        lb_in = sem("p4_lb_in")
        u_in = [sem(f"p4_u_in{i}") for i in range(2 * NB)]
        part_done, counts_ps_done, exp_done = sem("p4_part_done"), sem("p4_counts_ps_done"), sem("p4_exp_done")
        lw_done, tr_done, lwT_done = sem("p4_lw_done"), sem("p4_tr_done"), sem("p4_lwT_done")
        lora_done, z_done = sem("p4_lora_done"), sem("p4_z_done")
        var_done, std_done, shift_done = sem("p4_var_done"), sem("p4_std_done"), sem("p4_shift_done")
        res_done = sem("p4_res_done")
        stored = [sem(f"p4_stored{i}") for i in range(NB)]
        chain_sem, held_sem = sem("p4_chain"), sem("p4_held")

        block = ctx.enter_context(nc.Block())
        BODY = 2 * NB

        def per(t, k, n, times):
            return times * (t // n) if isinstance(t, int) else (t - k) * (times // n) + times * (k // n)

        @block.sync
        def _(sp):
            def load(t, k):
                sp.dma_start(u[k][:, :], u_t[bass.ds(t, 1), :, :].rearrange("o p d -> (o p) d")).then_inc(u_in[k], 16)

            def one(t, k, more=True):
                sp.wait_ge(res_done, t + 1)
                sp.dma_start(out_t[bass.ds(t, 1), :, :].rearrange("o p d -> (o p) d"), res[k % NB][:, :]
                             ).then_inc(stored[k % NB], 16)
                if more:
                    load(t + BODY, k)

            sp.dma_start(lb[:, :], lora_B.rearrange("e r o -> (e r) o")).then_inc(lb_in, 16)
            for k in range(BODY):
                load(k, k)
            with sp.Fori(0, NT // BODY - 1) as i:
                for k in range(BODY):
                    one(BODY * i + k, k)
            for k in range(BODY):
                one(NT - BODY + k, k, more=False)
            for i in range(NB):
                sp.wait_ge(stored[i], 16 * NT // NB)

        @block.gpsimd
        def _(pool):
            make_identity(pool, ident, ident_done)
            pool.memset(ones[:, :], 1.0).then_inc(pool_const, 1)
            pool.memset(eps[:, :], LN_EPS).then_inc(pool_const, 1)

        @block.tensor
        def _(pe):
            pe.wait_ge(ident_done, 2)
            pe.wait_ge(pool_const, 2)
            pe.wait_ge(part_done, 1)
            pe.matmul(tr[1][:, 0:TOPK * E], ones[:, :], counts[:, :], start=True, stop=True
                      ).then_inc(counts_ps_done, 1)
            pe.wait_ge(lb_in, 16)

            def turn(t, k):
                pe.wait_ge(lw_done, t + 1)
                at_least(pe, lwT_done, t - 1)
                pe.transpose(tr[k % 2][:, 0:P], lw[k % NB][:, :], ident[:, :]).then_inc(tr_done, 1)

            def products(t, k):
                pe.wait_ge(lwT_done, t + 1)
                at_least(pe, z_done, t - 1)
                for half in range(2):
                    last = pe.matmul(lo[k % 2][:, half, :], lwT[k % NB][:, :],
                                     lb[:, half * HALF:(half + 1) * HALF], start=True, stop=True)
                last.then_inc(lora_done, 1)

            turn(0, 0)
            for k in range(BODY):
                turn(k + 1, (k + 1) % BODY)
                products(k, k)
            with pe.Fori(0, NT // BODY - 2) as i:
                for k in range(BODY):
                    turn(BODY * i + BODY + k + 1, (k + 1) % BODY)
                    products(BODY * i + BODY + k, k)
            for k in range(BODY):
                if k + 1 < BODY:
                    turn(NT - BODY + k + 1, k + 1)
                products(NT - BODY + k, k)

        @block.scalar
        def _(act):
            act.wait_ge(pool_const, 2)
            act.activation(exp_d[:, :], diff[:, :], ACT.Exp).then_inc(exp_done, 1)

            def copy_T(t, k):
                act.wait_ge(tr_done, t + 1)
                at_least(act, lora_done, t - NB + 1)
                act.activation(lwT[k % NB][:, :], tr[k % 2][:, 0:P], ACT.Copy).then_inc(lwT_done, 1)

            def norm(t, k):
                b = k % NB
                act.wait_ge(var_done, t + 1)
                act.activation(std[b][:, :], mean_var[b][:, 1:2], ACT.Sqrt, bias=eps[:, :]).then_inc(std_done, 1)
                act.wait_ge(shift_done, t + 1)
                if not isinstance(t, int) or t >= NB:
                    act.wait_ge(stored[b], per(t, k, NB, 16))
                act.activation(res[b][:, :], u[k][:, :], ACT.Identity, bias=shift[b][:, :], scale=rstd[b][:, :]
                               ).then_inc(res_done, 1)

            copy_T(0, 0)
            for k in range(BODY):
                copy_T(k + 1, (k + 1) % BODY)
                norm(k, k)
            with act.Fori(0, NT // BODY - 2) as i:
                for k in range(BODY):
                    copy_T(BODY * i + BODY + k + 1, (k + 1) % BODY)
                    norm(BODY * i + BODY + k, k)
            for k in range(BODY):
                if k + 1 < BODY:
                    copy_T(NT - BODY + k + 1, k + 1)
                norm(NT - BODY + k, k)

        @block.vector
        def _(dve):
            chain = Chain(dve, chain_sem, held_sem)
            flat = onehot[:, :, :, :].rearrange("p t k e -> p (t k e)").rearrange("p (t s) -> p s t", t=NT)
            dve.reduce_sum(counts[:, :], flat, AX.X).then_inc(part_done, 1)
            dve.wait_ge(exp_done, 1)
            chain.link(dve.tensor_scalar(den[:, :], exp_d[:, :], 1.0, None, ALU.add))
            chain.link(dve.reciprocal(prob[:, 0, :], den[:, :]))
            chain.link(dve.tensor_tensor(prob[:, 1, :], exp_d[:, :], prob[:, 0, :], ALU.mult))
            dve.wait_ge(counts_ps_done, 1)
            chain.link(dve.tensor_scalar(allowed[:, :, :].rearrange("p k e -> p (k e)"), tr[1][:, 0:TOPK * E],
                                         float(CAPACITY), 1.0 / R, ALU.is_le, ALU.mult))
            for k, w in ((0, weights), (1, second)):
                chain.link(dve.tensor_tensor(w[:, :, :], onehot[:, :, k, :],
                                             prob[:, k, :].unsqueeze(2).to_broadcast([P, NT, E]), ALU.mult))
                chain.link(dve.tensor_tensor(w[:, :, :], w[:, :, :],
                                             allowed[:, k, :].unsqueeze(1).to_broadcast([P, NT, E]), ALU.mult))
            chain.link(dve.tensor_tensor(weights[:, :, :], weights[:, :, :], second[:, :, :], ALU.add))

            def weigh(t, k):
                at_least(dve, tr_done, t - NB + 1)
                dve.tensor_tensor(lw[k % NB][:, :].rearrange("p (e r) -> p e r", e=E),
                                  low[:, bass.ds(t, 1), :].rearrange("p o (e r) -> p (o e) r", e=E),
                                  weights[:, bass.ds(t, 1), :].rearrange("p o e -> p (o e)").unsqueeze(2)
                                  .to_broadcast([P, E, R]), ALU.mult).then_inc(lw_done, 1)

            def tile(t, k):
                b = k % NB
                dve.wait_ge(u_in[k], per(t, k, BODY, 16) + 16)
                dve.wait_ge(lora_done, t + 1)
                dve.tensor_tensor(u[k][:, :], lo[k % 2][:, :, :].rearrange("p a b -> p (a b)"), u[k][:, :],
                                  ALU.add).then_inc(z_done, 1)
                dve.wait_ge(z_done, t + 1)
                moments(dve, chain, u[k], D, stats[b], mean_var[b][:, :])
                dve.sem_inc(var_done, 1)
                dve.wait_ge(std_done, t + 1)
                at_least(dve, res_done, t - NB + 1)
                chain.link(dve.reciprocal(rstd[b][:, :], std[b][:, :]))
                dve.scalar_tensor_tensor(out=shift[b][:, :], in0=mean_var[b][:, 0:1], scalar=-1.0,
                                         in1=rstd[b][:, :], op0=ALU.mult, op1=ALU.mult).then_inc(shift_done, 1)

            LINKS = 3
            for k in range(2):
                weigh(k, k)
            for k in range(BODY):
                weigh(k + 2, (k + 2) % BODY)
                tile(k, k)
            before = chain.n
            with dve.Fori(0, NT // BODY - 2) as i:
                chain.start(before + i * (BODY * LINKS))
                for k in range(BODY):
                    weigh(BODY * i + BODY + k + 2, (k + 2) % BODY)
                    tile(BODY * i + BODY + k, k)
            assert chain.n == BODY * LINKS
            chain.start(before + (NT // BODY - 2) * BODY * LINKS)
            for k in range(BODY):
                if k + 2 < BODY:
                    weigh(NT - BODY + k + 2, k + 2)
                tile(NT - BODY + k, k)


def build(nc, x, wq, wk, wv, wo, weight, lora_A, lora_B, gw1, gb1, gamma, beta, gw2, gb2, out):
    dram = lambda name, shape: nc.dram_tensor(name, shape, F32, kind="Internal").ap()
    q_hi, q_lo = dram("q_hi", [D, N]), dram("q_lo", [D, N])
    k_hi, k_lo = dram("k_hi", [NKV * HD, N]), dram("k_lo", [NKV * HD, N])
    v_d = dram("v", [NKV, P, N // P, HD])
    aT_d = dram("attended_T", [D, N])
    u_d = dram("u", [N, D])
    with ExitStack() as ctx:
        sem = lambda name: ctx.enter_context(nc.semaphore(name))
        project_qkv(nc, sem, x, wq, wk, wv, q_hi, q_lo, k_hi, k_lo, v_d)
        attend(nc, sem, q_hi, q_lo, k_hi, k_lo, v_d, aT_d)
        keep = (ctx.enter_context(nc.sbuf_tensor("low", [P, N // P, E * R], F32)),
                ctx.enter_context(nc.sbuf_tensor("diff", [P, N // P], F32)),
                ctx.enter_context(nc.sbuf_tensor("onehot", [P, N // P, TOPK, E], F32)))
        project_and_gate(nc, sem, keep, x, aT_d, wo, weight, lora_A, gw1, gb1, gamma, beta, gw2, gb2, u_d)
        mix_experts(nc, sem, keep, u_d, lora_B, out)


_INS = ["L0_attn_x", "L0_attn_wq", "L0_attn_wk", "L0_attn_wv", "L0_attn_wo", "L0_ffn_weight", "L0_ffn_lora_A",
        "L0_ffn_lora_B", "L0_ffn_gw1", "L0_ffn_gb1", "L0_ffn_ln_gamma", "L0_ffn_ln_beta", "L0_ffn_gw2", "L0_ffn_gb2"]
_OUT = ((B, S, D), "float32")


def kernel(**inputs):
    import numpy as _np
    import concourse.bacc as _bacc
    from concourse.bass_utils import run_bass_kernel_spmd as _run

    nc = _bacc.Bacc("TRN2", target_bir_lowering=False, num_devices=1)
    arrays, args = {}, []
    for name in _INS:
        a = _np.ascontiguousarray(inputs[name])
        arrays[f"in_{name}"] = a
        args.append(nc.dram_tensor(f"in_{name}", a.shape, mybir.dt.from_np(a.dtype), kind="ExternalInput").ap())
    args.append(nc.dram_tensor("out", _OUT[0], mybir.dt.from_np(_np.dtype(_OUT[1])), kind="ExternalOutput").ap())
    build(nc, *args)
    return _run(nc, [arrays], core_ids=[0]).results[0]["out"]
```

```python
import concourse.bass as bass
from concourse import mybir
from contextlib import ExitStack
import numpy as np

F32 = mybir.dt.float32
F32R = mybir.dt.float32r
BF16 = mybir.dt.bfloat16
I32 = mybir.dt.int32
U32 = mybir.dt.uint32
ALU = mybir.AluOpType
ACT = mybir.ActivationFunctionType
AX = mybir.AxisListType

P = 128
BANK = 512
B, S, D = 2, 2048, 1024
N = B * S
NH, NKV, HD = 32, 8, 32
REP = NH // NKV
KC = D // P
SCALE = HD ** -0.5
NEG = -1e30
E, R, TOPK = 8, 16, 2
GH = 4 * E
CAPACITY = int(3.0 * N / E)
LN_EPS = 1e-5


def make_identity(pool, ident, sem):
    pool.memset(ident[:, :], 0.0).then_inc(sem, 1)
    pool.wait_ge(sem, 1)
    pool.affine_select(out=ident[:, :], in_=ident[:, :], compare_op=ALU.not_equal, fill=1.0,
                       base=0, pattern=[[-1, P]], channel_multiplier=1).then_inc(sem, 1)


def matmul3(pe, out, lhs_hi, lhs_lo, rhs_hi, rhs_lo, first, last):
    pe.matmul(out, lhs_hi, rhs_hi, start=first, stop=False)
    pe.matmul(out, lhs_hi, rhs_lo, start=False, stop=False)
    return pe.matmul(out, lhs_lo, rhs_hi, start=False, stop=last)


def project_qkv(nc, sem, x, wq, wk, wv, q_hi, q_lo, k_hi, k_lo, v_d):
    TT = 512
    NT = N // TT
    SUB = TT // P
    KV = NKV * HD
    WC = D + 2 * KV
    QG, KG, VG = D // P, KV // P, SUB
    G = QG + KG + VG
    GB = 4
    TB = 4
    T_AT = 4
    assert GB + TB == 8 and G % 2 == 0
    x_t = x.rearrange("b (t s p) d -> (b t) p s d", s=SUB, p=P)

    ctx = ExitStack()
    with ctx:
        sb = lambda name, shape, dt: ctx.enter_context(nc.sbuf_tensor(name, shape, dt))
        ident = sb("p1_ident", [P, P], F32)
        w_hi = sb("p1_w_hi", [P, KC, WC], F32R)
        w_lo = sb("p1_w_lo", [P, KC, WC], F32R)
        w_raw = sb("p1_w_raw", [P, 2, WC], F32)
        x_raw = sb("p1_x_raw", [P, SUB, D], F32)
        xT_hi = [sb(f"p1_xT_hi{i}", [P, KC, TT], F32R) for i in range(2)]
        xT_lo = [sb(f"p1_xT_lo{i}", [P, KC, TT], F32R) for i in range(2)]
        out_hi = sb("p1_out_hi", [P, 2, TT], F32R)
        out_lo = sb("p1_out_lo", [P, 2, TT], F32R)
        v_out = sb("p1_v_out", [P, 2, KV], F32)
        tp = [ctx.enter_context(nc.psum_tensor(f"p1_tp{i}", [P, BANK], F32)) for i in range(TB)]
        acc = [ctx.enter_context(nc.psum_tensor(f"p1_acc{i}", [P, BANK], F32)) for i in range(GB)]

        ident_done = sem("p1_ident_done")
        w_in = [sem(f"p1_w_in{i}") for i in range(2)]
        w_hi_done = sem("p1_w_hi_done")
        w_lo_done = sem("p1_w_lo_done")
        x_in = sem("p1_x_in")
        transposed = sem("p1_transposed")
        xT_hi_done = sem("p1_xT_hi_done")
        xT_lo_done = sem("p1_xT_lo_done")
        group_done = sem("p1_group_done")
        out_hi_done = sem("p1_out_hi_done")
        evacuated = sem("p1_evacuated")
        stored = [sem(f"p1_stored{i}") for i in range(2)]

        HALF = (QG + KG) // 2 * 32 + VG // 2 * 16

        def stored_before(t, g):
            n = g // 2
            return t * HALF + min(n, (QG + KG) // 2) * 32 + max(0, n - (QG + KG) // 2) * 16

        block = ctx.enter_context(nc.Block())

        @block.gpsimd
        def _(pool):
            make_identity(pool, ident, ident_done)

        @block.sync
        def _(sp):
            def load_x(t):
                sp.dma_start(x_raw[:, :, :], x_t[t, :, :, :]).then_inc(x_in, 16)

            def load_w(k):
                if k >= 2:
                    sp.wait_ge(w_lo_done, k - 1)
                rows = slice(k * P, (k + 1) * P)
                sp.dma_start(w_raw[:, k % 2, 0:D], wq[rows, :]).then_inc(w_in[k % 2], 16)
                sp.dma_start(w_raw[:, k % 2, D:D + KV], wk[rows, :]).then_inc(w_in[k % 2], 16)
                sp.dma_start(w_raw[:, k % 2, D + KV:WC], wv[rows, :]).then_inc(w_in[k % 2], 16)

            def tile(t, first=False, last=False):
                for g in range(G):
                    sp.wait_ge(evacuated, t * G + g + 1)
                    cols = bass.ds(t * TT, TT)
                    if g < QG + KG:
                        hi, lo, r = (q_hi, q_lo, g) if g < QG else (k_hi, k_lo, g - QG)
                        rows = slice(r * P, (r + 1) * P)
                        sp.dma_start(hi[rows, cols], out_hi[:, g % 2, :].bitcast(F32)).then_inc(stored[g % 2], 16)
                        sp.dma_start(lo[rows, cols], out_lo[:, g % 2, :].bitcast(F32)).then_inc(stored[g % 2], 16)
                    else:
                        s = g - QG - KG
                        sp.dma_start(v_d[:, :, bass.ds(t * SUB + s, 1), :].rearrange("g p t d -> p g (t d)"),
                                     v_out[:, g % 2, :].rearrange("p (g d) -> p g d", d=HD)
                                     ).then_inc(stored[g % 2], 16)
                    if g == T_AT + KC - 1 and not last and load_next[0]:
                        sp.wait_ge(transposed, (t + 2) * KC)
                        load_x(t + 2)

            load_next = [True]
            load_w(0)
            load_x(0)
            for k in range(1, KC):
                load_w(k)
            sp.wait_ge(transposed, KC)
            load_x(1)
            tile(0, first=True)
            with sp.Fori(0, NT // 2 - 2) as i:
                tile(2 * i + 1)
                tile(2 * i + 2)
            tile(NT - 3)
            load_next[0] = False
            tile(NT - 2)
            tile(NT - 1, last=True)
            for i in range(2):
                sp.wait_ge(stored[i], NT * HALF)

        @block.tensor
        def _(pe):
            def transpose_chunk(t, k):
                if k == 0:
                    pe.wait_ge(x_in, 16 * t + 16)
                if not (isinstance(t, int) and t * KC + k < TB):
                    pe.wait_ge(xT_lo_done, t * KC + k + 1 - TB)
                for s in range(SUB):
                    last = pe.transpose(tp[k % TB][:, s * P:(s + 1) * P], x_raw[:, s, k * P:(k + 1) * P],
                                        ident[:, :])
                last.then_inc(transposed, 1)

            def tile(t, par, last=False):
                xh, xl = xT_hi[par], xT_lo[par]
                pe.wait_ge(xT_lo_done, (t + 1) * KC)
                for g in range(G):
                    bank = acc[(par * G + g) % GB]
                    if not (isinstance(t, int) and t * G + g < GB):
                        pe.wait_ge(evacuated, t * G + g + 1 - GB)
                    for k in range(KC):
                        if g < QG + KG:
                            cols = slice(g * P, (g + 1) * P)
                            done = matmul3(pe, bank[:, :], w_hi[:, k, cols], w_lo[:, k, cols],
                                           xh[:, k, :], xl[:, k, :], k == 0, k == KC - 1)
                        else:
                            rows = slice((g - QG - KG) * P, (g - QG - KG + 1) * P)
                            done = matmul3(pe, bank[:, 0:KV], xh[:, k, rows], xl[:, k, rows],
                                           w_hi[:, k, D + KV:WC], w_lo[:, k, D + KV:WC], k == 0, k == KC - 1)
                    done.then_inc(group_done, 1)
                    if T_AT <= g < T_AT + KC and not last:
                        transpose_chunk(t + 1, g - T_AT)

            pe.wait_ge(ident_done, 2)
            for k in range(KC):
                transpose_chunk(0, k)
            pe.wait_ge(w_lo_done, KC)
            tile(0, 0)
            with pe.Fori(0, NT // 2 - 1) as i:
                tile(2 * i + 1, 1)
                tile(2 * i + 2, 0)
            tile(NT - 1, 1, last=True)

        @block.scalar
        def _(act):
            def split_x(t, par, k):
                act.wait_ge(transposed, t * KC + k + 1)
                act.activation(xT_hi[par][:, k, :], tp[k % TB][:, :], ACT.Copy).then_inc(xT_hi_done, 1)

            def tile(t, par, last=False):
                for g in range(G):
                    if g < QG + KG:
                        act.wait_ge(stored[g % 2], stored_before(t, g))
                        act.wait_ge(group_done, t * G + g + 1)
                        act.activation(out_hi[:, g % 2, :], acc[(par * G + g) % GB][:, :],
                                       ACT.Copy).then_inc(out_hi_done, 1)
                    if T_AT <= g < T_AT + KC and not last:
                        split_x(t + 1, 1 - par, g - T_AT)

            for k in range(KC):
                act.wait_ge(w_in[k % 2], 48 * (k // 2 + 1))
                act.activation(w_hi[:, k, :], w_raw[:, k % 2, :], ACT.Copy).then_inc(w_hi_done, 1)
                split_x(0, 0, k)
            tile(0, 0)
            with act.Fori(0, NT // 2 - 1) as i:
                tile(2 * i + 1, 1)
                tile(2 * i + 2, 0)
            tile(NT - 1, 1, last=True)

        @block.vector
        def _(dve):
            def split_x(t, par, k):
                dve.wait_ge(xT_hi_done, t * KC + k + 1)
                dve.tensor_tensor(xT_lo[par][:, k, :], tp[k % TB][:, :], xT_hi[par][:, k, :].bitcast(F32),
                                  ALU.subtract).then_inc(xT_lo_done, 1)

            def tile(t, par, last=False):
                for g in range(G):
                    bank = acc[(par * G + g) % GB]
                    if g < QG + KG:
                        dve.wait_ge(out_hi_done, t * (QG + KG) + g + 1)
                        dve.tensor_tensor(out_lo[:, g % 2, :], bank[:, :], out_hi[:, g % 2, :].bitcast(F32),
                                          ALU.subtract).then_inc(evacuated, 1)
                    else:
                        dve.wait_ge(stored[g % 2], stored_before(t, g))
                        dve.wait_ge(group_done, t * G + g + 1)
                        dve.tensor_copy(v_out[:, g % 2, :], bank[:, 0:KV]).then_inc(evacuated, 1)
                    if T_AT <= g < T_AT + KC and not last:
                        split_x(t + 1, 1 - par, g - T_AT)

            for k in range(KC):
                dve.wait_ge(w_hi_done, k + 1)
                dve.tensor_tensor(w_lo[:, k, :], w_raw[:, k % 2, :], w_hi[:, k, :].bitcast(F32),
                                  ALU.subtract).then_inc(w_lo_done, 1)
                split_x(0, 0, k)
            tile(0, 0)
            with dve.Fori(0, NT // 2 - 1) as i:
                tile(2 * i + 1, 1)
                tile(2 * i + 2, 0)
            tile(NT - 1, 1, last=True)


def attend(nc, sem, q_hi, q_lo, k_hi, k_lo, v_d, aT_d, den_d):
    NG = B * NKV
    CH = 512
    NC = S // CH
    SUB = CH // P
    NT = S // P
    ROWS = 3 * HD
    STEPS = [(c, t) for c in range(NC) for t in range(SUB * (c + 1))]
    NS = len(STEPS)
    FIRST_STEP = [STEPS.index((c, 0)) for c in range(NC)] + [NS]
    PB = 8
    assert NS % PB == 0
    FIN = 2

    def offset(c, t):
        return max(0, t - SUB * c) * P

    TLAG = 4
    units = [[("score", c, h, i, j) for h in range(REP) for i in range(SUB) for j in range(c + 1)]
             for c in range(NC)]
    ITEMS = []
    for c in range(NC):
        ITEMS += units[c][:TLAG] + ([("maxrow", c - 1)] if c else []) + units[c][TLAG:]
    ITEMS.append(("maxrow", NC - 1))
    NI = len(ITEMS)

    def item_width(i):
        if ITEMS[i][0] == "maxrow":
            return CH
        _, c, h, sub, j = ITEMS[i]
        return min(BANK, (SUB * c + sub + 1) * P - j * BANK)

    PARTS = []
    for s in range(NS):
        o, before = offset(*STEPS[s]), STEPS[s - 1]
        PARTS += [(s, "scores 0", 2 * (CH - o)), (s, "scores 1", 2 * (CH - o)), (s, "values", 4 * (CH - offset(*before)))]
        if before[1] == FIN:
            PARTS.append((s, "finish", 4 * CH))
    ADD_STEPS = [s for s, (c, t) in enumerate(STEPS) if t > 0 or c == 0]
    NADD = len(ADD_STEPS)

    def adds_through(s):
        return sum(x <= s for x in ADD_STEPS) if s >= 0 else sum(x <= s + NS for x in ADD_STEPS) - NADD

    OVERHEAD = 60
    part_ends = np.cumsum([cost for _, _, cost in PARTS]) / sum(cost for _, _, cost in PARTS[:-2])
    add_costs = np.cumsum([CH - offset(*STEPS[s]) + OVERHEAD if part == "scores 0" and s in ADD_STEPS else 0
                           for s, part, _ in PARTS])
    item_starts = np.cumsum([0] + [item_width(i) + OVERHEAD for i in range(NI)])
    dve_total = add_costs[-1] + item_starts[-1]
    ITEMS_BY = [min(NI - 1, int(np.searchsorted(item_starts, end * dve_total - added, "left")))
                for end, added in zip(part_ends, add_costs)]
    ITEMS_BY[-1] = NI
    ITEMS_BY = [max(ITEMS_BY[:k + 1]) for k in range(len(ITEMS_BY))]
    STEP_OF_ITEM = [PARTS[next(k for k, by in enumerate(ITEMS_BY) if by > i)][0] for i in range(NI)]
    QM = 3
    bank_of = lambda i: i % QM
    bank_user = lambda i: i - QM if i >= QM else max(x for x in range(NI) if x % QM == i) - NI

    def at_least(engine, semaphore, value):
        if not isinstance(value, int) or value > 0:
            engine.wait_ge(semaphore, value)

    ctx = ExitStack()
    with ctx:
        sb = lambda name, shape, dt: ctx.enter_context(nc.sbuf_tensor(name, shape, dt))
        ps = lambda name, shape: ctx.enter_context(nc.psum_tensor(name, shape, F32))
        ident = sb("p2_ident", [P, P], F32)
        ident_bf = sb("p2_ident_bf", [P, P], BF16)
        mask_q = sb("p2_mask_q", [P, P], BF16)
        mask_k = sb("p2_mask_k", [P, P], BF16)
        ones = sb("p2_ones", [P, HD], F32)
        zeros = sb("p2_zeros", [P, REP, P], F32)
        q_st = [sb(f"p2_q_st{i}", [P, REP, S], F32R) for i in range(2)]
        k_st = [sb(f"p2_k_st{i}", [P, S], F32R) for i in range(2)]
        v = [sb(f"p2_v{i}", [P, NT, HD], F32) for i in range(2)]
        probs = [sb(f"p2_probs{i}", [P, REP, CH], F32) for i in range(PB)]
        psums = [sb(f"p2_psums{i}", [P, REP, CH], F32) for i in range(2)]
        part_max = [sb(f"p2_part_max{c}", [P, REP * SUB, c + 1], F32) for c in range(NC)]
        row_max = [sb(f"p2_row_max{c}", [P, REP * SUB], F32) for c in range(NC)]
        neg_max = [sb(f"p2_neg_max{c}", [REP, CH], F32R) for c in range(NC)]
        o_raw = [sb(f"p2_o_raw{i}", [P, CH], F32) for i in range(2)]
        d_raw = [sb(f"p2_d_raw{i}", [P, CH], F32) for i in range(2)]
        qm = [ps(f"p2_qm{i}", [P, BANK]) for i in range(QM)]
        km = [ps(f"p2_km{i}", [P, 2, BANK]) for i in range(2)]
        o_ps = ps("p2_o", [P, BANK])

        ident_done = sem("p2_ident_done")
        consts_done = sem("p2_consts_done")
        q_in = [[sem(f"p2_q_in{i}_{c}") for c in range(NC)] for i in range(2)]
        k_in = [[sem(f"p2_k_in{i}_{c}") for c in range(NC)] for i in range(2)]
        v_in = [sem(f"p2_v_in{i}") for i in range(2)]
        m_in = [[sem(f"p2_m_in{i}_{c}") for c in range(NC)] for i in range(2)]
        item_done = sem("p2_item_done")
        item_read = sem("p2_item_read")
        max_done = sem("p2_max_done")
        scored = sem("p2_scored")
        exp_done = sem("p2_exp_done")
        pv_done = sem("p2_pv_done")
        added = sem("p2_added")
        added_0 = sem("p2_added_0")
        o_read = sem("p2_o_read")
        sums_done = sem("p2_sums_done")
        d_read = sem("p2_d_read")
        o_stored = [sem(f"p2_o_stored{i}") for i in range(2)]
        d_stored = [sem(f"p2_d_stored{i}") for i in range(2)]
        held = sem("p2_held")

        block = ctx.enter_context(nc.Block())


        @block.sync
        def _(sp):
            def batch_head(n):
                b, g = (n >> (NKV.bit_length() - 1)) & (B - 1), n & (NKV - 1)
                return b, g

            def hold():
                sp.sem_inc(held, 1)

            def load_q(b, g, par, c):
                rows, cols = bass.ds(g * P, P), bass.ds(b * S + c * CH, CH)
                for at, src in ((0, q_hi), (HD, q_lo), (2 * HD, q_hi)):
                    sp.dma_start(q_st[par][at:at + HD, :, c * CH:(c + 1) * CH].bitcast(F32),
                                 src[rows, cols].rearrange("(h d) t -> d h t", d=HD)).then_inc(q_in[par][c], 16)

            def load_k(b, g, par, c):
                rows, cols = bass.ds(g * HD, HD), bass.ds(b * S + c * CH, CH)
                for at, src in ((0, k_hi), (HD, k_hi), (2 * HD, k_lo)):
                    sp.dma_start(k_st[par][at:at + HD, c * CH:(c + 1) * CH].bitcast(F32), src[rows, cols]
                                 ).then_inc(k_in[par][c], 16)

            def load_v(b, g, par):
                sp.dma_start(v[par][:, :, :],
                             v_d[bass.ds(g, 1), :, bass.ds(b * NT, NT), :].rearrange("g p t d -> (g p) t d")
                             ).then_inc(v_in[par], 16)

            def send_max(done, par, c):
                sp.wait_ge(item_read, done)
                sp.dma_start(q_st[par][ROWS:ROWS + 1, :, c * CH:(c + 1) * CH].bitcast(F32),
                             neg_max[c][:, :].bitcast(F32)).then_inc(m_in[par][c], 16)

            def store_o(n, b, g, c):
                sp.wait_ge(o_read, n * NC + c + 1)
                hold()
                sp.dma_start(aT_d[bass.ds(g * P, P), bass.ds(b * S + c * CH, CH)],
                             o_raw[c % 2][:, :]).then_inc(o_stored[c % 2], 16)

            def store_d(n, b, g, c):
                sp.wait_ge(d_read, n * NC + c + 1)
                hold()
                sp.dma_start(den_d[bass.ds(g * REP, REP), bass.ds(b * S + c * CH, CH)],
                             d_raw[c % 2][0:P:HD, :]).then_inc(d_stored[c % 2], 16)

            def group(n, par, last=False, load=True):
                b, g = batch_head(n)
                b1, g1 = batch_head(n + 1)
                b2, g2 = batch_head(n + 2)
                before = batch_head(n - 1)
                events = []
                for c in range(NC):
                    end = FIRST_STEP[c + 1]
                    if load:
                        events.append((end + 0.5, "load q", c))
                        events.append((FIRST_STEP[NC - 1] + SUB * (c + 1) + 0.5, "load k", c))
                    if c < NC - 1:
                        events.append((end + 1.5, "store o", c))
                        events.append((end + FIN + 2.5, "store d", c))
                    if not last:
                        events.append((STEP_OF_ITEM[ITEMS.index(("maxrow", c))] + 1, "max", c))
                if not (isinstance(n, int) and n == 0):
                    events.append((1.5, "store o before", NC - 1))
                    events.append((FIN + 2.5, "store d before", NC - 1))
                    if not last:
                        events.append((1.4, "load v", 0))
                for _, what, c in sorted(events):
                    if what == "load q":
                        sp.wait_ge(scored, 2 * (n * NS + FIRST_STEP[c + 1]))
                        hold()
                        load_q(b2, g2, par, c)
                    elif what == "load k":
                        sp.wait_ge(scored, 2 * (n * NS + FIRST_STEP[NC - 1] + SUB * (c + 1)))
                        hold()
                        load_k(b2, g2, par, c)
                    elif what == "load v":
                        sp.wait_ge(pv_done, n * NS)
                        hold()
                        load_v(b1, g1, 1 - par)
                    elif what == "store o":
                        store_o(n, b, g, c)
                    elif what == "store d":
                        store_d(n, b, g, c)
                    elif what == "store o before":
                        store_o(n - 1, *before, c)
                    elif what == "store d before":
                        store_d(n - 1, *before, c)
                    else:
                        send_max((n + 1) * NI + ITEMS.index(("maxrow", c)) + 1, 1 - par, c)

            for g in range(2):
                for c in range(NC):
                    load_k(0, g, g, c)
                    load_q(0, g, g, c)
                load_v(0, g, g)
            for c in range(NC):
                send_max(ITEMS.index(("maxrow", c)) + 1, 0, c)
            group(0, 0)
            with sp.Fori(0, NG // 2 - 2) as i:
                group(2 * i + 1, 1)
                group(2 * i + 2, 0)
            group(NG - 3, 1)
            group(NG - 2, 0, load=False)
            group(NG - 1, 1, last=True, load=False)
            store_o(NG - 1, B - 1, NKV - 1, NC - 1)
            store_d(NG - 1, B - 1, NKV - 1, NC - 1)
            for i in range(2):
                sp.wait_ge(o_stored[i], 16 * NG * NC // 2)
                sp.wait_ge(d_stored[i], 16 * NG * NC // 2)

        def add(engine, heads, n, s, halves, done):
            c, t = STEPS[s]
            o = offset(c, t)
            sums, new, old = (x[:, heads] for x in (psums[c % 2], probs[s % PB], probs[(s - 1) % PB]))
            if t == (c > 0):
                at_least(engine, sums_done, n * NC + c - 1)
            engine.wait_ge(exp_done, 2 * (n * NS + s) + halves)
            if t == 0:
                engine.tensor_tensor(sums[:, :, 0:P], new[:, :, 0:P], zeros[:, heads, :], ALU.add).then_inc(done, 1)
            elif t == 1:
                engine.tensor_tensor(sums[:, :, o:CH], old[:, :, o:CH], new[:, :, o:CH], ALU.add).then_inc(done, 1)
            else:
                engine.wait_ge(done, n * NADD + adds_through(s) - 1)
                engine.tensor_tensor(sums[:, :, o:CH], sums[:, :, o:CH], new[:, :, o:CH], ALU.add).then_inc(done, 1)

        @block.gpsimd
        def _(pool):
            make_identity(pool, ident, ident_done)
            pool.memset(ones[:, :], 1.0).then_inc(consts_done, 1)
            pool.memset(zeros[:, :, :], 0.0).then_inc(ident_done, 1)
            pool.memset(mask_q[:, :], 0.0).then_inc(ident_done, 1)
            pool.memset(mask_k[:, :], 0.0).then_inc(ident_done, 1)
            pool.wait_ge(ident_done, 5)
            pool.tensor_copy(ident_bf[:, :], ident[:, :]).then_inc(consts_done, 1)
            pool.affine_select(out=mask_q[:, :], in_=mask_q[:, :], compare_op=ALU.is_ge, fill=NEG,
                               base=0, pattern=[[-1, P]], channel_multiplier=1).then_inc(consts_done, 1)
            pool.affine_select(out=mask_k[:, :], in_=mask_k[:, :], compare_op=ALU.is_ge, fill=NEG,
                               base=0, pattern=[[1, P]], channel_multiplier=-1).then_inc(consts_done, 1)

            def group(n):
                for s in ADD_STEPS:
                    add(pool, slice(1, REP), n, s, 2, added)

            group(0)
            with pool.Fori(0, NG // 2 - 1) as i:
                group(2 * i + 1)
                group(2 * i + 2)
            group(NG - 1)

        @block.tensor
        def _(pe):
            def item(m, par, i):
                at_least(pe, item_read, m * NI + bank_user(i) + 1)
                bank = qm[bank_of(i)]
                if ITEMS[i][0] == "maxrow":
                    c = ITEMS[i][1]
                    pe.wait_ge(max_done, m * NC + c + 1)
                    for sub in range(SUB):
                        last = pe.transpose(bank[0:REP, sub * P:(sub + 1) * P],
                                            row_max[c][:, sub * REP:(sub + 1) * REP], ident[:, :])
                    last.then_inc(item_done, 1)
                    return
                _, c, h, sub, j = ITEMS[i]
                if (h, sub, j) == (0, 0, 0):
                    pe.wait_ge(q_in[par][c], 48 * (m // 2 + 1) if isinstance(m, int) else q_loads(m, par))
                    pe.wait_ge(k_in[par][c], 48 * (m // 2 + 1) if isinstance(m, int) else q_loads(m, par))
                q0 = c * CH + sub * P
                w = item_width(i)
                last = pe.matmul(bank[:, 0:w], q_st[par][0:ROWS, h, q0:q0 + P],
                                 k_st[par][0:ROWS, j * BANK:j * BANK + w], start=True, stop=j < c)
                if j == c:
                    last = pe.matmul(bank[:, w - P:w], ident_bf[:, :], mask_q[:, :], start=False, stop=True)
                last.then_inc(item_done, 1)

            def q_loads(m, par):
                return 24 * (m - par) + 48

            def scores(n, par, s, half):
                c, t = STEPS[s]
                o = offset(c, t)
                at_least(pe, exp_done, 2 * (n * NS + s) + half - 1)
                if half == 0 and STEPS[s - 1][1] == FIN + 1 and s > 0:
                    at_least(pe, d_read, n * NC + STEPS[s - 1][0])
                if half == 0 and t == 0:
                    pe.wait_ge(m_in[par][c], q_loads(n, par) // 3)
                diag = t >= SUB * c
                for x in range(2):
                    h = 2 * half + x
                    last = pe.matmul(km[half][:, x, o:CH], k_st[par][0:ROWS + 1, t * P:(t + 1) * P],
                                     q_st[par][0:ROWS + 1, h, c * CH + o:(c + 1) * CH], start=True, stop=not diag)
                    if diag:
                        last = pe.matmul(km[half][:, x, o:o + P], ident_bf[:, :], mask_k[:, :],
                                         start=False, stop=True)
                last.then_inc(scored, 1)

            def heads_matmul(out, lhs, rhs, o, start, stop):
                for h in range(REP):
                    last = pe.matmul(out[h * HD:(h + 1) * HD, o:CH], lhs, rhs[:, h, o:CH], start=start, stop=stop)
                return last

            def values(n, par, s):
                c, t = STEPS[s]
                if s == 0:
                    pe.wait_ge(v_in[par], q_loads(n, par) // 3)
                pe.wait_ge(exp_done, 2 * (n * NS + s + 1))
                if t == 0:
                    at_least(pe, o_read, n * NC + c)
                heads_matmul(o_ps, v[par][:, t, :], probs[s % PB], offset(c, t), t == 0,
                             t == SUB * (c + 1) - 1).then_inc(pv_done, 1)

            def finish(n, c, scores_before):
                pe.wait_ge(added, n * NADD + adds_through(FIRST_STEP[c + 1] - 1))
                pe.wait_ge(added_0, n * NADD + adds_through(FIRST_STEP[c + 1] - 1))
                pe.wait_ge(exp_done, scores_before)
                heads_matmul(km[0][:, 0, :], ones[:, :], psums[c % 2], 0, True, True).then_inc(sums_done, 1)

            def group(n, par, last=False):
                done = 0
                for k, (s, part, _) in enumerate(PARTS):
                    if part.startswith("scores"):
                        scores(n, par, s, int(part[-1]))
                    elif part == "values":
                        if s > 0:
                            values(n, par, s - 1)
                        elif not (isinstance(n, int) and n == 0):
                            values(n - 1, 1 - par, NS - 1)
                    else:
                        c = STEPS[s - 1][0]
                        if c > 0:
                            finish(n, c - 1, 2 * (n * NS + s) + 1)
                        elif not (isinstance(n, int) and n == 0):
                            finish(n - 1, NC - 1, 2 * (n * NS + s) + 1)
                    if not last:
                        for i in range(done, ITEMS_BY[k]):
                            item(n + 1, 1 - par, i)
                        done = ITEMS_BY[k]

            pe.wait_ge(ident_done, 2)
            pe.wait_ge(consts_done, 6)
            for i in range(NI):
                item(0, 0, i)
            group(0, 0)
            with pe.Fori(0, NG // 2 - 1) as i:
                group(2 * i + 1, 1)
                group(2 * i + 2, 0)
            group(NG - 1, 1, last=True)
            values(NG - 1, 1, NS - 1)
            finish(NG - 1, NC - 1, 2 * NG * NS)

        @block.scalar
        def _(act):
            def reuse(stored, n, c):
                at_least(act, stored, 8 * NC * n + 16 * (c // 2))

            def denominators(n, c):
                act.wait_ge(sums_done, n * NC + c + 1)
                reuse(d_stored[c % 2], n, c)
                act.activation(d_raw[c % 2][:, :], km[0][:, 0, :], ACT.Copy).then_inc(d_read, 1)

            def output(n, c):
                act.wait_ge(pv_done, n * NS + FIRST_STEP[c + 1])
                reuse(o_stored[c % 2], n, c)
                act.activation(o_raw[c % 2][:, :], o_ps[:, :], ACT.Copy).then_inc(o_read, 1)

            def group(n):
                started = not (isinstance(n, int) and n == 0)
                for s, (c, t) in enumerate(STEPS):
                    o = offset(c, t)
                    at_least(act, pv_done, n * NS + s + 1 - PB)
                    used = s - PB + (STEPS[(s - PB) % NS][1] == 0)
                    at_least(act, added, n * NADD + adds_through(used))
                    at_least(act, added_0, n * NADD + adds_through(used))
                    for half in range(2):
                        act.wait_ge(scored, 2 * (n * NS + s) + half + 1)
                        act.activation(probs[s % PB][:, 2 * half:2 * half + 2, o:CH], km[half][:, :, o:CH],
                                       ACT.Exp, scale=SCALE).then_inc(exp_done, 1)
                    if t == 0 and (c > 0 or started):
                        output(*((n, c - 1) if c > 0 else (n - 1, NC - 1)))
                    if t == FIN + 1:
                        if c > 0:
                            denominators(n, c - 1)
                        elif started:
                            denominators(n - 1, NC - 1)

            group(0)
            with act.Fori(0, NG // 2 - 1) as i:
                group(2 * i + 1)
                group(2 * i + 2)
            group(NG - 1)
            output(NG - 1, NC - 1)
            denominators(NG - 1, NC - 1)

        @block.vector
        def _(dve):
            def item(m, i):
                dve.wait_ge(item_done, m * NI + i + 1)
                bank = qm[bank_of(i)]
                if ITEMS[i][0] == "maxrow":
                    c = ITEMS[i][1]
                    dve.tensor_scalar(neg_max[c][:, :], bank[0:REP, 0:CH], -1.0, None, ALU.mult
                                      ).then_inc(item_read, 1)
                    return
                _, c, h, sub, j = ITEMS[i]
                w = item_width(i)
                dve.reduce_max(part_max[c][:, sub * REP + h, j:j + 1], bank[:, 0:w], AX.X).then_inc(item_read, 1)
                if (h, sub, j) == (REP - 1, SUB - 1, c):
                    dve.wait_ge(item_read, m * NI + i + 1)
                    dve.reduce_max(row_max[c][:, :], part_max[c][:, :, :], AX.X).then_inc(max_done, 1)

            def group(n, last=False):
                done = 0
                for k, (s, part, _) in enumerate(PARTS):
                    if part == "scores 0" and s - 1 in ADD_STEPS:
                        add(dve, slice(0, 1), n, s - 1, 1, added_0)
                    if not last:
                        for i in range(done, ITEMS_BY[k]):
                            item(n + 1, i)
                        done = ITEMS_BY[k]
                add(dve, slice(0, 1), n, NS - 1, 1, added_0)

            for i in range(2):
                dve.memset(k_st[i][ROWS:ROWS + 1, :].bitcast(F32), 1.0).then_inc(consts_done, 1)
            for i in range(NI):
                item(0, i)
            dve.wait_ge(ident_done, 3)
            group(0)
            with dve.Fori(0, NG // 2 - 1) as i:
                group(2 * i + 1)
                group(2 * i + 2)
            group(NG - 1, last=True)


class Chain:

    def __init__(self, engine, semaphore, held):
        self.engine, self.semaphore, self.held, self.base, self.n = engine, semaphore, held, 0, 0

    def start(self, base):
        self.base, self.n = base, 0

    def link(self, instruction):
        self.n += 1
        instruction.then_inc(self.semaphore, 1)
        self.engine.wait_ge(self.semaphore, self.base + self.n)

    def hold(self):
        self.engine.sem_inc(self.held, 1)


def moments(dve, chain, rows, width, stats, mean_var):
    parts = max(1, width // BANK)
    for i in range(parts):
        ins = dve.bn_stats(stats[:, i, :], rows[:, i * (width // parts):(i + 1) * (width // parts)])
        if i == parts - 1:
            chain.link(ins)
    chain.hold()
    chain.link(dve.bn_aggr(mean_var, stats[:, 0:parts, :]))


def project_and_gate(nc, sem, keep, x, aT_d, wo, weight, lora_A, gw1, gb1, gamma, beta, gw2, gb2, den_d, rec_d, u_d):
    ER = E * R
    AG = ER + GH
    NT = N // P
    HALF = D // 2
    STEPS = NT + 2
    low, diff, onehot = keep
    x_t = x.rearrange("b (t p) d -> (b t) p d", p=P)
    u_t = u_d.rearrange("(t p) d -> t p d", p=P)

    def at_least(engine, semaphore, value):
        if not isinstance(value, int) or value > 0:
            engine.wait_ge(semaphore, value)

    ctx = ExitStack()
    with ctx:
        sb = lambda name, shape, dt=F32: ctx.enter_context(nc.sbuf_tensor(name, shape, dt))
        ps = lambda name, shape: ctx.enter_context(nc.psum_tensor(name, shape, F32))
        ident = sb("p3_ident", [P, P])
        ones_row = sb("p3_ones_row", [1, P])
        eps = sb("p3_eps", [P, 1])
        experts = sb("p3_experts", [P, E])
        experts_i = sb("p3_experts_i", [P, E], I32)
        wo_hi, wo_lo = sb("p3_wo_hi", [P, KC, D], F32R), sb("p3_wo_lo", [P, KC, D], F32R)
        wm_hi, wm_lo = sb("p3_wm_hi", [P, KC, D], F32R), sb("p3_wm_lo", [P, KC, D], F32R)
        ag_hi, ag_lo = sb("p3_ag_hi", [P, KC, AG], F32R), sb("p3_ag_lo", [P, KC, AG], F32R)
        gw2_raw = sb("p3_gw2_raw", [E, GH])
        gw2T = sb("p3_gw2T", [GH, E])
        rows_raw = sb("p3_rows_raw", [1, 3 * GH + E])
        rows = sb("p3_rows", [P, 3 * GH + E])
        x_in_sb = [sb(f"p3_x{i}", [P, D]) for i in range(2)]
        y = [sb(f"p3_y{i}", [P, D]) for i in range(2)]
        a_raw = sb("p3_a_raw", [P, KC, P])
        recip = sb("p3_recip", [P, KC, P])
        a_hi = [sb(f"p3_a_hi{i}", [P, KC, P], F32R) for i in range(2)]
        a_lo = [sb(f"p3_a_lo{i}", [P, KC, P], F32R) for i in range(2)]
        yT_hi, yT_lo = sb("p3_yT_hi", [P, KC, P], F32R), sb("p3_yT_lo", [P, KC, P], F32R)
        A_raw = low[:, 0:KC, :]
        stats = sb("p3_stats", [P, 2, 6])
        mean_var = sb("p3_mean_var", [P, 2])
        std = sb("p3_std", [P, 1])
        rstd = sb("p3_rstd", [P, 1])
        g_stats = sb("p3_g_stats", [P, 1, 6])
        g_mean_var = sb("p3_g_mean_var", [P, 2])
        g_std = sb("p3_g_std", [P, 1])
        g_rstd = sb("p3_g_rstd", [P, 1])
        hid = [sb(f"p3_hid{i}", [P, GH]) for i in range(2)]
        hidT = sb("p3_hidT", [GH, P])
        gates = sb("p3_gates", [P, E])
        top = sb("p3_top", [P, 8])
        top_at = sb("p3_top_at", [P, 8], U32)
        top_at_f = sb("p3_top_at_f", [P, 8])
        at_ps = ps("p3_at_ps", [P, 2, BANK])
        tr_ps = ps("p3_tr_ps", [P, 2, BANK])
        mm_ps = ps("p3_mm_ps", [P, 2, BANK])
        ag_ps = ps("p3_ag_ps", [P, BANK])
        sm_ps = ps("p3_sm_ps", [P, BANK])

        ident_done = sem("p3_ident_done")
        pool_const = sem("p3_pool_const")
        raw_in = [sem(f"p3_raw_in{i}") for i in range(2)]
        small_in = sem("p3_small_in")
        turned = sem("p3_turned")
        w_hi_done, w_lo_done = sem("p3_w_hi_done"), sem("p3_w_lo_done")
        small_pe, small_dve = sem("p3_small_pe"), sem("p3_small_dve")
        x_in = [sem(f"p3_x_in{i}") for i in range(2)]
        den_in, rec_done, rec_stored = sem("p3_den_in"), sem("p3_rec_done"), sem("p3_rec_stored")
        a_in = sem("p3_a_in")
        a_done = sem("p3_a_done")
        a_hi_done, a_lo_done = sem("p3_a_hi_done"), sem("p3_a_lo_done")
        wo_done = sem("p3_wo_done")
        sum_done = sem("p3_sum_done")
        var_done, std_done = sem("p3_var_done"), sem("p3_std_done")
        y_done = sem("p3_y_done")
        tr_done = sem("p3_tr_done")
        yT_hi_done, yT_lo_done = sem("p3_yT_hi_done"), sem("p3_yT_lo_done")
        mm_done = sem("p3_mm_done")
        u_done = sem("p3_u_done")
        u_stored = [sem(f"p3_u_stored{i}") for i in range(2)]
        ag_done = sem("p3_ag_done")
        low_done = sem("p3_low_done")
        h_done = sem("p3_h_done")
        g_var_done, g_std_done = sem("p3_g_var_done"), sem("p3_g_std_done")
        hid_done = sem("p3_hid_done")
        hidT_ps_done, hidT_done = sem("p3_hidT_ps_done"), sem("p3_hidT_done")
        gates_ps_done, gates_done = sem("p3_gates_ps_done"), sem("p3_gates_done")
        chain_sem, held_sem = sem("p3_chain"), sem("p3_held")

        block = ctx.enter_context(nc.Block())
        LOOPS = (NT - 2) // 2


        @block.sync
        def _(sp):
            def load_a(t):
                sp.dma_start(a_raw[:, :, :], aT_d[:, bass.ds(t * P, P)].rearrange("(k p) t -> p k t", p=P)
                             ).then_inc(a_in, 16)
                for h in range(REP):
                    sp.dma_start(recip[h * HD:(h + 1) * HD, :, :],
                                 rec_d[h:NH:REP, bass.ds(t * P, P)].unsqueeze(0).to_broadcast([HD, KC, P])
                                 ).then_inc(a_in, 16)

            def load_x(t, par):
                sp.dma_start(x_in_sb[par][:, :], x_t[bass.ds(t, 1), :, :].rearrange("o p d -> (o p) d")
                             ).then_inc(x_in[par], 16)

            def step(t, par):
                if not isinstance(t, int) or t + 2 < NT:
                    sp.wait_ge(a_lo_done, t + 2)
                    load_a(t + 2)
                    sp.wait_ge(sum_done, t + 1)
                    load_x(t + 2, par)
                if not isinstance(t, int) or t >= 1:
                    sp.wait_ge(u_done, t)
                    sp.dma_start(u_t[bass.ds(t - 1, 1), :, :].rearrange("o p d -> (o p) d"),
                                 y[1 - par][:, :]).then_inc(u_stored[1 - par], 16)

            sp.dma_start(gw2_raw[:, :], gw2).then_inc(small_in, 16)
            for i, row in enumerate((gb1, gamma, beta, gb2)):
                sp.dma_start(rows_raw[:, i * GH:i * GH + row.shape[0]],
                             row.rearrange("(o n) -> o n", o=1)).then_inc(small_in, 16)
            sp.dma_start(y[1][0:GH, :], gw1).then_inc(small_in, 16)
            for k in range(KC):
                sp.dma_start(A_raw[:, k, :].rearrange("p (e r) -> p e r", e=E),
                             lora_A[:, k * P:(k + 1) * P, :].rearrange("e p r -> p e r")).then_inc(small_in, 16)
            flat = lambda a: a.rearrange("h (q n) -> (h q) n", q=P // NH)
            sp.dma_start(y[0][:, :], flat(den_d)).then_inc(den_in, 16)
            for n in range(2 * KC):
                if n >= 2:
                    sp.wait_ge(w_lo_done, 2 * (n - 1))
                src = wo if n < KC else weight
                sp.dma_start(x_in_sb[n % 2][:, :], src[(n % KC) * P:(n % KC + 1) * P, :]).then_inc(raw_in[n % 2], 16)
                if n == 4:
                    sp.wait_ge(rec_done, 1)
                    sp.dma_start(flat(rec_d), y[0][:, :]).then_inc(rec_stored, 16)
                    sp.wait_ge(rec_stored, 16)
                    load_a(0)
            for t in range(2):
                sp.wait_ge(w_lo_done, 2 * (2 * KC - 1 + t))
                load_x(t, t)
            sp.wait_ge(a_lo_done, 1)
            load_a(1)
            step(0, 0)
            step(1, 1)
            with sp.Fori(0, LOOPS - 1) as i:
                step(2 * i + 2, 0)
                step(2 * i + 3, 1)
            step(NT - 2, 0)
            step(NT - 1, 1)
            step(NT, 0)
            for i in range(2):
                sp.wait_ge(u_stored[i], 16 * NT // 2)

        @block.gpsimd
        def _(pool):
            make_identity(pool, ident, ident_done)
            pool.memset(ones_row[:, :], 1.0).then_inc(pool_const, 1)
            pool.memset(eps[:, :], LN_EPS).then_inc(pool_const, 1)
            pool.iota(experts_i[:, :], pattern=[[1, E]], base=0, channel_multiplier=0).then_inc(pool_const, 1)

        @block.tensor
        def _(pe):
            pe.wait_ge(ident_done, 2)
            pe.wait_ge(pool_const, 3)
            pe.wait_ge(small_in, 16 * (6 + KC))
            pe.transpose(sm_ps[0:GH, 0:E], gw2_raw[:, :], ident[0:E, 0:E])
            pe.matmul(sm_ps[:, P:P + 3 * GH + E], ones_row[:, :], rows_raw[:, :], start=True, stop=True)
            for k in range(KC):
                last = pe.transpose(ag_ps[:, k * GH:(k + 1) * GH], y[1][0:GH, k * P:(k + 1) * P],
                                    ident[0:GH, 0:GH])
            last.then_inc(small_pe, 1)
            for n in range(KC):
                pe.wait_ge(raw_in[n % 2], 16 * ((KC + n) // 2 + 1))
                for half in range(2):
                    if n > 0:
                        pe.wait_ge(w_lo_done, 2 * (KC + n - 1) + half + 1)
                    for k in range(half * 4, half * 4 + 4):
                        last = pe.transpose(tr_ps[:, half, (k % 4) * P:(k % 4 + 1) * P],
                                            x_in_sb[n % 2][:, k * P:(k + 1) * P], ident[:, :])
                    last.then_inc(turned, 1)

            def step(t, par):
                a_ok = not isinstance(t, int) or t < NT
                b_ok = not isinstance(t, int) or 1 <= t <= NT
                c_ok = not isinstance(t, int) or t >= 2
                if a_ok:
                    at_least(pe, sum_done, t)
                    pe.wait_ge(a_lo_done, t + 1)
                    for half in range(2):
                        cols = slice(half * HALF, (half + 1) * HALF)
                        for k in range(KC):
                            last = matmul3(pe, at_ps[:, half, :], a_hi[par][:, k, :], a_lo[par][:, k, :],
                                           wo_hi[:, k, cols], wo_lo[:, k, cols], k == 0, k == KC - 1)
                    last.then_inc(wo_done, 1)
                if c_ok:
                    pe.wait_ge(hid_done, t - 1)
                    at_least(pe, gates_done, t - 2)
                    pe.transpose(sm_ps[0:GH, 0:P], hid[par][:, :], ident[:, :]).then_inc(hidT_ps_done, 1)
                if b_ok:
                    pe.wait_ge(yT_lo_done, t)
                    at_least(pe, u_done, t - 1)
                    for half in range(2):
                        cols = slice(half * HALF, (half + 1) * HALF)
                        for k in range(KC):
                            last = matmul3(pe, mm_ps[:, half, :], yT_hi[:, k, :], yT_lo[:, k, :],
                                           wm_hi[:, k, cols], wm_lo[:, k, cols], k == 0, k == KC - 1)
                    last.then_inc(mm_done, 1)
                    at_least(pe, low_done, t - 1)
                    at_least(pe, h_done, t - 1)
                    for k in range(KC):
                        last = matmul3(pe, ag_ps[:, 0:AG], yT_hi[:, k, :], yT_lo[:, k, :],
                                       ag_hi[:, k, :], ag_lo[:, k, :], k == 0, k == KC - 1)
                    last.then_inc(ag_done, 1)
                if c_ok:
                    pe.wait_ge(hidT_done, t - 1)
                    pe.matmul(sm_ps[:, P:P + E], hidT[:, :], gw2T[:, :], start=True, stop=True
                              ).then_inc(gates_ps_done, 1)
                if a_ok:
                    pe.wait_ge(y_done, t + 1)
                    at_least(pe, yT_lo_done, t)
                    for k in range(KC):
                        last = pe.transpose(tr_ps[:, k // 4, (k % 4) * P:(k % 4 + 1) * P],
                                            y[par][:, k * P:(k + 1) * P], ident[:, :])
                    last.then_inc(tr_done, 1)

            pe.wait_ge(w_lo_done, 4 * KC)
            pe.wait_ge(small_dve, 5)
            step(0, 0)
            step(1, 1)
            with pe.Fori(0, LOOPS) as i:
                step(2 * i + 2, 0)
                step(2 * i + 3, 1)
            step(NT, 0)
            step(NT + 1, 1)

        @block.scalar
        def _(act):
            def split_a(t, par):
                act.wait_ge(a_done, t + 1)
                at_least(act, wo_done, t - 1)
                act.activation(a_hi[par][:, :, :], a_raw[:, :, :], ACT.Copy).then_inc(a_hi_done, 1)

            def step(t, par):
                a_ok = not isinstance(t, int) or t < NT
                b_ok = not isinstance(t, int) or 1 <= t <= NT
                c_ok = not isinstance(t, int) or t >= 2
                if not isinstance(t, int) or t + 1 < NT:
                    split_a(t + 1, 1 - par)
                if a_ok:
                    act.wait_ge(var_done, t + 1)
                    act.activation(std[:, :], mean_var[:, 1:2], ACT.Sqrt, bias=eps[:, :]).then_inc(std_done, 1)
                if c_ok:
                    act.wait_ge(hidT_ps_done, t - 1)
                    act.activation(hidT[:, :], sm_ps[0:GH, 0:P], ACT.Copy).then_inc(hidT_done, 1)
                if b_ok:
                    act.wait_ge(ag_done, t)
                    act.activation(low[:, bass.ds(t - 1, 1), :].rearrange("p o r -> p (o r)"), ag_ps[:, 0:ER],
                                   ACT.Copy).then_inc(low_done, 1)
                    act.wait_ge(g_var_done, t)
                    act.activation(g_std[:, :], g_mean_var[:, 1:2], ACT.Sqrt, bias=eps[:, :]
                                   ).then_inc(g_std_done, 1)
                if a_ok:
                    act.wait_ge(tr_done, t + 1)
                    act.activation(yT_hi[:, :, :].rearrange("p k t -> p (k t)"),
                                   tr_ps[:, :, :].rearrange("p a b -> p (a b)"), ACT.Copy
                                   ).then_inc(yT_hi_done, 1)

            for n in range(KC):
                act.wait_ge(raw_in[n % 2], 16 * (n // 2 + 1))
                for half in range(2):
                    cols = slice(half * HALF, (half + 1) * HALF)
                    act.activation(wo_hi[:, n, cols], x_in_sb[n % 2][:, cols], ACT.Copy).then_inc(w_hi_done, 1)
            split_a(0, 0)
            for n in range(KC):
                for half in range(2):
                    act.wait_ge(turned, 2 * n + half + 1)
                    act.activation(wm_hi[:, 4 * half:4 * half + 4, n * P:(n + 1) * P],
                                   tr_ps[:, half, :].rearrange("p (k o) -> p k o", k=4), ACT.Copy
                                   ).then_inc(w_hi_done, 1)
            act.wait_ge(pool_const, 3)
            step(0, 0)
            step(1, 1)
            with act.Fori(0, LOOPS - 1) as i:
                step(2 * i + 2, 0)
                step(2 * i + 3, 1)
            step(NT - 2, 0)
            step(NT - 1, 1)
            step(NT, 0)
            step(NT + 1, 1)

        @block.vector
        def _(dve):
            chain = Chain(dve, chain_sem, held_sem)
            gb1_b, gamma_b, beta_b, gb2_b = (rows[:, 0:GH], rows[:, GH:2 * GH], rows[:, 2 * GH:3 * GH],
                                             rows[:, 3 * GH:3 * GH + E])

            def divide_a(t):
                dve.wait_ge(a_in, 16 * (1 + REP) * (t + 1))
                dve.tensor_tensor(a_raw[:, :, :], a_raw[:, :, :], recip[:, :, :], ALU.mult).then_inc(a_done, 1)

            def split_a(t, par):
                dve.wait_ge(a_hi_done, t + 1)
                at_least(dve, wo_done, t - 1)
                dve.tensor_tensor(a_lo[par][:, :, :], a_raw[:, :, :], a_hi[par][:, :, :].bitcast(F32),
                                  ALU.subtract).then_inc(a_lo_done, 1)

            def step(t, par):
                a_ok = not isinstance(t, int) or t < NT
                b_ok = not isinstance(t, int) or 1 <= t <= NT
                c_ok = not isinstance(t, int) or t >= 2
                if not isinstance(t, int) or t + 1 < NT:
                    divide_a(t + 1)
                    split_a(t + 1, 1 - par)
                if a_ok:
                    dve.wait_ge(x_in[par], 16 * (t // 2 + 1) if isinstance(t, int) else 8 * (t - par) + 16)
                    if not isinstance(t, int) or t >= 2:
                        dve.wait_ge(u_stored[par], 16 * (t // 2) if isinstance(t, int) else 8 * (t - par))
                    dve.wait_ge(wo_done, t + 1)
                    dve.tensor_tensor(y[par][:, :], at_ps[:, :, :].rearrange("p a b -> p (a b)"),
                                      x_in_sb[par][:, :], ALU.add).then_inc(sum_done, 1)
                    dve.wait_ge(sum_done, t + 1)
                    moments(dve, chain, y[par], D, stats, mean_var[:, :])
                    dve.sem_inc(var_done, 1)
                    dve.wait_ge(std_done, t + 1)
                    chain.link(dve.reciprocal(rstd[:, :], std[:, :]))
                    dve.tensor_scalar(y[par][:, :], y[par][:, :], mean_var[:, 0:1], rstd[:, :],
                                      ALU.subtract, ALU.mult).then_inc(y_done, 1)
                if c_ok:
                    dve.wait_ge(gates_ps_done, t - 1)
                    dve.tensor_tensor(gates[:, :], sm_ps[:, P:P + E], gb2_b, ALU.add).then_inc(gates_done, 1)
                    dve.wait_ge(gates_done, t - 1)
                    chain.hold()
                    chain.link(dve.max(top[:, :], gates[:, :]))
                    chain.hold()
                    chain.link(dve.max_index(top_at[:, :], top[:, :], gates[:, :]))
                    chain.link(dve.tensor_copy(top_at_f[:, :], top_at[:, :]))
                    dve.tensor_tensor(diff[:, bass.ds(t - 2, 1)], top[:, 1:2], top[:, 0:1], ALU.subtract)
                    for k in range(TOPK):
                        last = dve.tensor_scalar(onehot[:, bass.ds(t - 2, 1), k, :].rearrange("p o e -> p (o e)"),
                                                 experts[:, :], top_at_f[:, k:k + 1], None, ALU.is_equal)
                    chain.link(last)
                if b_ok:
                    dve.wait_ge(mm_done, t)
                    dve.tensor_tensor(y[1 - par][:, :], mm_ps[:, :, :].rearrange("p a b -> p (a b)"),
                                      y[1 - par][:, :], ALU.add).then_inc(u_done, 1)
                    h = hid[1 - par]
                    dve.wait_ge(ag_done, t)
                    dve.wait_ge(low_done, t)
                    dve.tensor_tensor(h[:, :], ag_ps[:, ER:AG], gb1_b, ALU.add).then_inc(h_done, 1)
                    dve.wait_ge(h_done, t)
                    moments(dve, chain, h, GH, g_stats, g_mean_var[:, :])
                    dve.sem_inc(g_var_done, 1)
                    dve.wait_ge(g_std_done, t)
                    chain.link(dve.reciprocal(g_rstd[:, :], g_std[:, :]))
                    chain.link(dve.tensor_scalar(h[:, :], h[:, :], g_mean_var[:, 0:1], g_rstd[:, :],
                                                 ALU.subtract, ALU.mult))
                    chain.link(dve.tensor_tensor(h[:, :], h[:, :], gamma_b, ALU.mult))
                    chain.link(dve.tensor_tensor(h[:, :], h[:, :], beta_b, ALU.add))
                    dve.tensor_scalar(h[:, :], h[:, :], 0.0, None, ALU.max).then_inc(hid_done, 1)
                if a_ok:
                    dve.wait_ge(yT_hi_done, t + 1)
                    dve.tensor_tensor(yT_lo[:, :, :].rearrange("p k t -> p (k t)"),
                                      tr_ps[:, :, :].rearrange("p a b -> p (a b)"),
                                      yT_hi[:, :, :].rearrange("p k t -> p (k t)").bitcast(F32),
                                      ALU.subtract).then_inc(yT_lo_done, 1)

            LINKS = 3 + 4 + 6

            dve.wait_ge(pool_const, 3)
            dve.tensor_copy(experts[:, :], experts_i[:, :]).then_inc(small_dve, 1)
            dve.wait_ge(small_pe, 1)
            dve.tensor_copy(gw2T[:, :], sm_ps[0:GH, 0:E]).then_inc(small_dve, 1)
            dve.tensor_copy(rows[:, :], sm_ps[:, P:P + 3 * GH + E]).then_inc(small_dve, 1)
            gw1T = ag_ps[:, 0:KC * GH].rearrange("p (k g) -> p k g", k=KC)
            dve.wait_ge(den_in, 16)
            chain.link(dve.reciprocal(recip[:, :, :], y[0][:, :].rearrange("p (k t) -> p k t", k=KC)))
            dve.tensor_copy(y[0][:, :].rearrange("p (k t) -> p k t", k=KC), recip[:, :, :]).then_inc(rec_done, 1)
            dve.wait_ge(small_in, 16 * (6 + KC))
            chain.link(dve.tensor_copy(ag_hi[:, :, ER:AG], gw1T))
            chain.link(dve.tensor_copy(ag_hi[:, :, 0:ER], A_raw))
            dve.tensor_tensor(ag_lo[:, :, ER:AG], gw1T, ag_hi[:, :, ER:AG].bitcast(F32), ALU.subtract
                              ).then_inc(small_dve, 1)
            dve.tensor_tensor(ag_lo[:, :, 0:ER], A_raw, ag_hi[:, :, 0:ER].bitcast(F32), ALU.subtract
                              ).then_inc(small_dve, 1)
            dve.wait_ge(small_dve, 5)
            for n in range(KC):
                for half in range(2):
                    cols = slice(half * HALF, (half + 1) * HALF)
                    dve.wait_ge(w_hi_done, 2 * n + half + 1)
                    dve.tensor_tensor(wo_lo[:, n, cols], x_in_sb[n % 2][:, cols], wo_hi[:, n, cols].bitcast(F32),
                                      ALU.subtract).then_inc(w_lo_done, 1)
            divide_a(0)
            split_a(0, 0)
            for n in range(KC):
                for half in range(2):
                    dve.wait_ge(w_hi_done, 2 * (KC + n) + half + 1)
                    out = slice(n * P, (n + 1) * P)
                    dve.tensor_tensor(wm_lo[:, 4 * half:4 * half + 4, out],
                                      tr_ps[:, half, :].rearrange("p (k o) -> p k o", k=4),
                                      wm_hi[:, 4 * half:4 * half + 4, out].bitcast(F32), ALU.subtract
                                      ).then_inc(w_lo_done, 1)
            step(0, 0)
            step(1, 1)
            before = chain.n
            with dve.Fori(0, LOOPS - 1) as i:
                chain.start(before + i * (2 * LINKS))
                step(2 * i + 2, 0)
                step(2 * i + 3, 1)
            assert chain.n == 2 * LINKS, chain.n
            chain.start(before + (LOOPS - 1) * 2 * LINKS)
            step(NT - 2, 0)
            step(NT - 1, 1)
            step(NT, 0)
            step(NT + 1, 1)


def mix_experts(nc, sem, keep, u_d, lora_B, out):
    ER = E * R
    NT = N // P
    HALF = D // 2
    NB = 4
    low, diff, onehot = keep
    u_t = u_d.rearrange("(t p) d -> t p d", p=P)
    out_t = out.rearrange("b (t p) d -> (b t) p d", p=P)

    def at_least(engine, semaphore, value):
        if not isinstance(value, int) or value > 0:
            engine.wait_ge(semaphore, value)

    ctx = ExitStack()
    with ctx:
        sb = lambda name, shape, dt=F32: ctx.enter_context(nc.sbuf_tensor(name, shape, dt))
        ident = sb("p4_ident", [P, P])
        ones = sb("p4_ones", [P, P])
        eps = sb("p4_eps", [P, 1])
        lb = sb("p4_lora_B", [ER, D])
        counts = sb("p4_counts", [P, TOPK * E])
        allowed = sb("p4_allowed", [P, TOPK, E])
        exp_d = sb("p4_exp", [P, NT])
        den = sb("p4_den", [P, NT])
        prob = sb("p4_prob", [P, TOPK, NT])
        weights = sb("p4_weights", [P, NT, E])
        second = sb("p4_second", [P, NT, E])
        u = [sb(f"p4_u{i}", [P, D]) for i in range(2 * NB)]
        lw = [sb(f"p4_lw{i}", [P, ER]) for i in range(NB)]
        lwT = [sb(f"p4_lwT{i}", [ER, P]) for i in range(NB)]
        res = [sb(f"p4_res{i}", [P, D]) for i in range(NB)]
        stats = [sb(f"p4_stats{i}", [P, 2, 6]) for i in range(NB)]
        mean_var = [sb(f"p4_mean_var{i}", [P, 2]) for i in range(NB)]
        std = [sb(f"p4_std{i}", [P, 1]) for i in range(NB)]
        rstd = [sb(f"p4_rstd{i}", [P, 1]) for i in range(NB)]
        shift = [sb(f"p4_shift{i}", [P, 1]) for i in range(NB)]
        tr = [ctx.enter_context(nc.psum_tensor(f"p4_tr{i}", [P, BANK], F32)) for i in range(2)]
        lo = [ctx.enter_context(nc.psum_tensor(f"p4_lo{i}", [P, 2, BANK], F32)) for i in range(3)]

        ident_done, pool_const = sem("p4_ident_done"), sem("p4_pool_const")
        lb_in = sem("p4_lb_in")
        u_in = [sem(f"p4_u_in{i}") for i in range(2 * NB)]
        part_done, counts_ps_done, exp_done = sem("p4_part_done"), sem("p4_counts_ps_done"), sem("p4_exp_done")
        lw_done, tr_done, lwT_done = sem("p4_lw_done"), sem("p4_tr_done"), sem("p4_lwT_done")
        lora_done, z_done = sem("p4_lora_done"), sem("p4_z_done")
        var_done, std_done, shift_done = sem("p4_var_done"), sem("p4_std_done"), sem("p4_shift_done")
        res_done = sem("p4_res_done")
        stored = [sem(f"p4_stored{i}") for i in range(NB)]
        chain_sem, held_sem = sem("p4_chain"), sem("p4_held")

        block = ctx.enter_context(nc.Block())
        BODY = 2 * NB

        def per(t, k, n, times):
            return times * (t // n) if isinstance(t, int) else (t - k) * (times // n) + times * (k // n)

        @block.sync
        def _(sp):
            def load(t, k):
                sp.dma_start(u[k][:, :], u_t[bass.ds(t, 1), :, :].rearrange("o p d -> (o p) d")).then_inc(u_in[k], 16)

            def one(t, k, more=True):
                sp.wait_ge(res_done, t + 1)
                sp.dma_start(out_t[bass.ds(t, 1), :, :].rearrange("o p d -> (o p) d"), res[k % NB][:, :]
                             ).then_inc(stored[k % NB], 16)
                if more:
                    load(t + BODY, k)

            sp.dma_start(lb[:, :], lora_B.rearrange("e r o -> (e r) o")).then_inc(lb_in, 16)
            for k in range(BODY):
                load(k, k)
            with sp.Fori(0, NT // BODY - 1) as i:
                for k in range(BODY):
                    one(BODY * i + k, k)
            for k in range(BODY):
                one(NT - BODY + k, k, more=False)
            for i in range(NB):
                sp.wait_ge(stored[i], 16 * NT // NB)

        @block.gpsimd
        def _(pool):
            make_identity(pool, ident, ident_done)
            pool.memset(ones[:, :], 1.0).then_inc(pool_const, 1)
            pool.memset(eps[:, :], LN_EPS).then_inc(pool_const, 1)

        @block.tensor
        def _(pe):
            pe.wait_ge(ident_done, 2)
            pe.wait_ge(pool_const, 2)
            pe.wait_ge(part_done, 1)
            pe.matmul(tr[1][:, 0:TOPK * E], ones[:, :], counts[:, :], start=True, stop=True
                      ).then_inc(counts_ps_done, 1)
            pe.wait_ge(lb_in, 16)

            def turn(t, k):
                pe.wait_ge(lw_done, t + 1)
                at_least(pe, lwT_done, t - 1)
                pe.transpose(tr[k % 2][:, 0:P], lw[k % NB][:, :], ident[:, :]).then_inc(tr_done, 1)

            def products(t, k):
                pe.wait_ge(lwT_done, t + 1)
                at_least(pe, z_done, t - 1)
                for half in range(2):
                    last = pe.matmul(lo[k % 2][:, half, :], lwT[k % NB][:, :],
                                     lb[:, half * HALF:(half + 1) * HALF], start=True, stop=True)
                last.then_inc(lora_done, 1)

            turn(0, 0)
            for k in range(BODY):
                turn(k + 1, (k + 1) % BODY)
                products(k, k)
            with pe.Fori(0, NT // BODY - 2) as i:
                for k in range(BODY):
                    turn(BODY * i + BODY + k + 1, (k + 1) % BODY)
                    products(BODY * i + BODY + k, k)
            for k in range(BODY):
                if k + 1 < BODY:
                    turn(NT - BODY + k + 1, k + 1)
                products(NT - BODY + k, k)

        @block.scalar
        def _(act):
            act.wait_ge(pool_const, 2)
            act.activation(exp_d[:, :], diff[:, :], ACT.Exp).then_inc(exp_done, 1)

            def copy_T(t, k):
                act.wait_ge(tr_done, t + 1)
                at_least(act, lora_done, t - NB + 1)
                act.activation(lwT[k % NB][:, :], tr[k % 2][:, 0:P], ACT.Copy).then_inc(lwT_done, 1)

            def norm(t, k):
                b = k % NB
                act.wait_ge(var_done, t + 1)
                act.activation(std[b][:, :], mean_var[b][:, 1:2], ACT.Sqrt, bias=eps[:, :]).then_inc(std_done, 1)
                act.wait_ge(shift_done, t + 1)
                if not isinstance(t, int) or t >= NB:
                    act.wait_ge(stored[b], per(t, k, NB, 16))
                act.activation(res[b][:, :], u[k][:, :], ACT.Identity, bias=shift[b][:, :], scale=rstd[b][:, :]
                               ).then_inc(res_done, 1)

            copy_T(0, 0)
            for k in range(BODY):
                copy_T(k + 1, (k + 1) % BODY)
                norm(k, k)
            with act.Fori(0, NT // BODY - 2) as i:
                for k in range(BODY):
                    copy_T(BODY * i + BODY + k + 1, (k + 1) % BODY)
                    norm(BODY * i + BODY + k, k)
            for k in range(BODY):
                if k + 1 < BODY:
                    copy_T(NT - BODY + k + 1, k + 1)
                norm(NT - BODY + k, k)

        @block.vector
        def _(dve):
            chain = Chain(dve, chain_sem, held_sem)
            flat = onehot[:, :, :, :].rearrange("p t k e -> p (t k e)").rearrange("p (t s) -> p s t", t=NT)
            dve.reduce_sum(counts[:, :], flat, AX.X).then_inc(part_done, 1)
            dve.wait_ge(exp_done, 1)
            chain.link(dve.tensor_scalar(den[:, :], exp_d[:, :], 1.0, None, ALU.add))
            chain.link(dve.reciprocal(prob[:, 0, :], den[:, :]))
            chain.link(dve.tensor_tensor(prob[:, 1, :], exp_d[:, :], prob[:, 0, :], ALU.mult))
            dve.wait_ge(counts_ps_done, 1)
            chain.link(dve.tensor_scalar(allowed[:, :, :].rearrange("p k e -> p (k e)"), tr[1][:, 0:TOPK * E],
                                         float(CAPACITY), 1.0 / R, ALU.is_le, ALU.mult))
            for k, w in ((0, weights), (1, second)):
                chain.link(dve.tensor_tensor(w[:, :, :], onehot[:, :, k, :],
                                             prob[:, k, :].unsqueeze(2).to_broadcast([P, NT, E]), ALU.mult))
                chain.link(dve.tensor_tensor(w[:, :, :], w[:, :, :],
                                             allowed[:, k, :].unsqueeze(1).to_broadcast([P, NT, E]), ALU.mult))
            chain.link(dve.tensor_tensor(weights[:, :, :], weights[:, :, :], second[:, :, :], ALU.add))

            def weigh(t, k):
                at_least(dve, tr_done, t - NB + 1)
                dve.tensor_tensor(lw[k % NB][:, :].rearrange("p (e r) -> p e r", e=E),
                                  low[:, bass.ds(t, 1), :].rearrange("p o (e r) -> p (o e) r", e=E),
                                  weights[:, bass.ds(t, 1), :].rearrange("p o e -> p (o e)").unsqueeze(2)
                                  .to_broadcast([P, E, R]), ALU.mult).then_inc(lw_done, 1)

            def tile(t, k):
                b = k % NB
                dve.wait_ge(u_in[k], per(t, k, BODY, 16) + 16)
                dve.wait_ge(lora_done, t + 1)
                dve.tensor_tensor(u[k][:, :], lo[k % 2][:, :, :].rearrange("p a b -> p (a b)"), u[k][:, :],
                                  ALU.add).then_inc(z_done, 1)
                dve.wait_ge(z_done, t + 1)
                moments(dve, chain, u[k], D, stats[b], mean_var[b][:, :])
                dve.sem_inc(var_done, 1)
                dve.wait_ge(std_done, t + 1)
                at_least(dve, res_done, t - NB + 1)
                chain.link(dve.reciprocal(rstd[b][:, :], std[b][:, :]))
                dve.scalar_tensor_tensor(out=shift[b][:, :], in0=mean_var[b][:, 0:1], scalar=-1.0,
                                         in1=rstd[b][:, :], op0=ALU.mult, op1=ALU.mult).then_inc(shift_done, 1)

            LINKS = 3
            for k in range(2):
                weigh(k, k)
            for k in range(BODY):
                weigh(k + 2, (k + 2) % BODY)
                tile(k, k)
            before = chain.n
            with dve.Fori(0, NT // BODY - 2) as i:
                chain.start(before + i * (BODY * LINKS))
                for k in range(BODY):
                    weigh(BODY * i + BODY + k + 2, (k + 2) % BODY)
                    tile(BODY * i + BODY + k, k)
            assert chain.n == BODY * LINKS
            chain.start(before + (NT // BODY - 2) * BODY * LINKS)
            for k in range(BODY):
                if k + 2 < BODY:
                    weigh(NT - BODY + k + 2, k + 2)
                tile(NT - BODY + k, k)


def build(nc, x, wq, wk, wv, wo, weight, lora_A, lora_B, gw1, gb1, gamma, beta, gw2, gb2, out):
    dram = lambda name, shape: nc.dram_tensor(name, shape, F32, kind="Internal").ap()
    q_hi, q_lo = dram("q_hi", [D, N]), dram("q_lo", [D, N])
    k_hi, k_lo = dram("k_hi", [NKV * HD, N]), dram("k_lo", [NKV * HD, N])
    v_d = dram("v", [NKV, P, N // P, HD])
    aT_d = dram("attended_T", [D, N])
    den_d, rec_d = dram("denominators", [NH, N]), dram("reciprocals", [NH, N])
    u_d = dram("u", [N, D])
    with ExitStack() as ctx:
        sem = lambda name: ctx.enter_context(nc.semaphore(name))
        project_qkv(nc, sem, x, wq, wk, wv, q_hi, q_lo, k_hi, k_lo, v_d)
        attend(nc, sem, q_hi, q_lo, k_hi, k_lo, v_d, aT_d, den_d)
        keep = (ctx.enter_context(nc.sbuf_tensor("low", [P, N // P, E * R], F32)),
                ctx.enter_context(nc.sbuf_tensor("diff", [P, N // P], F32)),
                ctx.enter_context(nc.sbuf_tensor("onehot", [P, N // P, TOPK, E], F32)))
        project_and_gate(nc, sem, keep, x, aT_d, wo, weight, lora_A, gw1, gb1, gamma, beta, gw2, gb2, den_d, rec_d, u_d)
        mix_experts(nc, sem, keep, u_d, lora_B, out)


_INS = ["L0_attn_x", "L0_attn_wq", "L0_attn_wk", "L0_attn_wv", "L0_attn_wo", "L0_ffn_weight", "L0_ffn_lora_A",
        "L0_ffn_lora_B", "L0_ffn_gw1", "L0_ffn_gb1", "L0_ffn_ln_gamma", "L0_ffn_ln_beta", "L0_ffn_gw2", "L0_ffn_gb2"]
_OUT = ((B, S, D), "float32")


def kernel(**inputs):
    import numpy as _np
    import concourse.bacc as _bacc
    from concourse.bass_utils import run_bass_kernel_spmd as _run

    nc = _bacc.Bacc("TRN2", target_bir_lowering=False, num_devices=1)
    arrays, args = {}, []
    for name in _INS:
        a = _np.ascontiguousarray(inputs[name])
        arrays[f"in_{name}"] = a
        args.append(nc.dram_tensor(f"in_{name}", a.shape, mybir.dt.from_np(a.dtype), kind="ExternalInput").ap())
    args.append(nc.dram_tensor("out", _OUT[0], mybir.dt.from_np(_np.dtype(_OUT[1])), kind="ExternalOutput").ap())
    build(nc, *args)
    return _run(nc, [arrays], core_ids=[0]).results[0]["out"]
```

```python
import concourse.bass as bass
from concourse import mybir
from contextlib import ExitStack
import numpy as np

F32 = mybir.dt.float32
F32R = mybir.dt.float32r
BF16 = mybir.dt.bfloat16
I32 = mybir.dt.int32
U32 = mybir.dt.uint32
ALU = mybir.AluOpType
ACT = mybir.ActivationFunctionType
AX = mybir.AxisListType

P = 128
BANK = 512
B, S, D = 2, 2048, 1024
N = B * S
NH, NKV, HD = 32, 8, 32
REP = NH // NKV
KC = D // P
SCALE = HD ** -0.5
NEG = -1e30
E, R, TOPK = 8, 16, 2
GH = 4 * E
CAPACITY = int(3.0 * N / E)
LN_EPS = 1e-5


def make_identity(pool, ident, sem):
    pool.memset(ident[:, :], 0.0).then_inc(sem, 1)
    pool.wait_ge(sem, 1)
    pool.affine_select(out=ident[:, :], in_=ident[:, :], compare_op=ALU.not_equal, fill=1.0,
                       base=0, pattern=[[-1, P]], channel_multiplier=1).then_inc(sem, 1)


def matmul3(pe, out, lhs_hi, lhs_lo, rhs_hi, rhs_lo, first, last):
    pe.matmul(out, lhs_hi, rhs_hi, start=first, stop=False)
    pe.matmul(out, lhs_hi, rhs_lo, start=False, stop=False)
    return pe.matmul(out, lhs_lo, rhs_hi, start=False, stop=last)


def project_qkv(nc, sem, x, wq, wk, wv, q_hi, q_lo, k_hi, k_lo, v_d):
    TT = 512
    NT = N // TT
    SUB = TT // P
    KV = NKV * HD
    WC = D + 2 * KV
    QG, KG, VG = D // P, KV // P, SUB
    G = QG + KG + VG
    GB = 4
    TB = 4
    T_AT = 4
    assert GB + TB == 8 and G % 2 == 0
    x_t = x.rearrange("b (t s p) d -> (b t) p s d", s=SUB, p=P)

    ctx = ExitStack()
    with ctx:
        sb = lambda name, shape, dt: ctx.enter_context(nc.sbuf_tensor(name, shape, dt))
        ident = sb("p1_ident", [P, P], F32)
        w_hi = sb("p1_w_hi", [P, KC, WC], F32R)
        w_lo = sb("p1_w_lo", [P, KC, WC], F32R)
        w_raw = sb("p1_w_raw", [P, 2, WC], F32)
        x_raw = sb("p1_x_raw", [P, SUB, D], F32)
        xT_hi = [sb(f"p1_xT_hi{i}", [P, KC, TT], F32R) for i in range(2)]
        xT_lo = [sb(f"p1_xT_lo{i}", [P, KC, TT], F32R) for i in range(2)]
        out_hi = sb("p1_out_hi", [P, 2, TT], F32R)
        out_lo = sb("p1_out_lo", [P, 2, TT], F32R)
        v_out = sb("p1_v_out", [P, 2, KV], F32)
        tp = [ctx.enter_context(nc.psum_tensor(f"p1_tp{i}", [P, BANK], F32)) for i in range(TB)]
        acc = [ctx.enter_context(nc.psum_tensor(f"p1_acc{i}", [P, BANK], F32)) for i in range(GB)]

        ident_done = sem("p1_ident_done")
        w_in = [sem(f"p1_w_in{i}") for i in range(2)]
        w_hi_done = sem("p1_w_hi_done")
        w_lo_done = sem("p1_w_lo_done")
        x_in = sem("p1_x_in")
        transposed = sem("p1_transposed")
        xT_hi_done = sem("p1_xT_hi_done")
        xT_lo_done = sem("p1_xT_lo_done")
        group_done = sem("p1_group_done")
        out_hi_done = sem("p1_out_hi_done")
        evacuated = sem("p1_evacuated")
        stored = [sem(f"p1_stored{i}") for i in range(2)]

        HALF = (QG + KG) // 2 * 32 + VG // 2 * 16

        def stored_before(t, g):
            n = g // 2
            return t * HALF + min(n, (QG + KG) // 2) * 32 + max(0, n - (QG + KG) // 2) * 16

        block = ctx.enter_context(nc.Block())

        @block.gpsimd
        def _(pool):
            make_identity(pool, ident, ident_done)

        @block.sync
        def _(sp):
            def load_x(t):
                sp.dma_start(x_raw[:, :, :], x_t[t, :, :, :]).then_inc(x_in, 16)

            def load_w(k):
                if k >= 2:
                    sp.wait_ge(w_lo_done, k - 1)
                rows = slice(k * P, (k + 1) * P)
                sp.dma_start(w_raw[:, k % 2, 0:D], wq[rows, :]).then_inc(w_in[k % 2], 16)
                sp.dma_start(w_raw[:, k % 2, D:D + KV], wk[rows, :]).then_inc(w_in[k % 2], 16)
                sp.dma_start(w_raw[:, k % 2, D + KV:WC], wv[rows, :]).then_inc(w_in[k % 2], 16)

            def tile(t, load=True):
                for g in range(G):
                    sp.wait_ge(evacuated, t * G + g + 1)
                    cols = bass.ds(t * TT, TT)
                    if g < QG + KG:
                        hi, lo, r = (q_hi, q_lo, g) if g < QG else (k_hi, k_lo, g - QG)
                        rows = slice(r * P, (r + 1) * P)
                        sp.dma_start(hi[rows, cols], out_hi[:, g % 2, :].bitcast(F32)).then_inc(stored[g % 2], 16)
                        sp.dma_start(lo[rows, cols], out_lo[:, g % 2, :].bitcast(F32)).then_inc(stored[g % 2], 16)
                    else:
                        s = g - QG - KG
                        sp.dma_start(v_d[:, :, bass.ds(t * SUB + s, 1), :].rearrange("g p t d -> p g (t d)"),
                                     v_out[:, g % 2, :].rearrange("p (g d) -> p g d", d=HD)
                                     ).then_inc(stored[g % 2], 16)
                    if g == T_AT + KC - 1 and load:
                        sp.wait_ge(transposed, (t + 2) * KC)
                        load_x(t + 2)

            load_w(0)
            load_x(0)
            for k in range(1, KC):
                load_w(k)
            sp.wait_ge(transposed, KC)
            load_x(1)
            tile(0)
            with sp.Fori(0, NT // 2 - 2) as i:
                tile(2 * i + 1)
                tile(2 * i + 2)
            tile(NT - 3)
            tile(NT - 2, load=False)
            tile(NT - 1, load=False)
            for i in range(2):
                sp.wait_ge(stored[i], NT * HALF)

        @block.tensor
        def _(pe):
            def transpose_chunk(t, k):
                if k == 0:
                    pe.wait_ge(x_in, 16 * t + 16)
                if not (isinstance(t, int) and t * KC + k < TB):
                    pe.wait_ge(xT_lo_done, t * KC + k + 1 - TB)
                for s in range(SUB):
                    last = pe.transpose(tp[k % TB][:, s * P:(s + 1) * P], x_raw[:, s, k * P:(k + 1) * P],
                                        ident[:, :])
                last.then_inc(transposed, 1)

            def product(t, par, g, k):
                xh, xl, bank = xT_hi[par], xT_lo[par], acc[(par * G + g) % GB]
                if g < QG + KG:
                    cols = slice(g * P, (g + 1) * P)
                    return matmul3(pe, bank[:, :], w_hi[:, k, cols], w_lo[:, k, cols],
                                   xh[:, k, :], xl[:, k, :], k == 0, k == KC - 1)
                rows = slice((g - QG - KG) * P, (g - QG - KG + 1) * P)
                return matmul3(pe, bank[:, 0:KV], xh[:, k, rows], xl[:, k, rows],
                               w_hi[:, k, D + KV:WC], w_lo[:, k, D + KV:WC], k == 0, k == KC - 1)

            def tile(t, par, begin=0, last=False):
                pe.wait_ge(xT_lo_done, (t + 1) * KC)
                for g in range(begin, G):
                    if not (isinstance(t, int) and t * G + g < GB):
                        pe.wait_ge(evacuated, t * G + g + 1 - GB)
                    for k in range(KC):
                        done = product(t, par, g, k)
                    done.then_inc(group_done, 1)
                    if T_AT <= g < T_AT + KC and not last:
                        transpose_chunk(t + 1, g - T_AT)

            pe.wait_ge(ident_done, 2)
            transpose_chunk(0, 0)
            for k in range(KC):
                if k + 1 < KC:
                    transpose_chunk(0, k + 1)
                pe.wait_ge(w_lo_done, k + 1)
                pe.wait_ge(xT_lo_done, k + 1)
                for g in range(GB):
                    done = product(0, 0, g, k)
                    if k == KC - 1:
                        done.then_inc(group_done, 1)
            tile(0, 0, begin=GB)
            with pe.Fori(0, NT // 2 - 1) as i:
                tile(2 * i + 1, 1)
                tile(2 * i + 2, 0)
            tile(NT - 1, 1, last=True)

        @block.scalar
        def _(act):
            def split_x(t, par, k):
                act.wait_ge(transposed, t * KC + k + 1)
                act.activation(xT_hi[par][:, k, :], tp[k % TB][:, :], ACT.Copy).then_inc(xT_hi_done, 1)

            def tile(t, par, last=False):
                for g in range(G):
                    if g < QG + KG:
                        act.wait_ge(stored[g % 2], stored_before(t, g))
                        act.wait_ge(group_done, t * G + g + 1)
                        act.activation(out_hi[:, g % 2, :], acc[(par * G + g) % GB][:, :],
                                       ACT.Copy).then_inc(out_hi_done, 1)
                    if T_AT <= g < T_AT + KC and not last:
                        split_x(t + 1, 1 - par, g - T_AT)

            for k in range(KC):
                act.wait_ge(w_in[k % 2], 48 * (k // 2 + 1))
                act.activation(w_hi[:, k, :], w_raw[:, k % 2, :], ACT.Copy).then_inc(w_hi_done, 1)
                split_x(0, 0, k)
            tile(0, 0)
            with act.Fori(0, NT // 2 - 1) as i:
                tile(2 * i + 1, 1)
                tile(2 * i + 2, 0)
            tile(NT - 1, 1, last=True)

        @block.vector
        def _(dve):
            def split_x(t, par, k):
                dve.wait_ge(xT_hi_done, t * KC + k + 1)
                dve.tensor_tensor(xT_lo[par][:, k, :], tp[k % TB][:, :], xT_hi[par][:, k, :].bitcast(F32),
                                  ALU.subtract).then_inc(xT_lo_done, 1)

            def tile(t, par, last=False):
                for g in range(G):
                    bank = acc[(par * G + g) % GB]
                    if g < QG + KG:
                        dve.wait_ge(out_hi_done, t * (QG + KG) + g + 1)
                        dve.tensor_tensor(out_lo[:, g % 2, :], bank[:, :], out_hi[:, g % 2, :].bitcast(F32),
                                          ALU.subtract).then_inc(evacuated, 1)
                    else:
                        dve.wait_ge(stored[g % 2], stored_before(t, g))
                        dve.wait_ge(group_done, t * G + g + 1)
                        dve.tensor_copy(v_out[:, g % 2, :], bank[:, 0:KV]).then_inc(evacuated, 1)
                    if T_AT <= g < T_AT + KC and not last:
                        split_x(t + 1, 1 - par, g - T_AT)

            for k in range(KC):
                dve.wait_ge(w_hi_done, k + 1)
                dve.tensor_tensor(w_lo[:, k, :], w_raw[:, k % 2, :], w_hi[:, k, :].bitcast(F32),
                                  ALU.subtract).then_inc(w_lo_done, 1)
                split_x(0, 0, k)
            tile(0, 0)
            with dve.Fori(0, NT // 2 - 1) as i:
                tile(2 * i + 1, 1)
                tile(2 * i + 2, 0)
            tile(NT - 1, 1, last=True)


def attend(nc, sem, q_hi, q_lo, k_hi, k_lo, v_d, aT_d, den_d):
    NG = B * NKV
    CH = 512
    NC = S // CH
    SUB = CH // P
    NT = S // P
    ROWS = 3 * HD
    STEPS = [(c, t) for c in range(NC) for t in range(SUB * (c + 1))]
    NS = len(STEPS)
    FIRST_STEP = [STEPS.index((c, 0)) for c in range(NC)] + [NS]
    PB = 8
    assert NS % PB == 0
    FIN = 2

    def offset(c, t):
        return max(0, t - SUB * c) * P

    TLAG = 4

    def key_tiles(c, sub, j):
        return SUB if j < c else sub + 1

    units = [[("score", c, h, sub, j) for sub in range(SUB) for j in range(c + 1)
              for h in range(0, REP, SUB // key_tiles(c, sub, j))] for c in range(NC)]
    ITEMS = []
    for c in range(NC):
        ITEMS += units[c][:TLAG] + ([("maxrow", c - 1)] if c else []) + units[c][TLAG:]
    ITEMS.append(("maxrow", NC - 1))
    NI = len(ITEMS)

    def item_heads(i):
        return SUB // key_tiles(*(ITEMS[i][k] for k in (1, 3, 4)))

    def item_keys(i):
        return P * key_tiles(*(ITEMS[i][k] for k in (1, 3, 4)))

    def item_width(i):
        return CH if ITEMS[i][0] == "maxrow" else item_heads(i) * item_keys(i)

    def items_read(i):
        return sum(item[0] == "score" for item in ITEMS[:i + 1])

    NR = items_read(NI - 1)

    PARTS = []
    for s in range(NS):
        o, before = offset(*STEPS[s]), STEPS[s - 1]
        half = 2 * (CH - o) + (2 * P if STEPS[s][1] >= SUB * STEPS[s][0] else 0)
        PARTS += [(s, "scores 0", half), (s, "scores 1", half), (s, "values", 4 * (CH - offset(*before)) + 300)]
        if before[1] == FIN:
            PARTS.append((s, "finish", 4 * CH + 300))
    ADD_STEPS = [s for s, (c, t) in enumerate(STEPS) if t > 0 or c == 0]
    NADD = len(ADD_STEPS)

    def adds_through(s):
        return sum(x <= s for x in ADD_STEPS) if s >= 0 else sum(x <= s + NS for x in ADD_STEPS) - NADD

    QM = 3
    COL_PE, COL_DVE, FIXED_DVE = 0.42, 1.04, 110

    def place_items():
        dve_cost = [0 if ITEMS[i][0] == "maxrow" else item_width(i) * COL_DVE + FIXED_DVE for i in range(NI)]
        add_cost = [(CH - offset(*STEPS[s - 1])) * COL_DVE + FIXED_DVE if part == "values" and s - 1 in ADD_STEPS
                    else 0 for s, part, _ in PARTS]
        dve_total = sum(dve_cost) + sum(add_cost)
        pe_total = COL_PE * (sum(cost for _, _, cost in PARTS[:-2]) + sum(item_width(i) for i in range(NI)))
        by, i, pe, dve = [], 0, 0.0, 0.0
        for (_, _, cost), add in zip(PARTS, add_cost):
            pe += cost * COL_PE
            dve += add
            while i < NI - 1 and dve * pe_total <= pe * dve_total:
                pe += item_width(i) * COL_PE
                dve += dve_cost[i]
                i += 1
            by.append(i)
        by[-1] = NI
        return by

    ITEMS_BY = place_items()
    STEP_OF_ITEM = [PARTS[next(k for k, by in enumerate(ITEMS_BY) if by > i)][0] for i in range(NI)]
    bank_of = lambda i: i % QM
    bank_user = lambda i: i - QM if i >= QM else max(x for x in range(NI) if x % QM == i) - NI

    def at_least(engine, semaphore, value):
        if not isinstance(value, int) or value > 0:
            engine.wait_ge(semaphore, value)

    ctx = ExitStack()
    with ctx:
        sb = lambda name, shape, dt: ctx.enter_context(nc.sbuf_tensor(name, shape, dt))
        ps = lambda name, shape: ctx.enter_context(nc.psum_tensor(name, shape, F32))
        ident = sb("p2_ident", [P, P], F32)
        ident_bf = sb("p2_ident_bf", [P, P], BF16)
        mask_q = sb("p2_mask_q", [P, P], BF16)
        mask_k = sb("p2_mask_k", [P, P], BF16)
        ones = sb("p2_ones", [P, HD], F32)
        zeros = sb("p2_zeros", [P, REP, P], F32)
        q_st = [sb(f"p2_q_st{i}", [P, REP, S], F32R) for i in range(2)]
        k_st = [sb(f"p2_k_st{i}", [P, S], F32R) for i in range(2)]
        v = [sb(f"p2_v{i}", [P, NT, HD], F32) for i in range(2)]
        probs = [sb(f"p2_probs{i}", [P, REP, CH], F32) for i in range(PB)]
        psums = [sb(f"p2_psums{i}", [P, REP, CH], F32) for i in range(2)]
        part_max = [sb(f"p2_part_max{c}", [P, REP * SUB, c + 1], F32) for c in range(NC)]
        row_max = [sb(f"p2_row_max{c}", [P, REP * SUB], F32) for c in range(NC)]
        neg_max = [sb(f"p2_neg_max{c}", [REP, CH], F32R) for c in range(NC)]
        o_raw = [sb(f"p2_o_raw{i}", [P, CH], F32) for i in range(2)]
        d_raw = [sb(f"p2_d_raw{i}", [P, CH], F32) for i in range(2)]
        qm = [ps(f"p2_qm{i}", [P, BANK]) for i in range(QM)]
        km = [ps(f"p2_km{i}", [P, 2, BANK]) for i in range(2)]
        o_ps = ps("p2_o", [P, BANK])

        ident_done = sem("p2_ident_done")
        consts_done = sem("p2_consts_done")
        q_in = [[sem(f"p2_q_in{i}_{c}") for c in range(NC)] for i in range(2)]
        k_in = [[sem(f"p2_k_in{i}_{c}") for c in range(NC)] for i in range(2)]
        v_in = [sem(f"p2_v_in{i}") for i in range(2)]
        m_in = [[sem(f"p2_m_in{i}_{c}") for c in range(NC)] for i in range(2)]
        item_done = sem("p2_item_done")
        item_read = sem("p2_item_read")
        neg_done = sem("p2_neg_done")
        max_done = sem("p2_max_done")
        scored = sem("p2_scored")
        exp_done = sem("p2_exp_done")
        pv_done = sem("p2_pv_done")
        added = sem("p2_added")
        added_0 = sem("p2_added_0")
        o_read = sem("p2_o_read")
        sums_done = sem("p2_sums_done")
        d_read = sem("p2_d_read")
        o_stored = [sem(f"p2_o_stored{i}") for i in range(2)]
        d_stored = [sem(f"p2_d_stored{i}") for i in range(2)]
        held = sem("p2_held")

        block = ctx.enter_context(nc.Block())


        @block.sync
        def _(sp):
            def batch_head(n):
                b, g = (n >> (NKV.bit_length() - 1)) & (B - 1), n & (NKV - 1)
                return b, g

            def hold():
                sp.sem_inc(held, 1)

            def load_q(b, g, par, c):
                rows, cols = bass.ds(g * P, P), bass.ds(b * S + c * CH, CH)
                for at, src in ((0, q_hi), (HD, q_lo), (2 * HD, q_hi)):
                    sp.dma_start(q_st[par][at:at + HD, :, c * CH:(c + 1) * CH].bitcast(F32),
                                 src[rows, cols].rearrange("(h d) t -> d h t", d=HD)).then_inc(q_in[par][c], 16)

            def load_k(b, g, par, c):
                rows, cols = bass.ds(g * HD, HD), bass.ds(b * S + c * CH, CH)
                for at, src in ((0, k_hi), (HD, k_hi), (2 * HD, k_lo)):
                    sp.dma_start(k_st[par][at:at + HD, c * CH:(c + 1) * CH].bitcast(F32), src[rows, cols]
                                 ).then_inc(k_in[par][c], 16)

            def load_v(b, g, par):
                sp.dma_start(v[par][:, :, :],
                             v_d[bass.ds(g, 1), :, bass.ds(b * NT, NT), :].rearrange("g p t d -> (g p) t d")
                             ).then_inc(v_in[par], 16)

            def send_max(m, par, c):
                sp.wait_ge(neg_done, m * NC + c + 1)
                hold()
                sp.dma_start(q_st[par][ROWS:ROWS + 1, :, c * CH:(c + 1) * CH].bitcast(F32),
                             neg_max[c][:, :].bitcast(F32)).then_inc(m_in[par][c], 16)

            def store_o(n, b, g, c):
                sp.wait_ge(o_read, n * NC + c + 1)
                hold()
                sp.dma_start(aT_d[bass.ds(g * P, P), bass.ds(b * S + c * CH, CH)],
                             o_raw[c % 2][:, :]).then_inc(o_stored[c % 2], 16)

            def store_d(n, b, g, c):
                sp.wait_ge(d_read, n * NC + c + 1)
                hold()
                sp.dma_start(den_d[bass.ds(g * REP, REP), bass.ds(b * S + c * CH, CH)],
                             d_raw[c % 2][0:P:HD, :]).then_inc(d_stored[c % 2], 16)

            def group(n, par, last=False, load=True):
                b, g = batch_head(n)
                b1, g1 = batch_head(n + 1)
                b2, g2 = batch_head(n + 2)
                before = batch_head(n - 1)
                events = []
                for c in range(NC):
                    end = FIRST_STEP[c + 1]
                    if load:
                        events.append((end + 0.5, "load q", c))
                        events.append((FIRST_STEP[NC - 1] + SUB * (c + 1) + 0.5, "load k", c))
                    if c < NC - 1:
                        events.append((end + 1.5, "store o", c))
                        events.append((end + FIN + 2.5, "store d", c))
                    if not last:
                        events.append((STEP_OF_ITEM[ITEMS.index(("maxrow", c))] + 1, "max", c))
                if not (isinstance(n, int) and n == 0):
                    events.append((1.5, "store o before", NC - 1))
                    events.append((FIN + 2.5, "store d before", NC - 1))
                    if not last:
                        events.append((1.4, "load v", 0))
                for _, what, c in sorted(events):
                    if what == "load q":
                        sp.wait_ge(scored, 2 * (n * NS + FIRST_STEP[c + 1]))
                        hold()
                        load_q(b2, g2, par, c)
                    elif what == "load k":
                        sp.wait_ge(scored, 2 * (n * NS + FIRST_STEP[NC - 1] + SUB * (c + 1)))
                        hold()
                        load_k(b2, g2, par, c)
                    elif what == "load v":
                        sp.wait_ge(pv_done, n * NS)
                        hold()
                        load_v(b1, g1, 1 - par)
                    elif what == "store o":
                        store_o(n, b, g, c)
                    elif what == "store d":
                        store_d(n, b, g, c)
                    elif what == "store o before":
                        store_o(n - 1, *before, c)
                    elif what == "store d before":
                        store_d(n - 1, *before, c)
                    else:
                        send_max(n + 1, 1 - par, c)

            for g in range(2):
                for c in range(NC):
                    load_k(0, g, g, c)
                    load_q(0, g, g, c)
                load_v(0, g, g)
            for c in range(NC):
                send_max(0, 0, c)
            group(0, 0)
            with sp.Fori(0, NG // 2 - 2) as i:
                group(2 * i + 1, 1)
                group(2 * i + 2, 0)
            group(NG - 3, 1)
            group(NG - 2, 0, load=False)
            group(NG - 1, 1, last=True, load=False)
            store_o(NG - 1, B - 1, NKV - 1, NC - 1)
            store_d(NG - 1, B - 1, NKV - 1, NC - 1)
            for i in range(2):
                sp.wait_ge(o_stored[i], 16 * NG * NC // 2)
                sp.wait_ge(d_stored[i], 16 * NG * NC // 2)

        def add(engine, heads, n, s, halves, done):
            c, t = STEPS[s]
            o = offset(c, t)
            sums, new, old = (x[:, heads] for x in (psums[c % 2], probs[s % PB], probs[(s - 1) % PB]))
            if t == (c > 0):
                at_least(engine, sums_done, n * NC + c - 1)
            engine.wait_ge(exp_done, 2 * (n * NS + s) + halves)
            if t == 0:
                engine.tensor_tensor(sums[:, :, 0:P], new[:, :, 0:P], zeros[:, heads, :], ALU.add).then_inc(done, 1)
            elif t == 1:
                engine.tensor_tensor(sums[:, :, o:CH], old[:, :, o:CH], new[:, :, o:CH], ALU.add).then_inc(done, 1)
            else:
                engine.wait_ge(done, n * NADD + adds_through(s) - 1)
                engine.tensor_tensor(sums[:, :, o:CH], sums[:, :, o:CH], new[:, :, o:CH], ALU.add).then_inc(done, 1)

        @block.gpsimd
        def _(pool):
            make_identity(pool, ident, ident_done)
            pool.memset(ones[:, :], 1.0).then_inc(consts_done, 1)
            pool.memset(zeros[:, :, :], 0.0).then_inc(ident_done, 1)
            pool.memset(mask_q[:, :], 0.0).then_inc(ident_done, 1)
            pool.memset(mask_k[:, :], 0.0).then_inc(ident_done, 1)
            pool.wait_ge(ident_done, 5)
            pool.tensor_copy(ident_bf[:, :], ident[:, :]).then_inc(consts_done, 1)
            pool.affine_select(out=mask_q[:, :], in_=mask_q[:, :], compare_op=ALU.is_ge, fill=NEG,
                               base=0, pattern=[[-1, P]], channel_multiplier=1).then_inc(consts_done, 1)
            pool.affine_select(out=mask_k[:, :], in_=mask_k[:, :], compare_op=ALU.is_ge, fill=NEG,
                               base=0, pattern=[[1, P]], channel_multiplier=-1).then_inc(consts_done, 1)

            def group(n, heads=slice(1, REP)):
                for s in ADD_STEPS:
                    add(pool, heads, n, s, 2, added)

            group(0)
            with pool.Fori(0, NG // 2 - 1) as i:
                group(2 * i + 1)
                group(2 * i + 2)
            group(NG - 1, slice(2, REP))

        @block.tensor
        def _(pe):
            def item(m, par, i):
                user = bank_user(i)
                if ITEMS[user][0] == "maxrow":
                    at_least(pe, neg_done, (m if user >= 0 else m - 1) * NC + ITEMS[user][1] + 1)
                else:
                    at_least(pe, item_read, (m if user >= 0 else m - 1) * NR + items_read(user % NI))
                bank = qm[bank_of(i)]
                if ITEMS[i][0] == "maxrow":
                    c = ITEMS[i][1]
                    pe.wait_ge(max_done, m * NC + c + 1)
                    for sub in range(SUB):
                        last = pe.transpose(bank[0:REP, sub * P:(sub + 1) * P],
                                            row_max[c][:, sub * REP:(sub + 1) * REP], ident[:, :])
                    last.then_inc(item_done, 1)
                    return
                _, c, h, sub, j = ITEMS[i]
                if (h, sub, j) == (0, 0, 0):
                    pe.wait_ge(q_in[par][c], 48 * (m // 2 + 1) if isinstance(m, int) else q_loads(m, par))
                    pe.wait_ge(k_in[par][c], 48 * (m // 2 + 1) if isinstance(m, int) else q_loads(m, par))
                q0 = c * CH + sub * P
                keys = item_keys(i)
                for x in range(item_heads(i)):
                    last = pe.matmul(bank[:, x * keys:(x + 1) * keys], q_st[par][0:ROWS, h + x, q0:q0 + P],
                                     k_st[par][0:ROWS, j * BANK:j * BANK + keys], start=True, stop=j < c)
                    if j == c:
                        last = pe.matmul(bank[:, (x + 1) * keys - P:(x + 1) * keys], ident_bf[:, :], mask_q[:, :],
                                         start=False, stop=True)
                last.then_inc(item_done, 1)

            def q_loads(m, par):
                return 24 * (m - par) + 48

            def scores(n, par, s, half):
                c, t = STEPS[s]
                o = offset(c, t)
                at_least(pe, exp_done, 2 * (n * NS + s) + half - 1)
                if half == 0 and STEPS[s - 1][1] == FIN + 1 and s > 0:
                    at_least(pe, d_read, n * NC + STEPS[s - 1][0])
                if half == 0 and t == 0:
                    pe.wait_ge(m_in[par][c], q_loads(n, par) // 3)
                diag = t >= SUB * c
                for x in range(2):
                    h = 2 * half + x
                    last = pe.matmul(km[half][:, x, o:CH], k_st[par][0:ROWS + 1, t * P:(t + 1) * P],
                                     q_st[par][0:ROWS + 1, h, c * CH + o:(c + 1) * CH], start=True, stop=not diag)
                    if diag:
                        last = pe.matmul(km[half][:, x, o:o + P], ident_bf[:, :], mask_k[:, :],
                                         start=False, stop=True)
                last.then_inc(scored, 1)

            def heads_matmul(out, lhs, rhs, o, start, stop):
                for h in range(REP):
                    last = pe.matmul(out[h * HD:(h + 1) * HD, o:CH], lhs, rhs[:, h, o:CH], start=start, stop=stop)
                return last

            def values(n, par, s):
                c, t = STEPS[s]
                if s == 0:
                    pe.wait_ge(v_in[par], q_loads(n, par) // 3)
                pe.wait_ge(exp_done, 2 * (n * NS + s + 1))
                if t == 0:
                    at_least(pe, o_read, n * NC + c)
                heads_matmul(o_ps, v[par][:, t, :], probs[s % PB], offset(c, t), t == 0,
                             t == SUB * (c + 1) - 1).then_inc(pv_done, 1)

            def finish(n, c, scores_before):
                pe.wait_ge(added, n * NADD + adds_through(FIRST_STEP[c + 1] - 1))
                pe.wait_ge(added_0, n * NADD + adds_through(FIRST_STEP[c + 1] - 1))
                pe.wait_ge(exp_done, scores_before)
                heads_matmul(km[0][:, 0, :], ones[:, :], psums[c % 2], 0, True, True).then_inc(sums_done, 1)

            def group(n, par, last=False):
                done = 0
                for k, (s, part, _) in enumerate(PARTS):
                    if part.startswith("scores"):
                        scores(n, par, s, int(part[-1]))
                    elif part == "values":
                        if s > 0:
                            values(n, par, s - 1)
                        elif not (isinstance(n, int) and n == 0):
                            values(n - 1, 1 - par, NS - 1)
                    else:
                        c = STEPS[s - 1][0]
                        if c > 0:
                            finish(n, c - 1, 2 * (n * NS + s) + 1)
                        elif not (isinstance(n, int) and n == 0):
                            finish(n - 1, NC - 1, 2 * (n * NS + s) + 1)
                    if not last:
                        for i in range(done, ITEMS_BY[k]):
                            item(n + 1, 1 - par, i)
                        done = ITEMS_BY[k]

            pe.wait_ge(ident_done, 2)
            pe.wait_ge(consts_done, 6)
            for i in range(NI):
                item(0, 0, i)
            group(0, 0)
            with pe.Fori(0, NG // 2 - 1) as i:
                group(2 * i + 1, 1)
                group(2 * i + 2, 0)
            group(NG - 1, 1, last=True)
            values(NG - 1, 1, NS - 1)
            finish(NG - 1, NC - 1, 2 * NG * NS)

        @block.scalar
        def _(act):
            def reuse(stored, n, c):
                at_least(act, stored, 8 * NC * n + 16 * (c // 2))

            def denominators(n, c):
                act.wait_ge(sums_done, n * NC + c + 1)
                reuse(d_stored[c % 2], n, c)
                act.activation(d_raw[c % 2][:, :], km[0][:, 0, :], ACT.Copy).then_inc(d_read, 1)

            def output(n, c):
                act.wait_ge(pv_done, n * NS + FIRST_STEP[c + 1])
                reuse(o_stored[c % 2], n, c)
                act.activation(o_raw[c % 2][:, :], o_ps[:, :], ACT.Copy).then_inc(o_read, 1)

            def negate(m, i):
                c = ITEMS[i][1]
                act.wait_ge(item_done, m * NI + i + 1)
                act.activation(neg_max[c][:, :], qm[bank_of(i)][0:REP, 0:CH], ACT.Copy, scale=-1.0
                               ).then_inc(neg_done, 1)

            def exps(n, s, half):
                c, t = STEPS[s]
                o = offset(c, t)
                if half == 0:
                    at_least(act, pv_done, n * NS + s + 1 - PB)
                    used = s - PB + (STEPS[(s - PB) % NS][1] == 0)
                    at_least(act, added, n * NADD + adds_through(used))
                    at_least(act, added_0, n * NADD + adds_through(used))
                act.wait_ge(scored, 2 * (n * NS + s) + half + 1)
                act.activation(probs[s % PB][:, 2 * half:2 * half + 2, o:CH], km[half][:, :, o:CH],
                               ACT.Exp, scale=SCALE).then_inc(exp_done, 1)

            def group(n, last=False):
                started = not (isinstance(n, int) and n == 0)
                done = 0
                for k, (s, part, _) in enumerate(PARTS):
                    c, t = STEPS[s]
                    if part.startswith("scores"):
                        exps(n, s, int(part[-1]))
                    elif part == "values" and t == 0:
                        if c > 0:
                            output(n, c - 1)
                        elif started:
                            output(n - 1, NC - 1)
                    elif part == "finish":
                        if c > 0:
                            denominators(n, c - 1)
                        elif started:
                            denominators(n - 1, NC - 1)
                    for i in range(done, ITEMS_BY[k]):
                        if ITEMS[i][0] == "maxrow" and not last:
                            negate(n + 1, i)
                    done = ITEMS_BY[k]

            for i in range(NI):
                if ITEMS[i][0] == "maxrow":
                    negate(0, i)
            group(0)
            with act.Fori(0, NG // 2 - 1) as i:
                group(2 * i + 1)
                group(2 * i + 2)
            group(NG - 1, last=True)
            output(NG - 1, NC - 1)
            denominators(NG - 1, NC - 1)

        @block.vector
        def _(dve):
            def item(m, i):
                if ITEMS[i][0] == "maxrow":
                    return
                _, c, h, sub, j = ITEMS[i]
                at, heads = sub * REP + h, item_heads(i)
                dve.wait_ge(item_done, m * NI + i + 1)
                dve.reduce_max(part_max[c][:, at:at + heads, j], qm[bank_of(i)][:, 0:item_width(i)].rearrange(
                    "p (h k) -> p h k", h=heads), AX.X).then_inc(item_read, 1)
                if (h + heads, sub, j) == (REP, SUB - 1, c):
                    dve.wait_ge(item_read, m * NR + items_read(i))
                    dve.reduce_max(row_max[c][:, :], part_max[c][:, :, :], AX.X).then_inc(max_done, 1)

            def group(n, last=False):
                heads = slice(0, 2 if last else 1)
                done = 0
                for k, (s, part, _) in enumerate(PARTS):
                    if part == "values" and s - 1 in ADD_STEPS:
                        add(dve, heads, n, s - 1, 1, added_0)
                    if not last:
                        for i in range(done, ITEMS_BY[k]):
                            item(n + 1, i)
                        done = ITEMS_BY[k]
                add(dve, heads, n, NS - 1, 1, added_0)

            for i in range(2):
                dve.memset(k_st[i][ROWS:ROWS + 1, :].bitcast(F32), 1.0).then_inc(consts_done, 1)
            for i in range(NI):
                item(0, i)
            dve.wait_ge(ident_done, 3)
            group(0)
            with dve.Fori(0, NG // 2 - 1) as i:
                group(2 * i + 1)
                group(2 * i + 2)
            group(NG - 1, last=True)


class Chain:

    def __init__(self, engine, semaphore, held):
        self.engine, self.semaphore, self.held, self.base, self.n = engine, semaphore, held, 0, 0

    def start(self, base):
        self.base, self.n = base, 0

    def link(self, instruction):
        self.n += 1
        instruction.then_inc(self.semaphore, 1)
        self.engine.wait_ge(self.semaphore, self.base + self.n)

    def hold(self):
        self.engine.sem_inc(self.held, 1)


def moments(dve, chain, rows, width, stats, mean_var):
    parts = max(1, width // BANK)
    for i in range(parts):
        ins = dve.bn_stats(stats[:, i, :], rows[:, i * (width // parts):(i + 1) * (width // parts)])
        if i == parts - 1:
            chain.link(ins)
    chain.hold()
    chain.link(dve.bn_aggr(mean_var, stats[:, 0:parts, :]))


def project_and_gate(nc, sem, keep, x, aT_d, wo, weight, lora_A, gw1, gb1, gamma, beta, gw2, gb2, den_d, rec_d, u_d):
    ER = E * R
    AG = ER + GH
    NT = N // P
    HALF = D // 2
    low, diff, onehot = keep
    x_t = x.rearrange("b (t p) d -> (b t) p d", p=P)
    u_t = u_d.rearrange("(t p) d -> t p d", p=P)

    def at_least(engine, semaphore, value):
        if not isinstance(value, int) or value > 0:
            engine.wait_ge(semaphore, value)

    ctx = ExitStack()
    with ctx:
        sb = lambda name, shape, dt=F32: ctx.enter_context(nc.sbuf_tensor(name, shape, dt))
        ps = lambda name, shape: ctx.enter_context(nc.psum_tensor(name, shape, F32))
        ident = sb("p3_ident", [P, P])
        ones_row = sb("p3_ones_row", [1, P])
        eps = sb("p3_eps", [P, 1])
        experts = sb("p3_experts", [P, E])
        experts_i = sb("p3_experts_i", [P, E], I32)
        wo_hi, wo_lo = sb("p3_wo_hi", [P, KC, D], F32R), sb("p3_wo_lo", [P, KC, D], F32R)
        wm_hi, wm_lo = sb("p3_wm_hi", [P, KC, D], F32R), sb("p3_wm_lo", [P, KC, D], F32R)
        ag_hi, ag_lo = sb("p3_ag_hi", [P, KC, AG], F32R), sb("p3_ag_lo", [P, KC, AG], F32R)
        gw2_raw = sb("p3_gw2_raw", [E, GH])
        gw2T = sb("p3_gw2T", [GH, E])
        rows_raw = sb("p3_rows_raw", [1, 3 * GH + E])
        rows = sb("p3_rows", [P, 3 * GH + E])
        x_in_sb = [sb(f"p3_x{i}", [P, D]) for i in range(2)]
        y = [sb(f"p3_y{i}", [P, D]) for i in range(2)]
        a_raw = sb("p3_a_raw", [P, KC, P])
        recip = sb("p3_recip", [P, KC, P])
        a_hi = [sb(f"p3_a_hi{i}", [P, KC, P], F32R) for i in range(2)]
        a_lo = [sb(f"p3_a_lo{i}", [P, KC, P], F32R) for i in range(2)]
        yT_hi, yT_lo = sb("p3_yT_hi", [P, KC, P], F32R), sb("p3_yT_lo", [P, KC, P], F32R)
        A_raw = low[:, 0:KC, :]
        raw = x_in_sb + [low[:, i * KC:(i + 1) * KC, :].rearrange("p k r -> p (k r)") for i in range(1, NT // KC)]
        RB = len(raw)
        stats = sb("p3_stats", [P, 2, 6])
        mean_var = sb("p3_mean_var", [P, 2])
        std = sb("p3_std", [P, 1])
        rstd = sb("p3_rstd", [P, 1])
        g_stats = sb("p3_g_stats", [P, 1, 6])
        g_mean_var = sb("p3_g_mean_var", [P, 2])
        g_std = sb("p3_g_std", [P, 1])
        g_rstd = sb("p3_g_rstd", [P, 1])
        hid = [sb(f"p3_hid{i}", [P, GH]) for i in range(2)]
        hidT = sb("p3_hidT", [GH, P])
        gates = sb("p3_gates", [P, E])
        top = sb("p3_top", [P, 8])
        top_at = sb("p3_top_at", [P, 8], U32)
        top_at_f = sb("p3_top_at_f", [P, 8])
        at_ps = ps("p3_at_ps", [P, 2, BANK])
        tr_ps = ps("p3_tr_ps", [P, 2, BANK])
        mm_ps = ps("p3_mm_ps", [P, 2, BANK])
        ag_ps = ps("p3_ag_ps", [P, BANK])
        sm_ps = ps("p3_sm_ps", [P, BANK])

        ident_done = sem("p3_ident_done")
        pool_const = sem("p3_pool_const")
        raw_in = [sem(f"p3_raw_in{i}") for i in range(RB)]
        small_in = sem("p3_small_in")
        turned = sem("p3_turned")
        w_hi_done, w_lo_done = sem("p3_w_hi_done"), sem("p3_w_lo_done")
        small_pe, small_dve = sem("p3_small_pe"), sem("p3_small_dve")
        x_in = [sem(f"p3_x_in{i}") for i in range(2)]
        den_in, rec_done, rec_stored = sem("p3_den_in"), sem("p3_rec_done"), sem("p3_rec_stored")
        a_in = sem("p3_a_in")
        a_done = sem("p3_a_done")
        a_hi_done, a_lo_done = sem("p3_a_hi_done"), sem("p3_a_lo_done")
        wo_done = sem("p3_wo_done")
        sum_done = sem("p3_sum_done")
        var_done, std_done = sem("p3_var_done"), sem("p3_std_done")
        y_done = sem("p3_y_done")
        tr_done = sem("p3_tr_done")
        yT_hi_done, yT_lo_done = sem("p3_yT_hi_done"), sem("p3_yT_lo_done")
        mm_done = sem("p3_mm_done")
        u_done = sem("p3_u_done")
        u_stored = [sem(f"p3_u_stored{i}") for i in range(2)]
        ag_done = sem("p3_ag_done")
        low_done = sem("p3_low_done")
        h_done = sem("p3_h_done")
        g_var_done, g_std_done = sem("p3_g_var_done"), sem("p3_g_std_done")
        hid_done = sem("p3_hid_done")
        hidT_ps_done, hidT_done = sem("p3_hidT_ps_done"), sem("p3_hidT_done")
        gates_ps_done, gates_done = sem("p3_gates_ps_done"), sem("p3_gates_done")
        chain_sem, held_sem = sem("p3_chain"), sem("p3_held")

        block = ctx.enter_context(nc.Block())
        LOOPS = (NT - 2) // 2


        @block.sync
        def _(sp):
            def load_a(t):
                sp.dma_start(a_raw[:, :, :], aT_d[:, bass.ds(t * P, P)].rearrange("(k p) t -> p k t", p=P)
                             ).then_inc(a_in, 16)
                for h in range(REP):
                    sp.dma_start(recip[h * HD:(h + 1) * HD, :, :],
                                 rec_d[h:NH:REP, bass.ds(t * P, P)].unsqueeze(0).to_broadcast([HD, KC, P])
                                 ).then_inc(a_in, 16)

            def load_x(t, par):
                sp.dma_start(x_in_sb[par][:, :], x_t[bass.ds(t, 1), :, :].rearrange("o p d -> (o p) d")
                             ).then_inc(x_in[par], 16)

            def step(t, par):
                if not isinstance(t, int) or t + 2 < NT:
                    sp.wait_ge(a_lo_done, t + 2)
                    load_a(t + 2)
                    sp.wait_ge(sum_done, t + 1)
                    load_x(t + 2, par)
                if not isinstance(t, int) or t >= 1:
                    sp.wait_ge(u_done, t)
                    sp.dma_start(u_t[bass.ds(t - 1, 1), :, :].rearrange("o p d -> (o p) d"),
                                 y[1 - par][:, :]).then_inc(u_stored[1 - par], 16)

            flat = lambda a: a.rearrange("h (q n) -> (h q) n", q=P // NH)
            sp.dma_start(y[0][:, :], flat(den_d)).then_inc(den_in, 16)
            for n in range(2 * KC):
                if n >= RB:
                    sp.wait_ge(w_lo_done, 2 * (n - RB + 1))
                src = wo if n < KC else weight
                sp.dma_start(raw[n % RB][:, :], src[(n % KC) * P:(n % KC + 1) * P, :]).then_inc(raw_in[n % RB], 16)
                if n == RB - 1:
                    sp.wait_ge(rec_done, 1)
                    sp.dma_start(flat(rec_d), y[0][:, :]).then_inc(rec_stored, 16)
                    sp.wait_ge(rec_stored, 16)
                    load_a(0)
                if n == KC + RB - 1:
                    sp.wait_ge(a_lo_done, 1)
                    load_a(1)
                if n == KC - 1:
                    sp.dma_start(gw2_raw[:, :], gw2).then_inc(small_in, 16)
                    for i, row in enumerate((gb1, gamma, beta, gb2)):
                        sp.dma_start(rows_raw[:, i * GH:i * GH + row.shape[0]],
                                     row.rearrange("(o n) -> o n", o=1)).then_inc(small_in, 16)
                    sp.dma_start(y[1][0:GH, :], gw1).then_inc(small_in, 16)
                    for k in range(KC):
                        sp.dma_start(A_raw[:, k, :].rearrange("p (e r) -> p e r", e=E),
                                     lora_A[:, k * P:(k + 1) * P, :].rearrange("e p r -> p e r")).then_inc(small_in, 16)
            for t in range(2):
                last_use = max(n for n in range(2 * KC) if n % RB == t)
                sp.wait_ge(w_lo_done, 2 * (last_use + 1))
                load_x(t, t)
            step(0, 0)
            step(1, 1)
            with sp.Fori(0, LOOPS - 1) as i:
                step(2 * i + 2, 0)
                step(2 * i + 3, 1)
            step(NT - 2, 0)
            step(NT - 1, 1)
            step(NT, 0)
            for i in range(2):
                sp.wait_ge(u_stored[i], 16 * NT // 2)

        @block.gpsimd
        def _(pool):
            make_identity(pool, ident, ident_done)
            pool.memset(ones_row[:, :], 1.0).then_inc(pool_const, 1)
            pool.memset(eps[:, :], LN_EPS).then_inc(pool_const, 1)
            pool.iota(experts_i[:, :], pattern=[[1, E]], base=0, channel_multiplier=0).then_inc(pool_const, 1)

        @block.tensor
        def _(pe):
            pe.wait_ge(ident_done, 2)
            pe.wait_ge(pool_const, 3)
            def attention_wo(t, par, half):
                if half == 0:
                    at_least(pe, sum_done, t)
                    pe.wait_ge(a_lo_done, t + 1)
                cols = slice(half * HALF, (half + 1) * HALF)
                for k in range(KC):
                    last = matmul3(pe, at_ps[:, half, :], a_hi[par][:, k, :], a_lo[par][:, k, :],
                                   wo_hi[:, k, cols], wo_lo[:, k, cols], k == 0, k == KC - 1)
                if half == 1:
                    last.then_inc(wo_done, 1)

            def step(t, par):
                a_ok = not isinstance(t, int) or t < NT
                b_ok = not isinstance(t, int) or 1 <= t <= NT
                c_ok = not isinstance(t, int) or t >= 2
                if a_ok and not (isinstance(t, int) and t == 0):
                    for half in range(2):
                        attention_wo(t, par, half)
                if c_ok:
                    pe.wait_ge(hid_done, t - 1)
                    at_least(pe, gates_done, t - 2)
                    pe.transpose(sm_ps[0:GH, 0:P], hid[par][:, :], ident[:, :]).then_inc(hidT_ps_done, 1)
                if b_ok:
                    pe.wait_ge(yT_lo_done, t)
                    at_least(pe, u_done, t - 1)
                    for half in range(2):
                        cols = slice(half * HALF, (half + 1) * HALF)
                        for k in range(KC):
                            last = matmul3(pe, mm_ps[:, half, :], yT_hi[:, k, :], yT_lo[:, k, :],
                                           wm_hi[:, k, cols], wm_lo[:, k, cols], k == 0, k == KC - 1)
                    last.then_inc(mm_done, 1)
                    at_least(pe, low_done, t - 1)
                    at_least(pe, h_done, t - 1)
                    for k in range(KC):
                        last = matmul3(pe, ag_ps[:, 0:AG], yT_hi[:, k, :], yT_lo[:, k, :],
                                       ag_hi[:, k, :], ag_lo[:, k, :], k == 0, k == KC - 1)
                    last.then_inc(ag_done, 1)
                if c_ok:
                    pe.wait_ge(hidT_done, t - 1)
                    pe.matmul(sm_ps[:, P:P + E], hidT[:, :], gw2T[:, :], start=True, stop=True
                              ).then_inc(gates_ps_done, 1)
                if a_ok:
                    pe.wait_ge(y_done, t + 1)
                    at_least(pe, yT_lo_done, t)
                    for k in range(KC):
                        last = pe.transpose(tr_ps[:, k // 4, (k % 4) * P:(k % 4 + 1) * P],
                                            y[par][:, k * P:(k + 1) * P], ident[:, :])
                    last.then_inc(tr_done, 1)

            for n in range(KC):
                pe.wait_ge(raw_in[(KC + n) % RB], 16 * ((KC + n) // RB + 1))
                for half in range(2):
                    if n > 0:
                        pe.wait_ge(w_lo_done, 2 * (KC + n - 1) + half + 1)
                    for k in range(half * 4, half * 4 + 4):
                        last = pe.transpose(tr_ps[:, half, (k % 4) * P:(k % 4 + 1) * P],
                                            raw[(KC + n) % RB][:, k * P:(k + 1) * P], ident[:, :])
                    last.then_inc(turned, 1)
                if n == 1:
                    pe.wait_ge(w_lo_done, 2 * KC)
                    attention_wo(0, 0, 0)
                elif n == 3:
                    attention_wo(0, 0, 1)
            pe.wait_ge(small_in, 16 * (6 + KC))
            pe.transpose(sm_ps[0:GH, 0:E], gw2_raw[:, :], ident[0:E, 0:E])
            pe.matmul(sm_ps[:, P:P + 3 * GH + E], ones_row[:, :], rows_raw[:, :], start=True, stop=True)
            for k in range(KC):
                last = pe.transpose(ag_ps[:, k * GH:(k + 1) * GH], y[1][0:GH, k * P:(k + 1) * P],
                                    ident[0:GH, 0:GH])
            last.then_inc(small_pe, 1)
            pe.wait_ge(w_lo_done, 4 * KC)
            pe.wait_ge(small_dve, 5)
            step(0, 0)
            step(1, 1)
            with pe.Fori(0, LOOPS) as i:
                step(2 * i + 2, 0)
                step(2 * i + 3, 1)
            step(NT, 0)
            step(NT + 1, 1)

        @block.scalar
        def _(act):
            def split_a(t, par):
                act.wait_ge(a_done, t + 1)
                at_least(act, wo_done, t - 1)
                act.activation(a_hi[par][:, :, :], a_raw[:, :, :], ACT.Copy).then_inc(a_hi_done, 1)

            def step(t, par):
                a_ok = not isinstance(t, int) or t < NT
                b_ok = not isinstance(t, int) or 1 <= t <= NT
                c_ok = not isinstance(t, int) or t >= 2
                if not isinstance(t, int) or t + 1 < NT:
                    split_a(t + 1, 1 - par)
                if a_ok:
                    act.wait_ge(var_done, t + 1)
                    act.activation(std[:, :], mean_var[:, 1:2], ACT.Sqrt, bias=eps[:, :]).then_inc(std_done, 1)
                if c_ok:
                    act.wait_ge(hidT_ps_done, t - 1)
                    act.activation(hidT[:, :], sm_ps[0:GH, 0:P], ACT.Copy).then_inc(hidT_done, 1)
                if b_ok:
                    act.wait_ge(ag_done, t)
                    act.activation(low[:, bass.ds(t - 1, 1), :].rearrange("p o r -> p (o r)"), ag_ps[:, 0:ER],
                                   ACT.Copy).then_inc(low_done, 1)
                    act.wait_ge(g_var_done, t)
                    act.activation(g_std[:, :], g_mean_var[:, 1:2], ACT.Sqrt, bias=eps[:, :]
                                   ).then_inc(g_std_done, 1)
                if a_ok:
                    act.wait_ge(tr_done, t + 1)
                    act.activation(yT_hi[:, :, :].rearrange("p k t -> p (k t)"),
                                   tr_ps[:, :, :].rearrange("p a b -> p (a b)"), ACT.Copy
                                   ).then_inc(yT_hi_done, 1)

            for n in range(KC):
                act.wait_ge(raw_in[n % RB], 16 * (n // RB + 1))
                for half in range(2):
                    cols = slice(half * HALF, (half + 1) * HALF)
                    act.activation(wo_hi[:, n, cols], raw[n % RB][:, cols], ACT.Copy).then_inc(w_hi_done, 1)
            split_a(0, 0)
            for n in range(KC):
                for half in range(2):
                    act.wait_ge(turned, 2 * n + half + 1)
                    act.activation(wm_hi[:, 4 * half:4 * half + 4, n * P:(n + 1) * P],
                                   tr_ps[:, half, :].rearrange("p (k o) -> p k o", k=4), ACT.Copy
                                   ).then_inc(w_hi_done, 1)
            act.wait_ge(pool_const, 3)
            step(0, 0)
            step(1, 1)
            with act.Fori(0, LOOPS - 1) as i:
                step(2 * i + 2, 0)
                step(2 * i + 3, 1)
            step(NT - 2, 0)
            step(NT - 1, 1)
            step(NT, 0)
            step(NT + 1, 1)

        @block.vector
        def _(dve):
            chain = Chain(dve, chain_sem, held_sem)
            gb1_b, gamma_b, beta_b, gb2_b = (rows[:, 0:GH], rows[:, GH:2 * GH], rows[:, 2 * GH:3 * GH],
                                             rows[:, 3 * GH:3 * GH + E])

            def divide_a(t):
                dve.wait_ge(a_in, 16 * (1 + REP) * (t + 1))
                dve.tensor_tensor(a_raw[:, :, :], a_raw[:, :, :], recip[:, :, :], ALU.mult).then_inc(a_done, 1)

            def split_a(t, par):
                dve.wait_ge(a_hi_done, t + 1)
                at_least(dve, wo_done, t - 1)
                dve.tensor_tensor(a_lo[par][:, :, :], a_raw[:, :, :], a_hi[par][:, :, :].bitcast(F32),
                                  ALU.subtract).then_inc(a_lo_done, 1)

            def step(t, par):
                a_ok = not isinstance(t, int) or t < NT
                b_ok = not isinstance(t, int) or 1 <= t <= NT
                c_ok = not isinstance(t, int) or t >= 2
                if not isinstance(t, int) or t + 1 < NT:
                    divide_a(t + 1)
                    split_a(t + 1, 1 - par)
                if a_ok:
                    dve.wait_ge(x_in[par], 16 * (t // 2 + 1) if isinstance(t, int) else 8 * (t - par) + 16)
                    if not isinstance(t, int) or t >= 2:
                        dve.wait_ge(u_stored[par], 16 * (t // 2) if isinstance(t, int) else 8 * (t - par))
                    dve.wait_ge(wo_done, t + 1)
                    dve.tensor_tensor(y[par][:, :], at_ps[:, :, :].rearrange("p a b -> p (a b)"),
                                      x_in_sb[par][:, :], ALU.add).then_inc(sum_done, 1)
                    dve.wait_ge(sum_done, t + 1)
                    moments(dve, chain, y[par], D, stats, mean_var[:, :])
                    dve.sem_inc(var_done, 1)
                    dve.wait_ge(std_done, t + 1)
                    chain.link(dve.reciprocal(rstd[:, :], std[:, :]))
                    dve.tensor_scalar(y[par][:, :], y[par][:, :], mean_var[:, 0:1], rstd[:, :],
                                      ALU.subtract, ALU.mult).then_inc(y_done, 1)
                if c_ok:
                    dve.wait_ge(gates_ps_done, t - 1)
                    dve.tensor_tensor(gates[:, :], sm_ps[:, P:P + E], gb2_b, ALU.add).then_inc(gates_done, 1)
                    dve.wait_ge(gates_done, t - 1)
                    chain.hold()
                    chain.link(dve.max(top[:, :], gates[:, :]))
                    chain.hold()
                    chain.link(dve.max_index(top_at[:, :], top[:, :], gates[:, :]))
                    chain.link(dve.tensor_copy(top_at_f[:, :], top_at[:, :]))
                    dve.tensor_tensor(diff[:, bass.ds(t - 2, 1)], top[:, 1:2], top[:, 0:1], ALU.subtract)
                    for k in range(TOPK):
                        last = dve.tensor_scalar(onehot[:, bass.ds(t - 2, 1), k, :].rearrange("p o e -> p (o e)"),
                                                 experts[:, :], top_at_f[:, k:k + 1], None, ALU.is_equal)
                    chain.link(last)
                if b_ok:
                    dve.wait_ge(mm_done, t)
                    dve.tensor_tensor(y[1 - par][:, :], mm_ps[:, :, :].rearrange("p a b -> p (a b)"),
                                      y[1 - par][:, :], ALU.add).then_inc(u_done, 1)
                    h = hid[1 - par]
                    dve.wait_ge(ag_done, t)
                    dve.wait_ge(low_done, t)
                    dve.tensor_tensor(h[:, :], ag_ps[:, ER:AG], gb1_b, ALU.add).then_inc(h_done, 1)
                    dve.wait_ge(h_done, t)
                    moments(dve, chain, h, GH, g_stats, g_mean_var[:, :])
                    dve.sem_inc(g_var_done, 1)
                    dve.wait_ge(g_std_done, t)
                    chain.link(dve.reciprocal(g_rstd[:, :], g_std[:, :]))
                    chain.link(dve.tensor_scalar(h[:, :], h[:, :], g_mean_var[:, 0:1], g_rstd[:, :],
                                                 ALU.subtract, ALU.mult))
                    chain.link(dve.tensor_tensor(h[:, :], h[:, :], gamma_b, ALU.mult))
                    chain.link(dve.tensor_tensor(h[:, :], h[:, :], beta_b, ALU.add))
                    dve.tensor_scalar(h[:, :], h[:, :], 0.0, None, ALU.max).then_inc(hid_done, 1)
                if a_ok:
                    dve.wait_ge(yT_hi_done, t + 1)
                    dve.tensor_tensor(yT_lo[:, :, :].rearrange("p k t -> p (k t)"),
                                      tr_ps[:, :, :].rearrange("p a b -> p (a b)"),
                                      yT_hi[:, :, :].rearrange("p k t -> p (k t)").bitcast(F32),
                                      ALU.subtract).then_inc(yT_lo_done, 1)

            LINKS = 3 + 4 + 6

            dve.wait_ge(den_in, 16)
            chain.link(dve.reciprocal(recip[:, :, :], y[0][:, :].rearrange("p (k t) -> p k t", k=KC)))
            dve.tensor_copy(y[0][:, :].rearrange("p (k t) -> p k t", k=KC), recip[:, :, :]).then_inc(rec_done, 1)
            for n in range(KC):
                for half in range(2):
                    cols = slice(half * HALF, (half + 1) * HALF)
                    dve.wait_ge(w_hi_done, 2 * n + half + 1)
                    dve.tensor_tensor(wo_lo[:, n, cols], raw[n % RB][:, cols], wo_hi[:, n, cols].bitcast(F32),
                                      ALU.subtract).then_inc(w_lo_done, 1)
            divide_a(0)
            split_a(0, 0)
            for n in range(KC):
                for half in range(2):
                    dve.wait_ge(w_hi_done, 2 * (KC + n) + half + 1)
                    out = slice(n * P, (n + 1) * P)
                    dve.tensor_tensor(wm_lo[:, 4 * half:4 * half + 4, out],
                                      tr_ps[:, half, :].rearrange("p (k o) -> p k o", k=4),
                                      wm_hi[:, 4 * half:4 * half + 4, out].bitcast(F32), ALU.subtract
                                      ).then_inc(w_lo_done, 1)
            dve.wait_ge(pool_const, 3)
            dve.tensor_copy(experts[:, :], experts_i[:, :]).then_inc(small_dve, 1)
            dve.wait_ge(small_pe, 1)
            dve.tensor_copy(gw2T[:, :], sm_ps[0:GH, 0:E]).then_inc(small_dve, 1)
            dve.tensor_copy(rows[:, :], sm_ps[:, P:P + 3 * GH + E]).then_inc(small_dve, 1)
            gw1T = ag_ps[:, 0:KC * GH].rearrange("p (k g) -> p k g", k=KC)
            dve.wait_ge(small_in, 16 * (6 + KC))
            chain.link(dve.tensor_copy(ag_hi[:, :, ER:AG], gw1T))
            chain.link(dve.tensor_copy(ag_hi[:, :, 0:ER], A_raw))
            dve.tensor_tensor(ag_lo[:, :, ER:AG], gw1T, ag_hi[:, :, ER:AG].bitcast(F32), ALU.subtract
                              ).then_inc(small_dve, 1)
            dve.tensor_tensor(ag_lo[:, :, 0:ER], A_raw, ag_hi[:, :, 0:ER].bitcast(F32), ALU.subtract
                              ).then_inc(small_dve, 1)
            dve.wait_ge(small_dve, 5)
            step(0, 0)
            step(1, 1)
            before = chain.n
            with dve.Fori(0, LOOPS - 1) as i:
                chain.start(before + i * (2 * LINKS))
                step(2 * i + 2, 0)
                step(2 * i + 3, 1)
            assert chain.n == 2 * LINKS, chain.n
            chain.start(before + (LOOPS - 1) * 2 * LINKS)
            step(NT - 2, 0)
            step(NT - 1, 1)
            step(NT, 0)
            step(NT + 1, 1)


def mix_experts(nc, sem, keep, u_d, lora_B, out):
    ER = E * R
    NT = N // P
    HALF = D // 2
    NB = 4
    low, diff, onehot = keep
    u_t = u_d.rearrange("(t p) d -> t p d", p=P)
    out_t = out.rearrange("b (t p) d -> (b t) p d", p=P)

    def at_least(engine, semaphore, value):
        if not isinstance(value, int) or value > 0:
            engine.wait_ge(semaphore, value)

    ctx = ExitStack()
    with ctx:
        sb = lambda name, shape, dt=F32: ctx.enter_context(nc.sbuf_tensor(name, shape, dt))
        ident = sb("p4_ident", [P, P])
        ones = sb("p4_ones", [P, P])
        eps = sb("p4_eps", [P, 1])
        lb = sb("p4_lora_B", [ER, D])
        counts = sb("p4_counts", [P, TOPK * E])
        allowed = sb("p4_allowed", [P, TOPK, E])
        exp_d = sb("p4_exp", [P, NT])
        den = sb("p4_den", [P, NT])
        prob = sb("p4_prob", [P, TOPK, NT])
        weights = sb("p4_weights", [P, NT, E])
        second = sb("p4_second", [P, NT, E])
        u = [sb(f"p4_u{i}", [P, D]) for i in range(2 * NB)]
        lw = [sb(f"p4_lw{i}", [P, ER]) for i in range(NB)]
        lwT = [sb(f"p4_lwT{i}", [ER, P]) for i in range(NB)]
        res = [sb(f"p4_res{i}", [P, D]) for i in range(NB)]
        stats = [sb(f"p4_stats{i}", [P, 2, 6]) for i in range(NB)]
        mean_var = [sb(f"p4_mean_var{i}", [P, 2]) for i in range(NB)]
        std = [sb(f"p4_std{i}", [P, 1]) for i in range(NB)]
        rstd = [sb(f"p4_rstd{i}", [P, 1]) for i in range(NB)]
        shift = [sb(f"p4_shift{i}", [P, 1]) for i in range(NB)]
        tr = [ctx.enter_context(nc.psum_tensor(f"p4_tr{i}", [P, BANK], F32)) for i in range(2)]
        lo = [ctx.enter_context(nc.psum_tensor(f"p4_lo{i}", [P, 2, BANK], F32)) for i in range(2)]

        ident_done, pool_const = sem("p4_ident_done"), sem("p4_pool_const")
        lb_in = sem("p4_lb_in")
        u_in = [sem(f"p4_u_in{i}") for i in range(2 * NB)]
        part_done, counts_ps_done, exp_done = sem("p4_part_done"), sem("p4_counts_ps_done"), sem("p4_exp_done")
        lw_done, tr_done, lwT_done = sem("p4_lw_done"), sem("p4_tr_done"), sem("p4_lwT_done")
        lora_done, z_done = sem("p4_lora_done"), sem("p4_z_done")
        var_done, std_done, shift_done = sem("p4_var_done"), sem("p4_std_done"), sem("p4_shift_done")
        res_done = sem("p4_res_done")
        stored = [sem(f"p4_stored{i}") for i in range(NB)]
        chain_sem, held_sem = sem("p4_chain"), sem("p4_held")

        block = ctx.enter_context(nc.Block())
        BODY = 2 * NB
        LEAD = 2

        def per(t, k, n, times):
            return times * (t // n) if isinstance(t, int) else (t - k) * (times // n) + times * (k // n)

        @block.sync
        def _(sp):
            def load(t, k):
                sp.dma_start(u[k][:, :], u_t[bass.ds(t, 1), :, :].rearrange("o p d -> (o p) d")).then_inc(u_in[k], 16)

            def one(t, k, more=True):
                sp.wait_ge(res_done, t + 1)
                sp.dma_start(out_t[bass.ds(t, 1), :, :].rearrange("o p d -> (o p) d"), res[k % NB][:, :]
                             ).then_inc(stored[k % NB], 16)
                if more:
                    load(t + BODY, k)

            sp.dma_start(lb[:, :], lora_B.rearrange("e r o -> (e r) o")).then_inc(lb_in, 16)
            for k in range(BODY):
                load(k, k)
            with sp.Fori(0, NT // BODY - 1) as i:
                for k in range(BODY):
                    one(BODY * i + k, k)
            for k in range(BODY):
                one(NT - BODY + k, k, more=False)
            for i in range(NB):
                sp.wait_ge(stored[i], 16 * NT // NB)

        @block.gpsimd
        def _(pool):
            make_identity(pool, ident, ident_done)
            pool.memset(ones[:, :], 1.0).then_inc(pool_const, 1)
            pool.memset(eps[:, :], LN_EPS).then_inc(pool_const, 1)

        @block.tensor
        def _(pe):
            pe.wait_ge(ident_done, 2)
            pe.wait_ge(pool_const, 2)
            pe.wait_ge(part_done, 1)
            pe.matmul(tr[1][:, 0:TOPK * E], ones[:, :], counts[:, :], start=True, stop=True
                      ).then_inc(counts_ps_done, 1)
            pe.wait_ge(lb_in, 16)

            def turn(t, k):
                pe.wait_ge(lw_done, t + 1)
                at_least(pe, lwT_done, t - 1)
                pe.transpose(tr[k % 2][:, 0:P], lw[k % NB][:, :], ident[:, :]).then_inc(tr_done, 1)

            def products(t, k):
                pe.wait_ge(lwT_done, t + 1)
                at_least(pe, z_done, t - 1)
                for half in range(2):
                    last = pe.matmul(lo[k % 2][:, half, :], lwT[k % NB][:, :],
                                     lb[:, half * HALF:(half + 1) * HALF], start=True, stop=True)
                last.then_inc(lora_done, 1)

            for k in range(LEAD):
                turn(k, k)
            for k in range(BODY):
                turn(k + LEAD, (k + LEAD) % BODY)
                products(k, k)
            with pe.Fori(0, NT // BODY - 2) as i:
                for k in range(BODY):
                    turn(BODY * i + BODY + k + LEAD, (k + LEAD) % BODY)
                    products(BODY * i + BODY + k, k)
            for k in range(BODY):
                if k + LEAD < BODY:
                    turn(NT - BODY + k + LEAD, k + LEAD)
                products(NT - BODY + k, k)

        @block.scalar
        def _(act):
            act.wait_ge(pool_const, 2)
            act.activation(exp_d[:, :], diff[:, :], ACT.Exp).then_inc(exp_done, 1)

            def copy_T(t, k):
                act.wait_ge(tr_done, t + 1)
                at_least(act, lora_done, t - NB + 1)
                act.activation(lwT[k % NB][:, :], tr[k % 2][:, 0:P], ACT.Copy).then_inc(lwT_done, 1)

            def root(t, k):
                act.wait_ge(var_done, t + 1)
                act.activation(std[k % NB][:, :], mean_var[k % NB][:, 1:2], ACT.Sqrt, bias=eps[:, :]
                               ).then_inc(std_done, 1)

            def norm(t, k):
                b = k % NB
                act.wait_ge(shift_done, t + 1)
                if not isinstance(t, int) or t >= NB:
                    act.wait_ge(stored[b], per(t, k, NB, 16))
                act.activation(res[b][:, :], u[k][:, :], ACT.Identity, bias=shift[b][:, :], scale=rstd[b][:, :]
                               ).then_inc(res_done, 1)

            for k in range(LEAD):
                copy_T(k, k)
            for k in range(BODY):
                copy_T(k + LEAD, (k + LEAD) % BODY)
                root(k, k)
                if k > 0:
                    norm(k - 1, k - 1)
            with act.Fori(0, NT // BODY - 2) as i:
                for k in range(BODY):
                    t = BODY * i + BODY + k
                    copy_T(t + LEAD, (k + LEAD) % BODY)
                    root(t, k)
                    norm(t - 1, (k - 1) % BODY)
            for k in range(BODY):
                if k + LEAD < BODY:
                    copy_T(NT - BODY + k + LEAD, k + LEAD)
                root(NT - BODY + k, k)
                norm(NT - BODY + k - 1, (k - 1) % BODY)
            norm(NT - 1, BODY - 1)

        @block.vector
        def _(dve):
            chain = Chain(dve, chain_sem, held_sem)
            flat = onehot[:, :, :, :].rearrange("p t k e -> p (t k e)").rearrange("p (t s) -> p s t", t=NT)
            dve.reduce_sum(counts[:, :], flat, AX.X).then_inc(part_done, 1)
            dve.wait_ge(exp_done, 1)
            chain.link(dve.tensor_scalar(den[:, :], exp_d[:, :], 1.0, None, ALU.add))
            chain.link(dve.reciprocal(prob[:, 0, :], den[:, :]))
            chain.link(dve.tensor_tensor(prob[:, 1, :], exp_d[:, :], prob[:, 0, :], ALU.mult))
            dve.wait_ge(counts_ps_done, 1)
            chain.link(dve.tensor_scalar(allowed[:, :, :].rearrange("p k e -> p (k e)"), tr[1][:, 0:TOPK * E],
                                         float(CAPACITY), 1.0 / R, ALU.is_le, ALU.mult))
            for k, w in ((0, weights), (1, second)):
                chain.link(dve.tensor_tensor(w[:, :, :], onehot[:, :, k, :],
                                             prob[:, k, :].unsqueeze(2).to_broadcast([P, NT, E]), ALU.mult))
                chain.link(dve.tensor_tensor(w[:, :, :], w[:, :, :],
                                             allowed[:, k, :].unsqueeze(1).to_broadcast([P, NT, E]), ALU.mult))
            chain.link(dve.tensor_tensor(weights[:, :, :], weights[:, :, :], second[:, :, :], ALU.add))

            def weigh(t, k):
                at_least(dve, tr_done, t - NB + 1)
                dve.tensor_tensor(lw[k % NB][:, :].rearrange("p (e r) -> p e r", e=E),
                                  low[:, bass.ds(t, 1), :].rearrange("p o (e r) -> p (o e) r", e=E),
                                  weights[:, bass.ds(t, 1), :].rearrange("p o e -> p (o e)").unsqueeze(2)
                                  .to_broadcast([P, E, R]), ALU.mult).then_inc(lw_done, 1)

            def tile(t, k):
                b = k % NB
                dve.wait_ge(u_in[k], per(t, k, BODY, 16) + 16)
                dve.wait_ge(lora_done, t + 1)
                dve.tensor_tensor(u[k][:, :], lo[k % 2][:, :, :].rearrange("p a b -> p (a b)"), u[k][:, :],
                                  ALU.add).then_inc(z_done, 1)
                dve.wait_ge(z_done, t + 1)
                moments(dve, chain, u[k], D, stats[b], mean_var[b][:, :])
                dve.sem_inc(var_done, 1)

            def scale_shift(t, k):
                b = k % NB
                dve.wait_ge(std_done, t + 1)
                at_least(dve, res_done, t - NB + 1)
                chain.link(dve.reciprocal(rstd[b][:, :], std[b][:, :]))
                dve.scalar_tensor_tensor(out=shift[b][:, :], in0=mean_var[b][:, 0:1], scalar=-1.0,
                                         in1=rstd[b][:, :], op0=ALU.mult, op1=ALU.mult).then_inc(shift_done, 1)

            LINKS = 3
            for k in range(LEAD + 1):
                weigh(k, k)
            for k in range(BODY):
                weigh(k + LEAD + 1, (k + LEAD + 1) % BODY)
                tile(k, k)
                if k > 0:
                    scale_shift(k - 1, k - 1)
            before = chain.n
            with dve.Fori(0, NT // BODY - 2) as i:
                chain.start(before + i * (BODY * LINKS))
                for k in range(BODY):
                    weigh(BODY * i + BODY + k + LEAD + 1, (k + LEAD + 1) % BODY)
                    tile(BODY * i + BODY + k, k)
                    scale_shift(BODY * i + BODY + k - 1, (k - 1) % BODY)
            assert chain.n == BODY * LINKS
            chain.start(before + (NT // BODY - 2) * BODY * LINKS)
            for k in range(BODY):
                if k + LEAD + 1 < BODY:
                    weigh(NT - BODY + k + LEAD + 1, k + LEAD + 1)
                tile(NT - BODY + k, k)
                scale_shift(NT - BODY + k - 1, (k - 1) % BODY)
            scale_shift(NT - 1, (NT - 1) % BODY)


def build(nc, x, wq, wk, wv, wo, weight, lora_A, lora_B, gw1, gb1, gamma, beta, gw2, gb2, out):
    dram = lambda name, shape: nc.dram_tensor(name, shape, F32, kind="Internal").ap()
    q_hi, q_lo = dram("q_hi", [D, N]), dram("q_lo", [D, N])
    k_hi, k_lo = dram("k_hi", [NKV * HD, N]), dram("k_lo", [NKV * HD, N])
    v_d = dram("v", [NKV, P, N // P, HD])
    aT_d = dram("attended_T", [D, N])
    den_d, rec_d = dram("denominators", [NH, N]), dram("reciprocals", [NH, N])
    u_d = dram("u", [N, D])
    with ExitStack() as ctx:
        sem = lambda name: ctx.enter_context(nc.semaphore(name))
        project_qkv(nc, sem, x, wq, wk, wv, q_hi, q_lo, k_hi, k_lo, v_d)
        attend(nc, sem, q_hi, q_lo, k_hi, k_lo, v_d, aT_d, den_d)
        keep = (ctx.enter_context(nc.sbuf_tensor("low", [P, N // P, E * R], F32)),
                ctx.enter_context(nc.sbuf_tensor("diff", [P, N // P], F32)),
                ctx.enter_context(nc.sbuf_tensor("onehot", [P, N // P, TOPK, E], F32)))
        project_and_gate(nc, sem, keep, x, aT_d, wo, weight, lora_A, gw1, gb1, gamma, beta, gw2, gb2, den_d, rec_d, u_d)
        mix_experts(nc, sem, keep, u_d, lora_B, out)


_INS = ["L0_attn_x", "L0_attn_wq", "L0_attn_wk", "L0_attn_wv", "L0_attn_wo", "L0_ffn_weight", "L0_ffn_lora_A",
        "L0_ffn_lora_B", "L0_ffn_gw1", "L0_ffn_gb1", "L0_ffn_ln_gamma", "L0_ffn_ln_beta", "L0_ffn_gw2", "L0_ffn_gb2"]
_OUT = ((B, S, D), "float32")


def kernel(**inputs):
    import numpy as _np
    import concourse.bacc as _bacc
    from concourse.bass_utils import run_bass_kernel_spmd as _run

    nc = _bacc.Bacc("TRN2", target_bir_lowering=False, num_devices=1)
    arrays, args = {}, []
    for name in _INS:
        a = _np.ascontiguousarray(inputs[name])
        arrays[f"in_{name}"] = a
        args.append(nc.dram_tensor(f"in_{name}", a.shape, mybir.dt.from_np(a.dtype), kind="ExternalInput").ap())
    args.append(nc.dram_tensor("out", _OUT[0], mybir.dt.from_np(_np.dtype(_OUT[1])), kind="ExternalOutput").ap())
    build(nc, *args)
    return _run(nc, [arrays], core_ids=[0]).results[0]["out"]
```
